# Optimizing a Trainium2 kernel written in Bass

```python
import numpy as np
import jax
import jax.numpy as jnp

def _softmax(x, axis=-1):
    return jax.nn.softmax(x, axis=axis)

def _gelu(x):
    return jax.nn.gelu(x, approximate=True)

def _silu(x):
    return jax.nn.silu(x)

def _sigmoid(x):
    return jax.nn.sigmoid(x)

def _layernorm(x, axis=-1, eps=1e-05):
    m = jnp.mean(x, axis=axis, keepdims=True)
    v = jnp.var(x, axis=axis, keepdims=True)
    return (x - m) / jnp.sqrt(v + eps)

def _scatter_add(tgt, idx, src, axis=0):
    return tgt.at[idx].add(src)

def _segment_sum(src, seg, n):
    return jax.ops.segment_sum(src, seg, n)
kernel_name = 'mk_decoder_preln_d4_seqx_r8_7ec63b'

def setup_inputs(seed: int=0):
    np.random.seed(seed)
    _w = jnp.asarray

    def _rec_inputs():
        import jax
        import jax.numpy as jnp
        _rk = jax.random.key(seed)
        x = 7.22e-05 + 1 * jax.random.normal(jax.random.fold_in(_rk, 1), (1, 1024, 128), jnp.float32)
        _lenS = 1024 - jax.random.randint(jax.random.fold_in(_rk, 7), (1,), 0, max(1, 1024 // 4) + 1, jnp.int32)
        _lenS2 = 6404 - jax.random.randint(jax.random.fold_in(_rk, 8), (1,), 0, max(1, 6404 // 4) + 1, jnp.int32)
        _ctx_1024P = jax.random.normal(jax.random.fold_in(_rk, 11), (1, 16, 128), jnp.float32)
        _ctx_1024c = jax.random.dirichlet(jax.random.fold_in(_rk, 511), 0.3 * jnp.ones((16,), jnp.float32), (1, 6404))
        _ctx_1024t = jnp.einsum('bsk,bkd->bsd', _ctx_1024c, _ctx_1024P)
        _ctx_1024t = _ctx_1024t * jax.lax.rsqrt(jnp.mean(jnp.square(_ctx_1024t)) + 1e-12) * 0.953939
        ctx_1024 = 4.13588e-05 + 0.999923 * (_ctx_1024t + 0.3 * jax.random.normal(jax.random.fold_in(_rk, 611), (1, 6404, 128), jnp.float32))
        _validS = jnp.arange(1024)[None, :] < _lenS[:, None]
        _validS2 = jnp.arange(6404)[None, :] < _lenS2[:, None]
        _causal = jnp.tril(jnp.ones((1024, 1024), dtype=bool))
        mask_BxS2_bf1 = jnp.ones((1, 6404), dtype=bool)
        mask_Bx1x1xS2_ik0 = jnp.where(jnp.broadcast_to(_validS2[:, None, None, :], (1, 1, 1, 6404)), 0, 1).astype(jnp.int32)
        return (x, ctx_1024, mask_BxS2_bf1, mask_Bx1x1xS2_ik0)
    x, ctx_1024, mask_BxS2_bf1, mask_Bx1x1xS2_ik0 = _rec_inputs()

    def _L0_attn_setup():
        import jax, jax.numpy as jnp
        import numpy as np
        NUM_HEADS = 16
        THETA = 10000.0

        def _rope(x, theta):
            S, d_k = (x.shape[1], x.shape[-1])
            k = jnp.arange(d_k // 2, dtype=jnp.float32)
            inv_freq = theta ** (-2.0 * k / d_k)
            ang = jnp.arange(S, dtype=jnp.float32)[:, None] * inv_freq
            cos = jnp.cos(ang)[None, :, None, :]
            sin = jnp.sin(ang)[None, :, None, :]
            x_even = x[..., 0::2]
            x_odd = x[..., 1::2]
            y_even = cos * x_even - sin * x_odd
            y_odd = sin * x_even + cos * x_odd
            y = jnp.stack([y_even, y_odd], axis=-1)
            return y.reshape(x.shape)
        key = jax.random.key(seed)
        ks = jax.random.split(key, 5)
        B, S, D = (2, 256, 128)
        std = 1.0 / np.sqrt(D)
        return {'in_features': jax.random.normal(ks[0], (B, S, D), dtype=jnp.float32), 'W_Q': jax.random.normal(ks[1], (D, D), dtype=jnp.float32) * std, 'W_K': jax.random.normal(ks[2], (D, D), dtype=jnp.float32) * std, 'W_V': jax.random.normal(ks[3], (D, D), dtype=jnp.float32) * std, 'W_O': jax.random.normal(ks[4], (D, D), dtype=jnp.float32) * std}
    _L0_attn_all = _L0_attn_setup()
    _L0_attn_in = {k: v for k, v in _L0_attn_all.items() if k in ('W_Q', 'W_K', 'W_V', 'W_O')}
    del _L0_attn_all

    def _L0_xattn_setup():
        import jax, jax.numpy as jnp
        import numpy as np
        HEADS, QSIZE, KSIZE = (16, 64, 64)
        key = jax.random.key(seed)
        ks = jax.random.split(key, 8)
        B, S, D = (4, 256, 128)
        sd = 1.0 / np.sqrt(D)
        return {'q_in': jax.random.normal(ks[0], (B, S, D), jnp.float32), 'k_in': jax.random.normal(ks[1], (B, S, D), jnp.float32), 'v_in': jax.random.normal(ks[2], (B, S, D), jnp.float32), 'key_mask': jnp.ones((B, S), dtype=bool), 'Wq': jax.random.normal(ks[3], (D, HEADS * QSIZE), jnp.float32) * sd, 'bq': jnp.zeros((HEADS * QSIZE,), jnp.float32), 'Wk': jax.random.normal(ks[4], (D, HEADS * QSIZE), jnp.float32) * sd, 'bk': jnp.zeros((HEADS * QSIZE,), jnp.float32), 'Wv': jax.random.normal(ks[5], (D, HEADS * KSIZE), jnp.float32) * sd, 'bv': jnp.zeros((HEADS * KSIZE,), jnp.float32), 'Wo': jax.random.normal(ks[6], (HEADS * KSIZE, D), jnp.float32) * sd, 'bo': jnp.zeros((D,), jnp.float32)}
    _L0_xattn_all = _L0_xattn_setup()
    _L0_xattn_in = {k: v for k, v in _L0_xattn_all.items() if k in ('Wq', 'bq', 'Wk', 'bk', 'Wv', 'bv', 'Wo', 'bo')}
    del _L0_xattn_all

    def _L0_ffn_setup():
        import jax, jax.numpy as jnp
        import numpy as np
        D_IN, D_HID = (128, 512)

        def _ternary(key, shape):
            return jax.random.randint(key, shape, -1, 2).astype(jnp.float32)

        def _tlin(x, w, s):
            return jnp.einsum('bsi,oi->bso', x, w) * s
        key = jax.random.key(seed)
        ks = jax.random.split(key, 12)
        inv = lambda fan: 1.0 / np.sqrt(fan).astype(np.float32)
        return {'x': jax.random.normal(ks[0], (4, 256, D_IN), dtype=jnp.float32), 'w1_w': _ternary(ks[1], (D_HID, D_IN)), 'w1_s': jax.random.uniform(ks[2], (D_HID,), dtype=jnp.float32) * inv(D_IN), 'w2_w': _ternary(ks[3], (D_HID, D_IN)), 'w2_s': jax.random.uniform(ks[4], (D_HID,), dtype=jnp.float32) * inv(D_IN), 'h1_w': _ternary(ks[5], (D_HID, D_HID)), 'h1_s': jax.random.uniform(ks[6], (D_HID,), dtype=jnp.float32) * inv(D_HID), 'h2_w': _ternary(ks[7], (D_HID, D_HID)), 'h2_s': jax.random.uniform(ks[8], (D_HID,), dtype=jnp.float32) * inv(D_HID), 'w3_w': _ternary(ks[9], (D_IN, D_HID)), 'w3_s': jax.random.uniform(ks[10], (D_IN,), dtype=jnp.float32) * inv(D_HID)}
    _L0_ffn_all = _L0_ffn_setup()
    _L0_ffn_in = {k: v for k, v in _L0_ffn_all.items() if k in ('w1_w', 'w1_s', 'w2_w', 'w2_s', 'h1_w', 'h1_s', 'h2_w', 'h2_s', 'w3_w', 'w3_s')}
    del _L0_ffn_all

    def _L1_attn_setup():
        import math
        import jax, jax.numpy as jnp
        import numpy as np
        NHEAD = 16
        HEAD_DIM = 64
        D_MODEL = 128
        B, T = (2, 512)

        def _cosformer(x, Wq, bq, Wk, bk, Wv, bv, Wo, bo):
            Bsz, Tlen, _ = x.shape
            H, dh = (NHEAD, HEAD_DIM)
            Q = (x @ Wq + bq).reshape(Bsz, Tlen, H, dh)
            K = (x @ Wk + bk).reshape(Bsz, Tlen, H, dh)
            V = (x @ Wv + bv).reshape(Bsz, Tlen, H, dh)
            Qp = jax.nn.relu(Q)
            Kp = jax.nn.relu(K)
            angles = math.pi / (2.0 * Tlen) * jnp.arange(Tlen, dtype=jnp.float32)
            cosw = jnp.cos(angles)[None, :, None, None]
            sinw = jnp.sin(angles)[None, :, None, None]
            Qc, Qs = (Qp * cosw, Qp * sinw)
            Kc, Ks = (Kp * cosw, Kp * sinw)
            tm = lambda a: jnp.moveaxis(a, 1, 0)
            Qc, Qs, Kc, Ks, Vt = (tm(Qc), tm(Qs), tm(Kc), tm(Ks), tm(V))
            S0 = jnp.zeros((Bsz, H, dh, dh), dtype=x.dtype)
            z0 = jnp.zeros((Bsz, H, dh), dtype=x.dtype)

            def step(carry, inp):
                S_cos, S_sin, z_cos, z_sin = carry
                qc, qs, kc, ks_, v = inp
                S_cos = S_cos + kc[..., :, None] * v[..., None, :]
                S_sin = S_sin + ks_[..., :, None] * v[..., None, :]
                z_cos = z_cos + kc
                z_sin = z_sin + ks_
                num = jnp.einsum('bhi,bhij->bhj', qc, S_cos) + jnp.einsum('bhi,bhij->bhj', qs, S_sin)
                den = jnp.sum(qc * z_cos + qs * z_sin, axis=-1)
                den = jnp.maximum(den, 1e-06)[..., None]
                return ((S_cos, S_sin, z_cos, z_sin), num / den)
            _, out = jax.lax.scan(step, (S0, S0, z0, z0), (Qc, Qs, Kc, Ks, Vt))
            out = jnp.moveaxis(out, 0, 1).reshape(Bsz, Tlen, H * dh)
            return out @ Wo + bo
        key = jax.random.key(seed)
        ks = jax.random.split(key, 9)
        HD = NHEAD * HEAD_DIM
        s_in = 1.0 / math.sqrt(D_MODEL)
        s_out = 1.0 / math.sqrt(HD)
        return {'x': jax.random.normal(ks[0], (B, T, D_MODEL), dtype=jnp.float32), 'Wq': jax.random.normal(ks[1], (D_MODEL, HD), dtype=jnp.float32) * s_in, 'bq': jnp.zeros((HD,), dtype=jnp.float32), 'Wk': jax.random.normal(ks[2], (D_MODEL, HD), dtype=jnp.float32) * s_in, 'bk': jnp.zeros((HD,), dtype=jnp.float32), 'Wv': jax.random.normal(ks[3], (D_MODEL, HD), dtype=jnp.float32) * s_in, 'bv': jnp.zeros((HD,), dtype=jnp.float32), 'Wo': jax.random.normal(ks[4], (HD, D_MODEL), dtype=jnp.float32) * s_out, 'bo': jnp.zeros((D_MODEL,), dtype=jnp.float32)}
    _L1_attn_all = _L1_attn_setup()
    _L1_attn_in = {k: v for k, v in _L1_attn_all.items() if k in ('Wq', 'bq', 'Wk', 'bk', 'Wv', 'bv', 'Wo', 'bo')}
    del _L1_attn_all

    def _L1_xattn_setup():
        import jax, jax.numpy as jnp
        import numpy as np
        EMBED_DIM = 128
        B, QL, KL = (4, 256, 256)
        key = jax.random.key(seed)
        k1, k2, k3, k4 = jax.random.split(key, 4)
        hidden_states = jax.random.normal(k1, (B, QL, EMBED_DIM), dtype=jnp.float32)
        decoder_hidden_states = jax.random.normal(k2, (B, KL, EMBED_DIM), dtype=jnp.float32)
        Wq = jax.random.normal(k3, (EMBED_DIM, EMBED_DIM), dtype=jnp.float32) * (1.0 / np.sqrt(EMBED_DIM))
        Wkv = jax.random.normal(k4, (EMBED_DIM, 2 * EMBED_DIM), dtype=jnp.float32) * (1.0 / np.sqrt(EMBED_DIM))
        return {'hidden_states': hidden_states, 'decoder_hidden_states': decoder_hidden_states, 'Wq': Wq, 'Wkv': Wkv}
    _L1_xattn_all = _L1_xattn_setup()
    _L1_xattn_in = {k: v for k, v in _L1_xattn_all.items() if k in ('Wq', 'Wkv')}
    del _L1_xattn_all

    def _L1_ffn_setup():
        import jax, jax.numpy as jnp
        import numpy as np
        EMB = 128
        FF = 4 * EMB

        def _ternary(w):
            scale = jnp.maximum(jnp.mean(jnp.abs(w)), 1e-08)
            w_t = jnp.clip(jnp.round(w / scale), -1.0, 1.0)
            return w + jax.lax.stop_gradient(w_t - w)
        key = jax.random.key(seed)
        kx, k1, k2, kb1, kb2 = jax.random.split(key, 5)
        x = jax.random.normal(kx, (4, 256, EMB), dtype=jnp.float32)
        lim1 = 1.0 / np.sqrt(EMB)
        lim2 = 1.0 / np.sqrt(FF)
        W1 = jax.random.uniform(k1, (FF, EMB), jnp.float32, -lim1, lim1)
        b1 = jax.random.uniform(kb1, (FF,), jnp.float32, -lim1, lim1)
        W2 = jax.random.uniform(k2, (EMB, FF), jnp.float32, -lim2, lim2)
        b2 = jax.random.uniform(kb2, (EMB,), jnp.float32, -lim2, lim2)
        return {'x': x, 'W1': W1, 'b1': b1, 'W2': W2, 'b2': b2}
    _L1_ffn_all = _L1_ffn_setup()
    _L1_ffn_in = {k: v for k, v in _L1_ffn_all.items() if k in ('W1', 'b1', 'W2', 'b2')}
    del _L1_ffn_all

    def _L2_attn_setup():
        import jax, jax.numpy as jnp
        import numpy as np
        DIM, HID, K, B, S = (128, 192, 4, 4, 512)
        EPS = 1e-05
        C = 8.0

        def rmsnorm(x, w):
            return x * jax.lax.rsqrt(jnp.mean(x * x, axis=-1, keepdims=True) + EPS) * w

        def _rg_lru(u, rg_in_w, rg_in_b, rg_gate_w, rg_gate_b, forget_lambda):
            ig = jnp.einsum('bsh,gh->bsg', u, rg_in_w) + rg_in_b
            rg = jnp.einsum('bsh,gh->bsg', u, rg_gate_w) + rg_gate_b
            alpha = jnp.exp(-C * jax.nn.softplus(forget_lambda) * jax.nn.sigmoid(rg))
            beta = jnp.sqrt(1.0 - alpha * alpha + 1e-06)
            xbeta = beta * jax.nn.sigmoid(ig) * u

            def combine(e1, e2):
                a1, b1 = e1
                a2, b2 = e2
                return (a2 * a1, a2 * b1 + b2)
            _, h = jax.lax.associative_scan(combine, (alpha, xbeta), axis=1)
            return h
        key = jax.random.key(seed)
        ks = jax.random.split(key, 16)
        n = jax.random.normal
        return {'x': n(ks[0], (B, S, DIM), jnp.float32), 'W_in': n(ks[1], (HID, DIM), jnp.float32) * DIM ** (-0.5), 'W_gate': n(ks[2], (HID, DIM), jnp.float32) * DIM ** (-0.5), 'conv_w': n(ks[3], (HID, 1, K), jnp.float32) * (1.0 / K) ** 0.5, 'conv_b': n(ks[4], (HID,), jnp.float32) * 0.02, 'W_out': n(ks[5], (DIM, HID), jnp.float32) * HID ** (-0.5), 'rg_in_w': n(ks[6], (HID, HID), jnp.float32) * HID ** (-0.5), 'rg_in_b': jnp.zeros((HID,), jnp.float32), 'rg_gate_w': n(ks[7], (HID, HID), jnp.float32) * HID ** (-0.5), 'rg_gate_b': jnp.zeros((HID,), jnp.float32), 'forget_lambda': jnp.linspace(-4.323, -9.0, HID, dtype=jnp.float32), 'mlp_gate_w': n(ks[8], (HID, DIM), jnp.float32) * DIM ** (-0.5), 'mlp_up_w': n(ks[9], (HID, DIM), jnp.float32) * DIM ** (-0.5), 'mlp_down_w': n(ks[10], (DIM, HID), jnp.float32) * HID ** (-0.5), 'norm1_w': jnp.ones((DIM,), jnp.float32), 'norm2_w': jnp.ones((DIM,), jnp.float32)}
    _L2_attn_all = _L2_attn_setup()
    _L2_attn_in = {k: v for k, v in _L2_attn_all.items() if k in ('W_in', 'W_gate', 'conv_w', 'conv_b', 'W_out', 'rg_in_w', 'rg_in_b', 'rg_gate_w', 'rg_gate_b', 'forget_lambda', 'mlp_gate_w', 'mlp_up_w', 'mlp_down_w', 'norm1_w', 'norm2_w')}
    del _L2_attn_all

    def _L2_xattn_setup():
        import jax, jax.numpy as jnp
        import numpy as np
        EMBED_DIM = 128
        NUM_HEADS = 16
        HEAD_DIM = EMBED_DIM // NUM_HEADS
        key = jax.random.key(seed)
        ks = jax.random.split(key, 7)
        B, S, E = (2, 256, EMBED_DIM)
        bound = float(np.sqrt(6.0 / (E + E)))
        mkw = lambda k: jax.random.uniform(k, (E, E), jnp.float32, -bound, bound)
        return {'query': jax.random.normal(ks[0], (B, S, E), jnp.float32), 'key': jax.random.normal(ks[1], (B, S, E), jnp.float32), 'value': jax.random.normal(ks[2], (B, S, E), jnp.float32), 'Wq': mkw(ks[3]), 'Wk': mkw(ks[4]), 'Wv': mkw(ks[5]), 'Wo': mkw(ks[6])}
    _L2_xattn_all = _L2_xattn_setup()
    _L2_xattn_in = {k: v for k, v in _L2_xattn_all.items() if k in ('Wq', 'Wk', 'Wv', 'Wo')}
    del _L2_xattn_all

    def _L2_ffn_setup():
        import jax, jax.numpy as jnp
        import numpy as np
        B, T, C, H, E, MIN_E = (4, 256, 128, 128, 16, 2)
        IS_CAUSAL = False

        def _forward(hidden_states, sim_matrix, gates, q_proj, k_proj, v_proj, o_proj):
            b, t, c = hidden_states.shape
            n = b * t
            x = hidden_states.reshape(n, c)
            xn = x / jnp.maximum(jnp.linalg.norm(x, axis=-1, keepdims=True), 1e-12)
            sn = sim_matrix / jnp.maximum(jnp.linalg.norm(sim_matrix, axis=0, keepdims=True), 1e-12)
            logits = xn @ sn - jax.nn.sigmoid(gates)
            gated = jax.nn.relu(logits)
            hard = (gated > 0).astype(gated.dtype)
            mask = gated + jax.lax.stop_gradient(hard - gated)
            inactive = jnp.sum(hard, axis=1) == 0
            _, fb_idx = jax.lax.top_k(logits, MIN_E)
            fb = jnp.zeros((n, logits.shape[1]), gated.dtype).at[jnp.arange(n)[:, None], fb_idx].set(1.0)
            put = jax.lax.stop_gradient(inactive[:, None].astype(gated.dtype) * fb)
            mask = mask * (1.0 - put) + put
            masked = jnp.where(mask > 0, gated, -jnp.inf)
            w = jax.nn.softmax(masked, axis=-1)

            def moe_proj(p):
                y = jnp.einsum('nc,ech->neh', x, p)
                return jnp.einsum('ne,neh->nh', w, y)
            q = moe_proj(q_proj).reshape(b, t, -1)
            k = moe_proj(k_proj).reshape(b, t, -1)
            v = moe_proj(v_proj).reshape(b, t, -1)
            h = q.shape[-1]
            scores = jnp.einsum('bth,bsh->bts', q, k) / jnp.sqrt(jnp.asarray(h, q.dtype))
            if IS_CAUSAL and t > 1:
                causal = jnp.tril(jnp.ones((t, t), bool))
                scores = jnp.where(causal[None], scores, -jnp.inf)
            attn = jax.nn.softmax(scores, axis=-1)
            o = jnp.einsum('bts,bsh->bth', attn, v).reshape(n, h)
            z = jnp.einsum('ne,nh->enh', w, o)
            out = jnp.einsum('enh,ehc->nc', z, o_proj)
            return out.reshape(b, t, c)
        key = jax.random.key(seed)
        ks = jax.random.split(key, 6)
        lim_qkv = float(np.sqrt(6.0 / (C + H)))
        inp = {'hidden_states': jax.random.normal(ks[0], (B, T, C), jnp.float32), 'sim_matrix': jax.random.normal(ks[1], (C, E), jnp.float32), 'gates': jnp.zeros((E,), jnp.float32), 'q_proj': jax.random.uniform(ks[2], (E, C, H), jnp.float32, -lim_qkv, lim_qkv), 'k_proj': jax.random.uniform(ks[3], (E, C, H), jnp.float32, -lim_qkv, lim_qkv), 'v_proj': jax.random.uniform(ks[4], (E, C, H), jnp.float32, -lim_qkv, lim_qkv), 'o_proj': jax.random.uniform(ks[5], (E, H, C), jnp.float32, -lim_qkv, lim_qkv)}
        return inp
    _L2_ffn_all = _L2_ffn_setup()
    _L2_ffn_in = {k: v for k, v in _L2_ffn_all.items() if k in ('sim_matrix', 'gates', 'q_proj', 'k_proj', 'v_proj', 'o_proj')}
    del _L2_ffn_all

    def _L3_attn_setup():
        import math
        import jax, jax.numpy as jnp
        import numpy as np
        HEADS = 8
        SCALE_BASE = 512.0
        GN_EPS = 1e-05

        def _gammas(heads):
            return 1.0 - np.exp(np.linspace(math.log(1.0 / 32.0), math.log(1.0 / 512.0), heads))

        def _xpos(x, downscale):
            N, S, d = x.shape
            half = d // 2
            scale = (jnp.arange(0, d, 2, dtype=jnp.float32) + 0.4 * d) / (1.4 * d)
            pos = jnp.arange(S, dtype=jnp.float32)
            sc = scale[None, :] ** (pos / SCALE_BASE)[:, None]
            inv_freq = 1.0 / 10000.0 ** (jnp.arange(half, dtype=jnp.float32) / half)
            sinusoid = pos[:, None] * inv_freq[None, :]
            sin, cos = (jnp.sin(sinusoid), jnp.cos(sinusoid))
            if downscale:
                sc = 1.0 / sc
            sin_s = jnp.repeat(sin * sc, 2, axis=-1)
            cos_s = jnp.repeat(cos * sc, 2, axis=-1)
            x1, x2 = (x[..., ::2], x[..., 1::2])
            rot = jnp.stack((-x2, x1), axis=-1).reshape(x.shape)
            return x * cos_s + rot * sin_s
        key = jax.random.key(seed)
        ks = jax.random.split(key, 6)
        B, S, H = (2, 256, 128)
        h = HEADS
        d = H // h
        X = jax.random.normal(ks[0], (B, S, H), dtype=jnp.float32)
        W_Q = jax.random.normal(ks[1], (h, d, d), dtype=jnp.float32) / d
        W_K = jax.random.normal(ks[2], (h, d, d), dtype=jnp.float32) / d
        W_V = jax.random.normal(ks[3], (h, d, d), dtype=jnp.float32) / d
        W_G = jax.random.normal(ks[4], (H, H), dtype=jnp.float32) / H
        W_O = jax.random.normal(ks[5], (H, H), dtype=jnp.float32) / H
        gn_weight = jnp.ones((H,), dtype=jnp.float32)
        gn_bias = jnp.zeros((H,), dtype=jnp.float32)
        return {'X': X, 'W_Q': W_Q, 'W_K': W_K, 'W_V': W_V, 'W_G': W_G, 'W_O': W_O, 'gn_weight': gn_weight, 'gn_bias': gn_bias}
    _L3_attn_all = _L3_attn_setup()
    _L3_attn_in = {k: v for k, v in _L3_attn_all.items() if k in ('W_Q', 'W_K', 'W_V', 'W_G', 'W_O', 'gn_weight', 'gn_bias')}
    del _L3_attn_all

    def _L3_xattn_setup():
        import jax, jax.numpy as jnp
        import numpy as np
        BS, SEQ, D_MODEL, N_HEADS = (4, 256, 128, 16)
        D_HEAD = D_MODEL // N_HEADS

        def _split_heads(x):
            b, s, _ = x.shape
            return x.reshape(b, s, N_HEADS, D_HEAD).transpose(0, 2, 1, 3)
        key = jax.random.key(seed)
        ks = jax.random.split(key, 12)
        s = 1.0 / np.sqrt(D_MODEL)
        return {'Q': jax.random.normal(ks[0], (BS, SEQ, D_MODEL), jnp.float32), 'K': jax.random.normal(ks[1], (BS, SEQ, D_MODEL), jnp.float32), 'V': jax.random.normal(ks[2], (BS, SEQ, D_MODEL), jnp.float32), 'mask': jax.random.randint(ks[3], (BS, 1, 1, SEQ), 0, 2, jnp.int32), 'Wq': jax.random.normal(ks[4], (D_MODEL, D_MODEL), jnp.float32) * s, 'bq': jnp.zeros((D_MODEL,), jnp.float32), 'Wk': jax.random.normal(ks[5], (D_MODEL, D_MODEL), jnp.float32) * s, 'bk': jnp.zeros((D_MODEL,), jnp.float32), 'Wv': jax.random.normal(ks[6], (D_MODEL, D_MODEL), jnp.float32) * s, 'bv': jnp.zeros((D_MODEL,), jnp.float32), 'Wo': jax.random.normal(ks[7], (D_MODEL, D_MODEL), jnp.float32) * s, 'bo': jnp.zeros((D_MODEL,), jnp.float32)}
    _L3_xattn_all = _L3_xattn_setup()
    _L3_xattn_in = {k: v for k, v in _L3_xattn_all.items() if k in ('Wq', 'bq', 'Wk', 'bk', 'Wv', 'bv', 'Wo', 'bo')}
    del _L3_xattn_all

    def _L3_ffn_setup():
        import jax, jax.numpy as jnp
        import numpy as np
        W_SCALE = 0.02
        TOP_K = 2
        key = jax.random.key(seed)
        ks = jax.random.split(key, 5)
        B, S, H, I, E = (2, 128, 128, 512, 8)
        return {'x': jax.random.normal(ks[0], (B, S, H), dtype=jnp.float32), 'gate': jax.random.normal(ks[1], (H, E), dtype=jnp.float32) * W_SCALE, 'experts_w1': jax.random.normal(ks[2], (E, H, I), dtype=jnp.float32) * W_SCALE, 'experts_w2': jax.random.normal(ks[3], (E, I, H), dtype=jnp.float32) * W_SCALE, 'experts_w3': jax.random.normal(ks[4], (E, H, I), dtype=jnp.float32) * W_SCALE}
    _L3_ffn_all = _L3_ffn_setup()
    _L3_ffn_in = {k: v for k, v in _L3_ffn_all.items() if k in ('gate', 'experts_w1', 'experts_w2', 'experts_w3')}
    del _L3_ffn_all
    return {'x': x, 'ctx_1024': ctx_1024, 'mask_BxS2_bf1': mask_BxS2_bf1, 'mask_Bx1x1xS2_ik0': mask_Bx1x1xS2_ik0, 'L0_attn_W_Q': _L0_attn_in['W_Q'], 'L0_attn_W_K': _L0_attn_in['W_K'], 'L0_attn_W_V': _L0_attn_in['W_V'], 'L0_attn_W_O': _L0_attn_in['W_O'], 'L0_xattn_Wq': _L0_xattn_in['Wq'], 'L0_xattn_bq': _L0_xattn_in['bq'], 'L0_xattn_Wk': _L0_xattn_in['Wk'], 'L0_xattn_bk': _L0_xattn_in['bk'], 'L0_xattn_Wv': _L0_xattn_in['Wv'], 'L0_xattn_bv': _L0_xattn_in['bv'], 'L0_xattn_Wo': _L0_xattn_in['Wo'], 'L0_xattn_bo': _L0_xattn_in['bo'], 'L0_ffn_w1_w': _L0_ffn_in['w1_w'], 'L0_ffn_w1_s': _L0_ffn_in['w1_s'], 'L0_ffn_w2_w': _L0_ffn_in['w2_w'], 'L0_ffn_w2_s': _L0_ffn_in['w2_s'], 'L0_ffn_h1_w': _L0_ffn_in['h1_w'], 'L0_ffn_h1_s': _L0_ffn_in['h1_s'], 'L0_ffn_h2_w': _L0_ffn_in['h2_w'], 'L0_ffn_h2_s': _L0_ffn_in['h2_s'], 'L0_ffn_w3_w': _L0_ffn_in['w3_w'], 'L0_ffn_w3_s': _L0_ffn_in['w3_s'], 'L1_attn_Wq': _L1_attn_in['Wq'], 'L1_attn_bq': _L1_attn_in['bq'], 'L1_attn_Wk': _L1_attn_in['Wk'], 'L1_attn_bk': _L1_attn_in['bk'], 'L1_attn_Wv': _L1_attn_in['Wv'], 'L1_attn_bv': _L1_attn_in['bv'], 'L1_attn_Wo': _L1_attn_in['Wo'], 'L1_attn_bo': _L1_attn_in['bo'], 'L1_xattn_Wq': _L1_xattn_in['Wq'], 'L1_xattn_Wkv': _L1_xattn_in['Wkv'], 'L1_ffn_W1': _L1_ffn_in['W1'], 'L1_ffn_b1': _L1_ffn_in['b1'], 'L1_ffn_W2': _L1_ffn_in['W2'], 'L1_ffn_b2': _L1_ffn_in['b2'], 'L2_attn_W_in': _L2_attn_in['W_in'], 'L2_attn_W_gate': _L2_attn_in['W_gate'], 'L2_attn_conv_w': _L2_attn_in['conv_w'], 'L2_attn_conv_b': _L2_attn_in['conv_b'], 'L2_attn_W_out': _L2_attn_in['W_out'], 'L2_attn_rg_in_w': _L2_attn_in['rg_in_w'], 'L2_attn_rg_in_b': _L2_attn_in['rg_in_b'], 'L2_attn_rg_gate_w': _L2_attn_in['rg_gate_w'], 'L2_attn_rg_gate_b': _L2_attn_in['rg_gate_b'], 'L2_attn_forget_lambda': _L2_attn_in['forget_lambda'], 'L2_attn_mlp_gate_w': _L2_attn_in['mlp_gate_w'], 'L2_attn_mlp_up_w': _L2_attn_in['mlp_up_w'], 'L2_attn_mlp_down_w': _L2_attn_in['mlp_down_w'], 'L2_attn_norm1_w': _L2_attn_in['norm1_w'], 'L2_attn_norm2_w': _L2_attn_in['norm2_w'], 'L2_xattn_Wq': _L2_xattn_in['Wq'], 'L2_xattn_Wk': _L2_xattn_in['Wk'], 'L2_xattn_Wv': _L2_xattn_in['Wv'], 'L2_xattn_Wo': _L2_xattn_in['Wo'], 'L2_ffn_sim_matrix': _L2_ffn_in['sim_matrix'], 'L2_ffn_gates': _L2_ffn_in['gates'], 'L2_ffn_q_proj': _L2_ffn_in['q_proj'], 'L2_ffn_k_proj': _L2_ffn_in['k_proj'], 'L2_ffn_v_proj': _L2_ffn_in['v_proj'], 'L2_ffn_o_proj': _L2_ffn_in['o_proj'], 'L3_attn_W_Q': _L3_attn_in['W_Q'], 'L3_attn_W_K': _L3_attn_in['W_K'], 'L3_attn_W_V': _L3_attn_in['W_V'], 'L3_attn_W_G': _L3_attn_in['W_G'], 'L3_attn_W_O': _L3_attn_in['W_O'], 'L3_attn_gn_weight': _L3_attn_in['gn_weight'], 'L3_attn_gn_bias': _L3_attn_in['gn_bias'], 'L3_xattn_Wq': _L3_xattn_in['Wq'], 'L3_xattn_bq': _L3_xattn_in['bq'], 'L3_xattn_Wk': _L3_xattn_in['Wk'], 'L3_xattn_bk': _L3_xattn_in['bk'], 'L3_xattn_Wv': _L3_xattn_in['Wv'], 'L3_xattn_bv': _L3_xattn_in['bv'], 'L3_xattn_Wo': _L3_xattn_in['Wo'], 'L3_xattn_bo': _L3_xattn_in['bo'], 'L3_ffn_gate': _L3_ffn_in['gate'], 'L3_ffn_experts_w1': _L3_ffn_in['experts_w1'], 'L3_ffn_experts_w2': _L3_ffn_in['experts_w2'], 'L3_ffn_experts_w3': _L3_ffn_in['experts_w3']}

def reference(x, ctx_1024, mask_BxS2_bf1, mask_Bx1x1xS2_ik0, L0_attn_W_Q, L0_attn_W_K, L0_attn_W_V, L0_attn_W_O, L0_xattn_Wq, L0_xattn_bq, L0_xattn_Wk, L0_xattn_bk, L0_xattn_Wv, L0_xattn_bv, L0_xattn_Wo, L0_xattn_bo, L0_ffn_w1_w, L0_ffn_w1_s, L0_ffn_w2_w, L0_ffn_w2_s, L0_ffn_h1_w, L0_ffn_h1_s, L0_ffn_h2_w, L0_ffn_h2_s, L0_ffn_w3_w, L0_ffn_w3_s, L1_attn_Wq, L1_attn_bq, L1_attn_Wk, L1_attn_bk, L1_attn_Wv, L1_attn_bv, L1_attn_Wo, L1_attn_bo, L1_xattn_Wq, L1_xattn_Wkv, L1_ffn_W1, L1_ffn_b1, L1_ffn_W2, L1_ffn_b2, L2_attn_W_in, L2_attn_W_gate, L2_attn_conv_w, L2_attn_conv_b, L2_attn_W_out, L2_attn_rg_in_w, L2_attn_rg_in_b, L2_attn_rg_gate_w, L2_attn_rg_gate_b, L2_attn_forget_lambda, L2_attn_mlp_gate_w, L2_attn_mlp_up_w, L2_attn_mlp_down_w, L2_attn_norm1_w, L2_attn_norm2_w, L2_xattn_Wq, L2_xattn_Wk, L2_xattn_Wv, L2_xattn_Wo, L2_ffn_sim_matrix, L2_ffn_gates, L2_ffn_q_proj, L2_ffn_k_proj, L2_ffn_v_proj, L2_ffn_o_proj, L3_attn_W_Q, L3_attn_W_K, L3_attn_W_V, L3_attn_W_G, L3_attn_W_O, L3_attn_gn_weight, L3_attn_gn_bias, L3_xattn_Wq, L3_xattn_bq, L3_xattn_Wk, L3_xattn_bk, L3_xattn_Wv, L3_xattn_bv, L3_xattn_Wo, L3_xattn_bo, L3_ffn_gate, L3_ffn_experts_w1, L3_ffn_experts_w2, L3_ffn_experts_w3):
    import jax
    import jax.numpy as jnp

    def _L0_attn_ref(in_features, W_Q, W_K, W_V, W_O):
        import jax, jax.numpy as jnp
        import numpy as np
        NUM_HEADS = 16
        THETA = 10000.0

        def _rope(x, theta):
            S, d_k = (x.shape[1], x.shape[-1])
            k = jnp.arange(d_k // 2, dtype=jnp.float32)
            inv_freq = theta ** (-2.0 * k / d_k)
            ang = jnp.arange(S, dtype=jnp.float32)[:, None] * inv_freq
            cos = jnp.cos(ang)[None, :, None, :]
            sin = jnp.sin(ang)[None, :, None, :]
            x_even = x[..., 0::2]
            x_odd = x[..., 1::2]
            y_even = cos * x_even - sin * x_odd
            y_odd = sin * x_even + cos * x_odd
            y = jnp.stack([y_even, y_odd], axis=-1)
            return y.reshape(x.shape)
        B, S, D = in_features.shape
        H = NUM_HEADS
        d_k = D // H
        scale = 1.0 / np.sqrt(np.float32(d_k))
        q = jnp.einsum('kd,bsd->bsk', W_Q, in_features).reshape(B, S, H, d_k)
        k = jnp.einsum('kd,bsd->bsk', W_K, in_features).reshape(B, S, H, d_k)
        v = jnp.einsum('vd,bsd->bsv', W_V, in_features).reshape(B, S, H, d_k)
        q = _rope(q, THETA)
        k = _rope(k, THETA)
        q = q.transpose(0, 2, 1, 3)
        k = k.transpose(0, 2, 1, 3)
        v = v.transpose(0, 2, 1, 3)
        scores = jnp.einsum('bhqd,bhkd->bhqk', q, k) * scale
        causal = jnp.tril(jnp.ones((S, S), dtype=bool))
        scores = jnp.where(causal[None, None], scores, -jnp.inf)
        attn = jax.nn.softmax(scores, axis=-1)
        out = jnp.einsum('bhqk,bhkd->bhqd', attn, v)
        out = out.transpose(0, 2, 1, 3).reshape(B, S, D)
        return jnp.einsum('dv,bsv->bsd', W_O, out)

    def _L0_xattn_ref(q_in, k_in, v_in, key_mask, Wq, bq, Wk, bk, Wv, bv, Wo, bo):
        import jax, jax.numpy as jnp
        import numpy as np
        HEADS, QSIZE, KSIZE = (16, 64, 64)
        B, M, _ = q_in.shape
        N = k_in.shape[1]
        qw = (q_in @ Wq + bq).reshape(B, M, HEADS, QSIZE)
        kw = (k_in @ Wk + bk).reshape(B, N, HEADS, QSIZE)
        vw = (v_in @ Wv + bv).reshape(B, N, HEADS, KSIZE)
        a = jnp.einsum('bmhd,bnhd->bhmn', qw, kw) / jnp.sqrt(jnp.float32(QSIZE))
        a = jnp.where(key_mask[:, None, None, :], a, -jnp.inf)
        a = jax.nn.softmax(a, axis=-1)
        o = jnp.einsum('bhmn,bnhd->bmhd', a, vw).reshape(B, M, HEADS * KSIZE)
        return o @ Wo + bo

    def _L0_ffn_ref(x, w1_w, w1_s, w2_w, w2_s, h1_w, h1_s, h2_w, h2_s, w3_w, w3_s):
        import jax, jax.numpy as jnp
        import numpy as np
        D_IN, D_HID = (128, 512)

        def _ternary(key, shape):
            return jax.random.randint(key, shape, -1, 2).astype(jnp.float32)

        def _tlin(x, w, s):
            return jnp.einsum('bsi,oi->bso', x, w) * s
        h = jax.nn.silu(_tlin(x, w1_w, w1_s)) * _tlin(x, w2_w, w2_s)
        h = jax.nn.gelu(_tlin(h, h1_w, h1_s), approximate=False)
        h = jax.nn.gelu(_tlin(h, h2_w, h2_s), approximate=False)
        return _tlin(h, w3_w, w3_s)

    def _L1_attn_ref(x, Wq, bq, Wk, bk, Wv, bv, Wo, bo):
        import math
        import jax, jax.numpy as jnp
        import numpy as np
        NHEAD = 16
        HEAD_DIM = 64
        D_MODEL = 128
        B, T = (2, 512)

        def _cosformer(x, Wq, bq, Wk, bk, Wv, bv, Wo, bo):
            Bsz, Tlen, _ = x.shape
            H, dh = (NHEAD, HEAD_DIM)
            Q = (x @ Wq + bq).reshape(Bsz, Tlen, H, dh)
            K = (x @ Wk + bk).reshape(Bsz, Tlen, H, dh)
            V = (x @ Wv + bv).reshape(Bsz, Tlen, H, dh)
            Qp = jax.nn.relu(Q)
            Kp = jax.nn.relu(K)
            angles = math.pi / (2.0 * Tlen) * jnp.arange(Tlen, dtype=jnp.float32)
            cosw = jnp.cos(angles)[None, :, None, None]
            sinw = jnp.sin(angles)[None, :, None, None]
            Qc, Qs = (Qp * cosw, Qp * sinw)
            Kc, Ks = (Kp * cosw, Kp * sinw)
            tm = lambda a: jnp.moveaxis(a, 1, 0)
            Qc, Qs, Kc, Ks, Vt = (tm(Qc), tm(Qs), tm(Kc), tm(Ks), tm(V))
            S0 = jnp.zeros((Bsz, H, dh, dh), dtype=x.dtype)
            z0 = jnp.zeros((Bsz, H, dh), dtype=x.dtype)

            def step(carry, inp):
                S_cos, S_sin, z_cos, z_sin = carry
                qc, qs, kc, ks_, v = inp
                S_cos = S_cos + kc[..., :, None] * v[..., None, :]
                S_sin = S_sin + ks_[..., :, None] * v[..., None, :]
                z_cos = z_cos + kc
                z_sin = z_sin + ks_
                num = jnp.einsum('bhi,bhij->bhj', qc, S_cos) + jnp.einsum('bhi,bhij->bhj', qs, S_sin)
                den = jnp.sum(qc * z_cos + qs * z_sin, axis=-1)
                den = jnp.maximum(den, 1e-06)[..., None]
                return ((S_cos, S_sin, z_cos, z_sin), num / den)
            _, out = jax.lax.scan(step, (S0, S0, z0, z0), (Qc, Qs, Kc, Ks, Vt))
            out = jnp.moveaxis(out, 0, 1).reshape(Bsz, Tlen, H * dh)
            return out @ Wo + bo
        return _cosformer(x, Wq, bq, Wk, bk, Wv, bv, Wo, bo)

    def _L1_xattn_ref(hidden_states, decoder_hidden_states, Wq, Wkv):
        import jax, jax.numpy as jnp
        import numpy as np
        EMBED_DIM = 128
        B, QL, KL = (4, 256, 256)
        d = Wq.shape[0]
        scale = 1.0 / np.sqrt(d)
        query = hidden_states @ Wq
        kv = decoder_hidden_states @ Wkv
        key, value = jnp.split(kv, 2, axis=-1)
        scores = jnp.einsum('bqd,bkd->bqk', query, key) * scale
        w = jax.nn.softmax(scores, axis=-1)
        return jnp.einsum('bqk,bkd->bqd', w, value)

    def _L1_ffn_ref(x, W1, b1, W2, b2):
        import jax, jax.numpy as jnp
        import numpy as np
        EMB = 128
        FF = 4 * EMB

        def _ternary(w):
            scale = jnp.maximum(jnp.mean(jnp.abs(w)), 1e-08)
            w_t = jnp.clip(jnp.round(w / scale), -1.0, 1.0)
            return w + jax.lax.stop_gradient(w_t - w)
        h = jnp.einsum('bsd,fd->bsf', x, _ternary(W1)) + b1
        h = jax.nn.gelu(h, approximate=False)
        out = jnp.einsum('bsf,df->bsd', h, _ternary(W2)) + b2
        return out

    def _L2_attn_ref(x, W_in, W_gate, conv_w, conv_b, W_out, rg_in_w, rg_in_b, rg_gate_w, rg_gate_b, forget_lambda, mlp_gate_w, mlp_up_w, mlp_down_w, norm1_w, norm2_w):
        import jax, jax.numpy as jnp
        import numpy as np
        DIM, HID, K, B, S = (128, 192, 4, 4, 512)
        EPS = 1e-05
        C = 8.0

        def rmsnorm(x, w):
            return x * jax.lax.rsqrt(jnp.mean(x * x, axis=-1, keepdims=True) + EPS) * w

        def _rg_lru(u, rg_in_w, rg_in_b, rg_gate_w, rg_gate_b, forget_lambda):
            ig = jnp.einsum('bsh,gh->bsg', u, rg_in_w) + rg_in_b
            rg = jnp.einsum('bsh,gh->bsg', u, rg_gate_w) + rg_gate_b
            alpha = jnp.exp(-C * jax.nn.softplus(forget_lambda) * jax.nn.sigmoid(rg))
            beta = jnp.sqrt(1.0 - alpha * alpha + 1e-06)
            xbeta = beta * jax.nn.sigmoid(ig) * u

            def combine(e1, e2):
                a1, b1 = e1
                a2, b2 = e2
                return (a2 * a1, a2 * b1 + b2)
            _, h = jax.lax.associative_scan(combine, (alpha, xbeta), axis=1)
            return h
        seq_len = x.shape[1]
        h = rmsnorm(x, norm1_w)
        gate = jnp.einsum('bsd,hd->bsh', h, W_gate)
        u = jnp.einsum('bsd,hd->bsh', h, W_in)
        uc = jax.lax.conv_general_dilated(u.transpose(0, 2, 1), conv_w, window_strides=(1,), padding=[(K - 1, 0)], dimension_numbers=('NCH', 'OIH', 'NCH'), feature_group_count=HID)
        u = (uc + conv_b[None, :, None]).transpose(0, 2, 1)[:, :seq_len, :]
        hrec = _rg_lru(u, rg_in_w, rg_in_b, rg_gate_w, rg_gate_b, forget_lambda)
        mix = jnp.einsum('bsh,dh->bsd', jax.nn.gelu(gate, approximate=False) * hrec, W_out)
        x = x + mix
        n2 = rmsnorm(x, norm2_w)
        g = jax.nn.gelu(jnp.einsum('bsd,hd->bsh', n2, mlp_gate_w), approximate=False)
        up = jnp.einsum('bsd,hd->bsh', n2, mlp_up_w)
        mlp = jnp.einsum('bsh,dh->bsd', g * up, mlp_down_w)
        return x + mlp

    def _L2_xattn_ref(query, key, value, Wq, Wk, Wv, Wo):
        import jax, jax.numpy as jnp
        import numpy as np
        EMBED_DIM = 128
        NUM_HEADS = 16
        HEAD_DIM = EMBED_DIM // NUM_HEADS
        B, L, E = query.shape
        H, D = (NUM_HEADS, HEAD_DIM)
        scale = D ** (-0.5)
        q = (query @ Wq.T).reshape(B, L, H, D) * scale
        k = (key @ Wk.T).reshape(B, -1, H, D)
        v = (value @ Wv.T).reshape(B, -1, H, D)
        scores = jax.nn.sigmoid(jnp.einsum('blhd,bshd->bhls', q, k))
        o = jnp.einsum('bhls,bshd->blhd', scores, v).reshape(B, L, E)
        return o @ Wo.T

    def _L2_ffn_ref(hidden_states, sim_matrix, gates, q_proj, k_proj, v_proj, o_proj):
        import jax, jax.numpy as jnp
        import numpy as np
        B, T, C, H, E, MIN_E = (4, 256, 128, 128, 16, 2)
        IS_CAUSAL = False

        def _forward(hidden_states, sim_matrix, gates, q_proj, k_proj, v_proj, o_proj):
            b, t, c = hidden_states.shape
            n = b * t
            x = hidden_states.reshape(n, c)
            xn = x / jnp.maximum(jnp.linalg.norm(x, axis=-1, keepdims=True), 1e-12)
            sn = sim_matrix / jnp.maximum(jnp.linalg.norm(sim_matrix, axis=0, keepdims=True), 1e-12)
            logits = xn @ sn - jax.nn.sigmoid(gates)
            gated = jax.nn.relu(logits)
            hard = (gated > 0).astype(gated.dtype)
            mask = gated + jax.lax.stop_gradient(hard - gated)
            inactive = jnp.sum(hard, axis=1) == 0
            _, fb_idx = jax.lax.top_k(logits, MIN_E)
            fb = jnp.zeros((n, logits.shape[1]), gated.dtype).at[jnp.arange(n)[:, None], fb_idx].set(1.0)
            put = jax.lax.stop_gradient(inactive[:, None].astype(gated.dtype) * fb)
            mask = mask * (1.0 - put) + put
            masked = jnp.where(mask > 0, gated, -jnp.inf)
            w = jax.nn.softmax(masked, axis=-1)

            def moe_proj(p):
                y = jnp.einsum('nc,ech->neh', x, p)
                return jnp.einsum('ne,neh->nh', w, y)
            q = moe_proj(q_proj).reshape(b, t, -1)
            k = moe_proj(k_proj).reshape(b, t, -1)
            v = moe_proj(v_proj).reshape(b, t, -1)
            h = q.shape[-1]
            scores = jnp.einsum('bth,bsh->bts', q, k) / jnp.sqrt(jnp.asarray(h, q.dtype))
            if IS_CAUSAL and t > 1:
                causal = jnp.tril(jnp.ones((t, t), bool))
                scores = jnp.where(causal[None], scores, -jnp.inf)
            attn = jax.nn.softmax(scores, axis=-1)
            o = jnp.einsum('bts,bsh->bth', attn, v).reshape(n, h)
            z = jnp.einsum('ne,nh->enh', w, o)
            out = jnp.einsum('enh,ehc->nc', z, o_proj)
            return out.reshape(b, t, c)
        return _forward(hidden_states, sim_matrix, gates, q_proj, k_proj, v_proj, o_proj)

    def _L3_attn_ref(X, W_Q, W_K, W_V, W_G, W_O, gn_weight, gn_bias):
        import math
        import jax, jax.numpy as jnp
        import numpy as np
        HEADS = 8
        SCALE_BASE = 512.0
        GN_EPS = 1e-05

        def _gammas(heads):
            return 1.0 - np.exp(np.linspace(math.log(1.0 / 32.0), math.log(1.0 / 512.0), heads))

        def _xpos(x, downscale):
            N, S, d = x.shape
            half = d // 2
            scale = (jnp.arange(0, d, 2, dtype=jnp.float32) + 0.4 * d) / (1.4 * d)
            pos = jnp.arange(S, dtype=jnp.float32)
            sc = scale[None, :] ** (pos / SCALE_BASE)[:, None]
            inv_freq = 1.0 / 10000.0 ** (jnp.arange(half, dtype=jnp.float32) / half)
            sinusoid = pos[:, None] * inv_freq[None, :]
            sin, cos = (jnp.sin(sinusoid), jnp.cos(sinusoid))
            if downscale:
                sc = 1.0 / sc
            sin_s = jnp.repeat(sin * sc, 2, axis=-1)
            cos_s = jnp.repeat(cos * sc, 2, axis=-1)
            x1, x2 = (x[..., ::2], x[..., 1::2])
            rot = jnp.stack((-x2, x1), axis=-1).reshape(x.shape)
            return x * cos_s + rot * sin_s
        B, S, H = X.shape
        h = HEADS
        d = H // h
        gammas = jnp.asarray(_gammas(h), dtype=X.dtype)
        Xh = X.reshape(B, S, h, d)
        Q = jnp.einsum('bshd,hde->bhse', Xh, W_Q)
        K = jnp.einsum('bshd,hde->bhse', Xh, W_K)
        V = jnp.einsum('bshd,hde->bhse', Xh, W_V)
        Q = _xpos(Q.reshape(B * h, S, d), downscale=False).reshape(B, h, S, d)
        K = _xpos(K.reshape(B * h, S, d), downscale=True).reshape(B, h, S, d)
        n = jnp.arange(S)
        diff = n[:, None] - n[None, :]
        causal = diff >= 0
        D = gammas[:, None, None] ** jnp.where(causal, diff, 0).astype(X.dtype) * causal[None].astype(X.dtype)
        att = jnp.einsum('bhsd,bhtd->bhst', Q, K) * D[None]
        Y = jnp.einsum('bhst,bhtd->bshd', att, V).reshape(B, S, H)
        Yg = Y.reshape(B * S, h, d)
        mu = Yg.mean(axis=-1, keepdims=True)
        var = Yg.var(axis=-1, keepdims=True)
        Yn = ((Yg - mu) / jnp.sqrt(var + GN_EPS)).reshape(B * S, H)
        Yn = (Yn * gn_weight + gn_bias).reshape(B, S, H)
        G = X @ W_G
        return G * jax.nn.sigmoid(G) * Yn @ W_O

    def _L3_xattn_ref(Q, K, V, mask, Wq, bq, Wk, bk, Wv, bv, Wo, bo):
        import jax, jax.numpy as jnp
        import numpy as np
        BS, SEQ, D_MODEL, N_HEADS = (4, 256, 128, 16)
        D_HEAD = D_MODEL // N_HEADS

        def _split_heads(x):
            b, s, _ = x.shape
            return x.reshape(b, s, N_HEADS, D_HEAD).transpose(0, 2, 1, 3)
        q = _split_heads(Q @ Wq.T + bq)
        k = _split_heads(K @ Wk.T + bk)
        v = _split_heads(V @ Wv.T + bv)
        scores = jnp.einsum('bhqd,bhkd->bhqk', q, k) / np.sqrt(D_HEAD).astype(np.float32)
        scores = jnp.where(mask == 0, jnp.float32(-1000000000.0), scores)
        attn = jax.nn.softmax(scores, axis=-1)
        ctx = jnp.einsum('bhqk,bhkd->bhqd', attn, v)
        b, h, s, d = ctx.shape
        ctx = ctx.transpose(0, 2, 1, 3).reshape(b, s, h * d)
        return ctx @ Wo.T + bo

    def _L3_ffn_ref(x, gate, experts_w1, experts_w2, experts_w3):
        import jax, jax.numpy as jnp
        import numpy as np
        W_SCALE = 0.02
        TOP_K = 2
        E = experts_w1.shape[0]
        router_logits = jnp.einsum('bsh,he->bse', x, gate)
        routing_weights, selected = jax.lax.top_k(router_logits, TOP_K)
        routing_weights = jax.nn.softmax(routing_weights, axis=-1)
        onehot = jax.nn.one_hot(selected, E, dtype=x.dtype)
        tok_w = jnp.einsum('bsk,bske->bse', routing_weights, onehot)
        g = jnp.einsum('bsh,ehi->ebsi', x, experts_w1)
        u = jnp.einsum('bsh,ehi->ebsi', x, experts_w3)
        hid = jax.nn.silu(g) * u
        eo = jnp.einsum('ebsi,eih->ebsh', hid, experts_w2)
        out = jnp.einsum('ebsh,bse->bsh', eo, tok_w)
        return out
    x = x + _L0_attn_ref(_layernorm(x, axis=-1), L0_attn_W_Q, L0_attn_W_K, L0_attn_W_V, L0_attn_W_O)
    x = x + _L0_xattn_ref(_layernorm(x, axis=-1), ctx_1024, ctx_1024, mask_BxS2_bf1, L0_xattn_Wq, L0_xattn_bq, L0_xattn_Wk, L0_xattn_bk, L0_xattn_Wv, L0_xattn_bv, L0_xattn_Wo, L0_xattn_bo)
    x = x + _L0_ffn_ref(_layernorm(x, axis=-1), L0_ffn_w1_w, L0_ffn_w1_s, L0_ffn_w2_w, L0_ffn_w2_s, L0_ffn_h1_w, L0_ffn_h1_s, L0_ffn_h2_w, L0_ffn_h2_s, L0_ffn_w3_w, L0_ffn_w3_s)
    x = x + _L1_attn_ref(_layernorm(x, axis=-1), L1_attn_Wq, L1_attn_bq, L1_attn_Wk, L1_attn_bk, L1_attn_Wv, L1_attn_bv, L1_attn_Wo, L1_attn_bo)
    x = x + _L1_xattn_ref(_layernorm(x, axis=-1), ctx_1024, L1_xattn_Wq, L1_xattn_Wkv)
    x = x + _L1_ffn_ref(_layernorm(x, axis=-1), L1_ffn_W1, L1_ffn_b1, L1_ffn_W2, L1_ffn_b2)
    x = x + _L2_attn_ref(_layernorm(x, axis=-1), L2_attn_W_in, L2_attn_W_gate, L2_attn_conv_w, L2_attn_conv_b, L2_attn_W_out, L2_attn_rg_in_w, L2_attn_rg_in_b, L2_attn_rg_gate_w, L2_attn_rg_gate_b, L2_attn_forget_lambda, L2_attn_mlp_gate_w, L2_attn_mlp_up_w, L2_attn_mlp_down_w, L2_attn_norm1_w, L2_attn_norm2_w)
    x = x + _L2_xattn_ref(_layernorm(x, axis=-1), ctx_1024, ctx_1024, L2_xattn_Wq, L2_xattn_Wk, L2_xattn_Wv, L2_xattn_Wo)
    x = x + _L2_ffn_ref(_layernorm(x, axis=-1), L2_ffn_sim_matrix, L2_ffn_gates, L2_ffn_q_proj, L2_ffn_k_proj, L2_ffn_v_proj, L2_ffn_o_proj)
    x = x + _L3_attn_ref(_layernorm(x, axis=-1), L3_attn_W_Q, L3_attn_W_K, L3_attn_W_V, L3_attn_W_G, L3_attn_W_O, L3_attn_gn_weight, L3_attn_gn_bias)
    x = x + _L3_xattn_ref(_layernorm(x, axis=-1), ctx_1024, ctx_1024, mask_Bx1x1xS2_ik0, L3_xattn_Wq, L3_xattn_bq, L3_xattn_Wk, L3_xattn_bk, L3_xattn_Wv, L3_xattn_bv, L3_xattn_Wo, L3_xattn_bo)
    x = x + _L3_ffn_ref(_layernorm(x, axis=-1), L3_ffn_gate, L3_ffn_experts_w1, L3_ffn_experts_w2, L3_ffn_experts_w3)
    return x

_drawn_inputs = setup_inputs


def setup_inputs(seed=0):
    import zlib

    import numpy as np

    out = dict(_drawn_inputs(seed))
    spreads = {'L0_xattn_bq': (0.0, 0.1),
     'L0_xattn_bk': (0.0, 0.1),
     'L0_xattn_bv': (0.0, 0.1),
     'L0_xattn_bo': (0.0, 0.1),
     'L1_attn_bq': (0.0, 0.1),
     'L1_attn_bk': (0.0, 0.1),
     'L1_attn_bv': (0.0, 0.1),
     'L1_attn_bo': (0.0, 0.1),
     'L2_attn_rg_in_b': (0.0, 0.1),
     'L2_attn_rg_gate_b': (0.0, 0.1),
     'L2_attn_norm1_w': (1.0, 0.2),
     'L2_attn_norm2_w': (1.0, 0.2),
     'L2_ffn_gates': (0.0, 0.1),
     'L3_attn_gn_weight': (1.0, 0.2),
     'L3_attn_gn_bias': (0.0, 0.1),
     'L3_xattn_bq': (0.0, 0.1),
     'L3_xattn_bk': (0.0, 0.1),
     'L3_xattn_bv': (0.0, 0.1),
     'L3_xattn_bo': (0.0, 0.1)}
    factors = {}
    for name, (base, spread) in spreads.items():
        noise = np.random.default_rng([zlib.crc32(name.encode()), seed]).standard_normal(out[name].shape)
        drawn = base * np.exp(spread * noise) if base else spread * noise
        out[name] = jnp.asarray(drawn.astype(out[name].dtype))
    for name, factor in factors.items():
        out[name] = (out[name] * factor).astype(out[name].dtype)
    return out
```

```python
from contextlib import ExitStack, contextmanager
import math

import numpy as np

import concourse.bass as bass
from concourse import mybir

F32 = mybir.dt.float32
BF16 = mybir.dt.bfloat16
I32 = mybir.dt.int32
U32 = mybir.dt.uint32
U8 = mybir.dt.uint8
ALU = mybir.AluOpType
ACT = mybir.ActivationFunctionType
AX = mybir.AxisListType.X

D = 128
S = 1024
HALF = 512
TOK_TILES = S // 128
CHUNK = 512
TPC = CHUNK // 128
LN_EPS = 1e-5
MASKED = -1e9
START = 512
LAYERS = list(range(12))


class Signal:

    def __init__(self, prog, name):
        self.prog, self.sem, self.n = prog, prog.ctx.enter_context(prog.nc.semaphore(name)), 0
        prog.counted.append(self)

    def now(self):
        return Mark(self, self.n, list(self.prog.frames))

    def count(self, instruction, by=1):
        instruction.then_inc(self.sem, by)
        self.n += by
        return self.now()


class Mark:

    def __init__(self, sig, n, frames):
        self.sig, self.n, self.frames = sig, n, frames

    def key(self):
        return len(self.frames), self.n

    def value(self):
        v = self.n
        for f in self.frames:
            if f.per.get(self.sig, 0):
                v = f.reg * f.per[self.sig] + v
        return v


class Ring:

    def __init__(self, prog, label, n):
        self.prog, self.label, self.n, self.marks = prog, label, n, {}

    def get(self, slot):
        if slot in self.marks:
            return self.marks[slot]
        if not self.prog.frames:
            return []
        return self.prog.lags(f"{self.label}{slot}")

    def put(self, slot, marks):
        self.marks[slot] = marks

    def close(self):
        for slot, marks in self.marks.items():
            for k, m in enumerate(marks):
                self.prog.name(f"{self.label}{slot}.{k}", m)


class Frame:

    def __init__(self, reg, per, base):
        self.reg, self.per, self.base, self.names = reg, per, base, {}


class Engine:
    def __init__(self, prog, e, name):
        self.prog, self.e, self.sig, self.waited = prog, e, Signal(prog, name), {}

    def wait(self, *marks):
        need = {}

        def gather(m):
            if isinstance(m, Mark):
                have = need.get(m.sig)
                if have is None or m.key() > have.key():
                    need[m.sig] = m
            elif m is not None:
                for x in m:
                    gather(x)
        gather(marks)
        for sig, m in need.items():
            if m.n <= 0 or self.waited.get(sig, (0, 0)) >= m.key():
                continue
            self.waited[sig] = m.key()
            v = m.value()
            self.e.wait_ge(sig.sem, v)
            if self is self.prog.sp and not isinstance(v, int):
                self.prog.settle(self)

    def __call__(self, marks, op, *a, **k):
        self.wait(marks)
        return self.sig.count(op(*a, **k))

    def quiet(self, marks, op, *a, **k):
        self.wait(marks)
        op(*a, **k)

    def dma(self, marks, sig, out, in_):
        self.wait(marks)
        return sig.count(self.e.dma_start(out, in_), 16)


class Prog:
    def __init__(self, nc, ctx, counts):
        self.nc, self.ctx, self.counts, self.seen = nc, ctx, counts, []
        self.frames, self.counted, self.tiles = [], [], 0
        self.pe = Engine(self, nc.tensor, "pe_done")
        self.act = Engine(self, nc.scalar, "act_done")
        self.dve = Engine(self, nc.vector, "dve_done")
        self.pool = Engine(self, nc.gpsimd, "pool_done")
        self.sp = Engine(self, nc.sync, "sp_done")
        self.engines = (self.pe, self.act, self.dve, self.pool, self.sp)
        self.ps = ctx.enter_context(nc.psum_tensor("ps", [128, 8, HALF], F32))
        self.free = [None] * 8
        self.turn = 0
        self.banks = list(range(8))
        self.loads = {}
        for e in self.engines:
            e.e.sem_inc(e.sig.sem, START)
            e.sig.n = START
        self.barrier()

    def stream(self, name):
        if name not in self.loads:
            self.loads[name] = Signal(self, name)
        return self.loads[name]

    def barrier(self):
        for e in self.engines:
            if e is not self.sp:
                e.wait(e.sig.now())
        for sig in self.loads.values():
            self.sp.wait(sig.now())
        self.nc.all_engine_barrier()
        for e in self.engines:
            for sig in self.counted:
                e.waited[sig] = (len(self.frames), sig.n)
        self.free = [None] * 8

    def settle(self, e):
        e.e.sem_inc(e.sig.sem, 1)
        e.sig.n += 1

    def meet(self):
        marks = self.all_now()
        for e in self.engines:
            e.wait(marks)
            if e is not self.sp:
                self.settle(e)

    def meet_engines(self):
        marks = [e.sig.now() for e in self.engines]
        for e in self.engines:
            e.wait(marks)
            if e is not self.sp:
                self.settle(e)

    def all_now(self):
        return [s.now() for s in self.counted]

    def name_if(self, label, mark):
        if self.frames:
            self.name(label, mark)

    def lags_of(self, label):
        return [self.lag(label)] if label in self.frames[-1].known else []

    @contextmanager
    def loop(self, count):
        key = len(self.seen)
        self.seen.append(None)
        known = self.counts.get(key)
        with self.nc.Fori(0, count) as reg:
            per = {s: known[0][n] for n, s in enumerate(self.counted)} if known else {}
            f = Frame(reg, per, {s: s.n for s in self.counted})
            f.known = known[1] if known else {}
            self.frames.append(f)
            for e in self.engines:
                e.waited = {}
            yield reg
            self.frames.pop()
            grown = [s.n - f.base.get(s, 0) for s in self.counted]
        self.counts[key] = (grown, f.names)
        for s, g in zip(self.counted, grown):
            s.n = f.base.get(s, 0) + g * count
        for e in self.engines:
            e.waited = {}

    def name(self, label, mark):
        f = self.frames[-1]
        f.names[label] = (self.counted.index(mark.sig), mark.n - f.base.get(mark.sig, 0))
        return mark

    def lag(self, label):
        f = self.frames[-1]
        index, off = f.known.get(label, (0, 0))
        sig = self.counted[index]
        per = f.per.get(sig, 0)
        return Mark(sig, f.base.get(sig, 0) + off - per, list(self.frames))

    def lags(self, label):
        names = [n for n in self.frames[-1].known if n.rsplit(".", 1)[0] == label]
        return [self.lag(n) for n in names]

    def bank(self):
        b = self.banks[self.turn % len(self.banks)]
        self.turn += 1
        self.pe.wait(self.free[b])
        return b



def halves():
    return [slice(h * HALF, (h + 1) * HALF) for h in range(S // HALF)]


def load(P, stack, name, src, shape=None, dt=F32, dst=None):
    shape = list(shape or src.shape)
    t = tile(P, stack, name, shape, dt)
    P.sp.dma(None, P.stream("weights"), t[:] if dst is None else dst(t), src)
    return t


def tile(P, stack, name, shape, dt=F32):
    P.tiles += 1
    return stack.enter_context(P.nc.sbuf_tensor(f"{name}_{P.tiles}", list(shape), dt))


def linear(P, marks, weights, inputs, n_out, evacuate, width=None):
    out = []
    cols = [slice(0, width)] if width else halves()
    for m in range(n_out):
        for h, sl in enumerate(cols):
            b = P.bank()
            n = len(inputs)
            for k in range(n):
                w = weights(k, m)
                ps = P.ps[0:w.shape[-1], b, 0:sl.stop - sl.start]
                mark = P.pe(marks, P.nc.tensor.matmul, ps, lhsT=w, rhs=inputs[k][:, sl], start=k == 0, stop=k == n - 1)
            P.free[b] = evacuate(m, sl, ps, mark)
            out.append(P.free[b])
    return out


def normalize(P, C, marks, src, dst, tmp, center=True, weight=None):
    nc = P.nc
    done = []
    for sl in halves():
        base = src
        m = marks
        if center:
            b = P.bank()
            t = P.pe(marks, nc.tensor.matmul, P.ps[:, b, :], lhsT=C.mean[:], rhs=src[:, sl], start=True, stop=True)
            m = P.dve([t, marks], nc.vector.tensor_tensor, dst[:, sl], src[:, sl], P.ps[:, b, :], ALU.subtract)
            P.free[b] = m
            base = dst
        q = P.act([m, marks], nc.scalar.activation, tmp[:, sl], base[:, sl], ACT.Square)
        b = P.bank()
        t = P.pe([q], nc.tensor.matmul, P.ps[:, b, :], lhsT=C.mean[:], rhs=tmp[:, sl], start=True, stop=True)
        r = P.act([t], nc.scalar.activation, tmp[:, sl], P.ps[:, b, :], ACT.Sqrt, bias=C.eps[:, 0:1])
        P.free[b] = r
        r = P.dve([r], nc.vector.reciprocal, tmp[:, sl], tmp[:, sl])
        if weight is None:
            r = P.dve([r], nc.vector.tensor_tensor, dst[:, sl], base[:, sl], tmp[:, sl], ALU.mult)
        else:
            r = P.dve([r], nc.vector.scalar_tensor_tensor, dst[:, sl], base[:, sl], weight, tmp[:, sl], ALU.mult, ALU.mult)
        done.append(r)
    return done


def add_to_x(P, X, bias=None):
    def evacuate(m, sl, ps, mark):
        if bias is None:
            return P.dve([mark], P.nc.vector.tensor_tensor, X[:, sl], X[:, sl], ps, ALU.add)
        return P.dve([mark], P.nc.vector.scalar_tensor_tensor, X[:, sl], ps, bias, X[:, sl], ALU.add, ALU.add)
    return evacuate


def ffn_ternary_gated(P, C, io, X, stack):
    nc = P.nc
    F = io["L0_ffn_w1_w"].shape[1]
    T = F // 128
    w1, w2 = (load(P, stack, n, io[n]) for n in ("L0_ffn_w1_w", "L0_ffn_w2_w"))
    h1, h2 = (load(P, stack, n, io[n].rearrange("(k p) n -> p k n", p=128), [128, T, F])
              for n in ("L0_ffn_h1_w", "L0_ffn_h2_w"))
    w3 = load(P, stack, "w3", io["L0_ffn_w3_w"].rearrange("(k p) n -> p k n", p=128), [128, T, D])
    s1, s2, t1, t2 = (load(P, stack, n, io[n])
                      for n in ("L0_ffn_w1_s", "L0_ffn_w2_s", "L0_ffn_h1_s", "L0_ffn_h2_s"))
    s3 = load(P, stack, "s3", io["L0_ffn_w3_s"])
    wts = P.stream("weights").now()
    h, tmp = tile(P, stack, "h", [D, S]), tile(P, stack, "tmp", [D, S])
    a, b = tile(P, stack, "a", [128, T, S]), tile(P, stack, "b", [128, T, S])
    n = normalize(P, C, [], X, h, tmp)
    gates = linear(P, [n, wts], lambda k, m: w1[:, m * 128:(m + 1) * 128], [h], T, lambda m, sl, ps, t: P.act(
        [t], nc.scalar.activation, a[:, m, sl], ps, ACT.Silu, scale=s1[:, m:m + 1]))
    up = linear(P, [], lambda k, m: w2[:, m * 128:(m + 1) * 128], [h], T, lambda m, sl, ps, t: P.dve(
        [t, gates], nc.vector.scalar_tensor_tensor, a[:, m, sl], ps, s2[:, m:m + 1], a[:, m, sl], ALU.mult, ALU.mult))
    one = linear(P, [up], lambda k, m: h1[:, k, m * 128:(m + 1) * 128], [a[:, k, :] for k in range(T)], T,
                 lambda m, sl, ps, t: P.act([t], nc.scalar.activation, b[:, m, sl], ps, ACT.Gelu, scale=t1[:, m:m + 1]))
    two = linear(P, [one], lambda k, m: h2[:, k, m * 128:(m + 1) * 128], [b[:, k, :] for k in range(T)], T,
                 lambda m, sl, ps, t: P.act([t], nc.scalar.activation, a[:, m, sl], ps, ACT.Gelu, scale=t2[:, m:m + 1]))
    linear(P, [two], lambda k, m: w3[:, k, :], [a[:, k, :] for k in range(T)], 1, lambda m, sl, ps, t: P.dve(
        [t], nc.vector.scalar_tensor_tensor, X[:, sl], ps, s3[:, 0:1], X[:, sl], ALU.mult, ALU.add))


def ternary(P, C, marks, w, work, stack, name):
    nc = P.nc
    n = w.shape[-1]
    s = tile(P, stack, name, [128, 4])
    r = P.dve([marks], nc.vector.tensor_reduce, s[:, 0:1], w, AX, ALU.add, apply_absolute_value=True)
    b = P.bank()
    t = P.pe([r], nc.tensor.matmul, P.ps[:, b, 0:1], lhsT=C.mean[:], rhs=s[:, 0:1], start=True, stop=True)
    r = P.dve([t], nc.vector.tensor_scalar, s[:, 1:2], P.ps[:, b, 0:1], 1.0 / n, 1e-8, ALU.mult, ALU.max)
    P.free[b] = r
    r1 = P.dve([r], nc.vector.tensor_scalar, s[:, 2:3], s[:, 1:2], 0.5, None, ALU.mult)
    r2 = P.dve([r], nc.vector.tensor_scalar, s[:, 3:4], s[:, 1:2], -0.5, None, ALU.mult)
    r = P.dve([r1, r2], nc.vector.tensor_scalar, work, w, s[:, 3:4], None, ALU.is_lt)
    r = P.dve([r], nc.vector.scalar_tensor_tensor, work, w, s[:, 2:3], work, ALU.is_gt, ALU.subtract)
    r = P.dve([r], nc.vector.tensor_tensor, work, work, w, ALU.subtract)
    return P.dve([r], nc.vector.tensor_tensor, w, w, work, ALU.add)


def ffn_ternary_gelu(P, C, io, X, stack):
    nc = P.nc
    F = io["L1_ffn_W1"].shape[1]
    T = F // 128
    w1 = load(P, stack, "w1", io["L1_ffn_W1"])
    w2 = load(P, stack, "w2", io["L1_ffn_W2"].rearrange("(k p) n -> p k n", p=128), [128, T, D])
    b1 = load(P, stack, "b1", io["L1_ffn_b1"])
    b2 = load(P, stack, "b2", io["L1_ffn_b2"])
    wts = P.stream("weights").now()
    h, tmp = tile(P, stack, "h", [D, S]), tile(P, stack, "tmp", [D, S])
    work, a = tile(P, stack, "work", [128, F]), tile(P, stack, "a", [128, T, S])
    flat2 = w2[:].rearrange("p k n -> p (k n)")
    m1 = ternary(P, C, [wts], w1[:], work[:], stack, "scale1")
    m2 = ternary(P, C, [wts, m1], flat2, work[:], stack, "scale2")
    n = normalize(P, C, [], X, h, tmp)
    hid = linear(P, [n, m1], lambda k, m: w1[:, m * 128:(m + 1) * 128], [h], T, lambda m, sl, ps, t: P.act(
        [t], nc.scalar.activation, a[:, m, sl], ps, ACT.Gelu, bias=b1[:, m:m + 1]))
    linear(P, [hid, m2], lambda k, m: w2[:, k, :], [a[:, k, :] for k in range(T)], 1, add_to_x(P, X, b2[:, 0:1]))


def recurrent_block(P, C, io, X, stack):
    nc = P.nc
    HID = io["L2_attn_W_in"].shape[1]
    R, T = HID // 2, 2
    K = io["L2_attn_conv_w"].shape[-1]
    col = lambda n: load(P, stack, n, io[n])
    w_in, w_gate, m_gate, m_up = (load(P, stack, n, io["L2_attn_" + n]) for n in ("W_in", "W_gate", "mlp_gate_w", "mlp_up_w"))
    rg_in, rg_gate, w_out, m_down = (load(P, stack, n, io["L2_attn_" + n].rearrange("(t p) n -> p t n", p=R),
                                          [R, T, io["L2_attn_" + n].shape[1]]) for n in ("rg_in_w", "rg_gate_w", "W_out", "mlp_down_w"))
    conv_w = load(P, stack, "conv_w", io["L2_attn_conv_w"].rearrange("(t p) a k -> p t (a k)", p=R), [R, T, K])
    conv_b, in_b, gate_b, lam = (col("L2_attn_" + n) for n in ("conv_b", "rg_in_b", "rg_gate_b", "forget_lambda"))
    n1, n2 = (load(P, stack, n, io["L2_attn_" + n]) for n in ("norm1_w", "norm2_w"))
    wts = P.stream("weights").now()
    x, h, tmp = (tile(P, stack, n, [D, S]) for n in ("x", "h", "tmp"))
    u_pad = tile(P, stack, "u_pad", [R, T, K - 1 + S])
    gate, u, ig, rg, t1 = (tile(P, stack, n, [R, T, S]) for n in ("gate", "u", "ig", "rg", "t1"))
    c = tile(P, stack, "c", [R, 2, T])
    r = P.act([wts], nc.scalar.activation, c[:, 0, :], lam[:], ACT.Abs)
    r = P.act([r], nc.scalar.activation, c[:, 0, :], c[:, 0, :], ACT.Exp, scale=-1.0)
    r = P.act([r], nc.scalar.activation, c[:, 0, :], c[:, 0, :], ACT.Ln, bias=1.0)
    r = P.dve([r, wts], nc.vector.scalar_tensor_tensor, c[:, 1, :], lam[:], 0.0, c[:, 0, :], ALU.max, ALU.add)
    decay = P.dve([r], nc.vector.tensor_scalar, c[:, 1, :], c[:, 1, :], -8.0, None, ALU.mult)
    zero = P.dve([], nc.vector.memset, u_pad[:, :, 0:K - 1], 0.0)

    n = normalize(P, C, [], X, x, tmp)
    n = normalize(P, C, [n, wts], x, h, tmp, center=False, weight=n1[:, 0:1])
    tiles = lambda w: (lambda k, m: w[:, m * R:(m + 1) * R])
    deep = lambda w: (lambda k, m: w[:, k, m * R:(m + 1) * R])
    gates = linear(P, [n], tiles(w_gate), [h], T, lambda m, sl, ps, t: P.act([t], nc.scalar.activation, gate[:, m, sl], ps, ACT.Gelu))
    us = linear(P, [n], tiles(w_in), [h], T, lambda m, sl, ps, t: P.act(
        [t], nc.scalar.copy, u_pad[:, m, K - 1 + sl.start:K - 1 + sl.stop], ps))
    conv = []
    for m in range(T):
        r = P.dve([us, zero], nc.vector.tensor_scalar, u[:, m, :], u_pad[:, m, 0:S], conv_w[:, m, 0:1], conv_b[:, m:m + 1], ALU.mult, ALU.add)
        for k in range(1, K):
            r = P.dve([r], nc.vector.scalar_tensor_tensor, u[:, m, :], u_pad[:, m, k:k + S], conv_w[:, m, k:k + 1], u[:, m, :], ALU.mult, ALU.add)
        conv.append(r)
    us = [u[:, k, :] for k in range(T)]
    igs = linear(P, [conv], deep(rg_in), us, T, lambda m, sl, ps, t: P.act([t], nc.scalar.activation, ig[:, m, sl], ps, ACT.Sigmoid, bias=in_b[:, m:m + 1]))
    rgs = linear(P, [conv], deep(rg_gate), us, T, lambda m, sl, ps, t: P.act([t], nc.scalar.activation, rg[:, m, sl], ps, ACT.Sigmoid, bias=gate_b[:, m:m + 1]))
    recs = []
    for m in range(T):
        a = P.act([rgs, decay], nc.scalar.activation, rg[:, m, :], rg[:, m, :], ACT.Exp, scale=c[:, 1, m:m + 1])
        b = P.act([a], nc.scalar.activation, t1[:, m, :], rg[:, m, :], ACT.Square)
        b = P.act([b], nc.scalar.activation, t1[:, m, :], t1[:, m, :], ACT.Sqrt, scale=-1.0, bias=C.one_eps[0:R, 0:1])
        b = P.dve([b, igs], nc.vector.tensor_tensor, t1[:, m, :], t1[:, m, :], ig[:, m, :], ALU.mult)
        b = P.dve([b], nc.vector.tensor_tensor, t1[:, m, :], t1[:, m, :], u[:, m, :], ALU.mult)
        b = P.dve([a, b], nc.vector.tensor_tensor_scan, ig[:, m, :], rg[:, m, :], t1[:, m, :], 0.0, ALU.mult, ALU.add)
        recs.append(P.dve([b, gates], nc.vector.tensor_tensor, ig[:, m, :], ig[:, m, :], gate[:, m, :], ALU.mult))
    mix = linear(P, [recs], lambda k, m: w_out[:, k, :], [ig[:, k, :] for k in range(T)], 1, add_to_x(P, x))
    n = normalize(P, C, [mix], x, h, tmp, center=False, weight=n2[:, 0:1])
    gs = linear(P, [n], tiles(m_gate), [h], T, lambda m, sl, ps, t: P.act([t], nc.scalar.activation, gate[:, m, sl], ps, ACT.Gelu))
    gs = linear(P, [n], tiles(m_up), [h], T, lambda m, sl, ps, t: P.dve([t, gs], nc.vector.tensor_tensor, gate[:, m, sl], ps, gate[:, m, sl], ALU.mult))
    outs = linear(P, [gs], lambda k, m: m_down[:, k, :], [gate[:, k, :] for k in range(T)], 1, add_to_x(P, x))
    for sl in halves():
        P.dve([outs], nc.vector.tensor_tensor, X[:, sl], X[:, sl], x[:, sl], ALU.add)


def transpose_back(P, C, marks, src, dst, parts):
    nc = P.nc
    out = []
    for h, sl in enumerate(halves()):
        b = P.bank()
        for j in range(4):
            t = P.pe(marks, nc.tensor.transpose, P.ps[0:parts, b, j * 128:(j + 1) * 128], src[:, 4 * h + j, :], C.ident[:])
        P.free[b] = P.act([t], nc.scalar.copy, dst[:, sl], P.ps[0:parts, b, :])
        out.append(P.free[b])
    return out


def one_hot_rows(P, C, marks, rows, n, sel):
    z = P.pool(marks, P.nc.gpsimd.memset, sel[:], 0.0)
    return P.pool([z], P.nc.gpsimd.affine_select, out=sel[:], in_=sel[:], compare_op=ALU.not_equal, fill=1.0, base=0,
                  pattern=[[-1, n], [0, 128]], channel_multiplier=1)


def ffn_experts(P, C, io, X, stack):
    nc = P.nc
    E, F = io["L3_ffn_experts_w1"].shape[0], io["L3_ffn_experts_w1"].shape[2]
    T = F // 128
    gate = load(P, stack, "gate", io["L3_ffn_gate"])
    w1, w3 = (tile(P, stack, n, [128, 2, F]) for n in ("w1", "w3"))
    w2 = tile(P, stack, "w2", [128, 2, T, D])
    wts = P.stream("weights").now()
    h, tmp, acc = (tile(P, stack, n, [D, S]) for n in ("h", "tmp", "acc"))
    a = tile(P, stack, "a", [128, T, S])
    logits, w, hot = (tile(P, stack, n, [128, TOK_TILES, E]) for n in ("logits", "w", "hot"))
    top, both = tile(P, stack, "top", [128, TOK_TILES, 8]), tile(P, stack, "both", [128, TOK_TILES, 2])
    which, whichf = tile(P, stack, "which", [128, TOK_TILES, 8], U32), tile(P, stack, "whichf", [128, TOK_TILES, 8])
    number = tile(P, stack, "number", [128, E])
    wT, wB = tile(P, stack, "wT", [E, S]), tile(P, stack, "wB", [128, E, S])
    sel = tile(P, stack, "sel", [E, E, 128])
    sels = one_hot_rows(P, C, [], None, E, sel)
    iot = P.pool([], nc.gpsimd.iota, number[:], [[1, E]], 0, 0, allow_small_or_imprecise_dtypes=True)
    loads = [P.stream("expert0"), P.stream("expert1")]

    def fetch(e, marks):
        for t, n in ((w1, "w1"), (w3, "w3")):
            P.sp.dma(marks, loads[e % 2], t[:, e % 2, :], io["L3_ffn_experts_" + n][e])
        return P.sp.dma(marks, loads[e % 2], w2[:, e % 2], io["L3_ffn_experts_w2"][e].rearrange("(k p) n -> p k n", p=128))

    here = [fetch(0, []), fetch(1, [])]
    n = normalize(P, C, [], X, h, tmp)
    b = P.bank()
    for j in range(TOK_TILES):
        t = P.pe([n, wts], nc.tensor.matmul, P.ps[:, b, j * E:(j + 1) * E], lhsT=h[:, j * 128:(j + 1) * 128], rhs=gate[:], start=True, stop=True)
    r = P.dve([t], nc.vector.tensor_copy, logits[:], P.ps[:, b, 0:TOK_TILES * E].rearrange("p (j e) -> p j e", e=E))
    P.free[b] = r
    for j in range(TOK_TILES):
        m = P.dve([r], nc.vector.max, top[:, j, :], logits[:, j, :])
        m = P.dve([m], nc.vector.max_index, which[:, j, :], top[:, j, :], logits[:, j, :])
    m = P.dve([m], nc.vector.tensor_copy, whichf[:], which[:])
    r = P.dve([m], nc.vector.tensor_tensor, both[:, :, 1:2], top[:, :, 1:2], top[:, :, 0:1], ALU.subtract)
    r = P.act([r], nc.scalar.activation, both[:, :, 1:2], both[:, :, 1:2], ACT.Exp)
    r = P.dve([r], nc.vector.tensor_scalar, both[:, :, 0:1], both[:, :, 1:2], 1.0, None, ALU.add)
    r = P.dve([r], nc.vector.reciprocal, both[:, :, 0:1], both[:, :, 0:1])
    r = P.dve([r], nc.vector.tensor_tensor, both[:, :, 1:2], both[:, :, 1:2], both[:, :, 0:1], ALU.mult)
    for j in range(TOK_TILES):
        q = P.dve([r, m, iot], nc.vector.tensor_scalar, w[:, j, :], number[:], whichf[:, j, 0:1], both[:, j, 0:1], ALU.is_equal, ALU.mult)
        p = P.dve([r], nc.vector.tensor_scalar, hot[:, j, :], number[:], whichf[:, j, 1:2], both[:, j, 1:2], ALU.is_equal, ALU.mult)
        q = P.dve([p, q], nc.vector.tensor_tensor, w[:, j, :], w[:, j, :], hot[:, j, :], ALU.add)
    t = transpose_back(P, C, [q], w, wT, E)
    spread = linear(P, [t, sels], lambda k, m: sel[:, m, :], [wT], E, lambda m, sl, ps, t: P.act([t], nc.scalar.copy, wB[:, m, sl], ps))
    zero = P.dve([], nc.vector.memset, acc[:], 0.0)
    last = [zero, spread]
    down = []
    for e in range(E):
        s = e % 2
        g = linear(P, [n, here[s], down], lambda k, m: w1[:, s, m * 128:(m + 1) * 128], [h], T, lambda m, sl, ps, t: P.act(
            [t, down], nc.scalar.activation, a[:, m, sl], ps, ACT.Silu))
        u = linear(P, [], lambda k, m: w3[:, s, m * 128:(m + 1) * 128], [h], T, lambda m, sl, ps, t: P.dve(
            [t, g], nc.vector.tensor_tensor, a[:, m, sl], ps, a[:, m, sl], ALU.mult))

        def weigh(m, sl, ps, t):
            q = P.dve([t, last], nc.vector.tensor_tensor, tmp[:, sl], ps, wB[:, e, sl], ALU.mult)
            P.dve([q], nc.vector.tensor_tensor, acc[:, sl], acc[:, sl], tmp[:, sl], ALU.add)
            return q
        down = linear(P, [u], lambda k, m: w2[:, s, k, :], [a[:, k, :] for k in range(T)], 1, weigh)
        last = [P.dve.sig.now()]
        if e + 2 < E:
            here[s] = fetch(e + 2, [P.pe.sig.now()])
    for sl in halves():
        P.dve(last, nc.vector.tensor_tensor, X[:, sl], X[:, sl], acc[:, sl], ALU.add)



def output_projection(P, C, marks, O, weight, X, stack, bias=None):
    parts = O.shape[-1] // 128
    OT = tile(P, stack, "OT", [128, parts, S])
    done = [transpose_back(P, C, marks, O[:, :, f * 128:(f + 1) * 128], OT[:, f, :], 128) for f in range(parts)]
    return linear(P, [done], weight, [OT[:, f, :] for f in range(parts)], 1, add_to_x(P, X, bias))


def values_by_token(P, marks, h, w, heads, dv, V, ones):
    nc = P.nc
    out = []
    width = min(HALF, heads * dv)
    if ones:
        out.append(P.pool([], nc.gpsimd.memset, V[:, :, :, dv:dv + 1], 1.0))
    for j in range(TOK_TILES):
        for c in range(heads * dv // width):
            b = P.bank()
            t = P.pe(marks, nc.tensor.matmul, P.ps[:, b, 0:width], lhsT=h[:, j * 128:(j + 1) * 128],
                     rhs=w[:, c * width:(c + 1) * width], start=True, stop=True)
            k = width // dv
            P.free[b] = P.act([t], nc.scalar.copy, V[:, j, c * k:(c + 1) * k, 0:dv], P.ps[:, b, 0:width].rearrange("p (h d) -> p h d", d=dv))
            out.append(P.free[b])
    return out


def head_of(V, head):
    n, d = V.shape[2], V.shape[3]
    return V[:].rearrange("p j h d -> p j (h d)")[:, :, bass.ds(head * d, d)]


def causal_products(P, C, make_head, heads, Q, K, V, dv, stack, finish):
    nc = P.nc
    Vh = tile(P, stack, "Vh", [128, 2, TOK_TILES, dv])
    A = tile(P, stack, "A", [128, 4, HALF])
    steps = [(half, k) for half in range(2) for k in range(TOK_TILES) if k * 128 < (half + 1) * HALF]
    with P.loop(heads // 2) as pair:
        banks, slots = Ring(P, "score_bank", 4), Ring(P, "A_slot", 4)
        dens = Ring(P, "denominator", 4)
        accs, head_in, vals = Ring(P, "accumulator", 4), Ring(P, "head", 2), Ring(P, "values", 2)
        n = 0
        for s in range(2):
            head = pair * 2 + s
            ready = make_head(s, head, head_in.get(s), banks)
            v = P.dve(vals.get(s), nc.vector.tensor_scalar, Vh[:, s], head_of(V, head), 1.0, None, ALU.mult)

            def products(half, k, slot, m):
                for j in range(4):
                    if half * 4 + j >= k:
                        t = P.pe([m, v], nc.tensor.matmul, P.ps[:, 4 + 2 * s + half, j * dv:(j + 1) * dv],
                                 lhsT=A[:, slot, j * 128:(j + 1) * 128], rhs=Vh[:, s, k, :], start=False, stop=True,
                                 skip_group_check=True)
                slots.put(slot, [t])
                return t

            for half in range(2):
                P.pe(accs.get(2 * s + half), nc.tensor.matmul, P.ps[:, 4 + 2 * s + half, 0:4 * dv], lhsT=C.zero[0:1, 0:128],
                     rhs=C.zero[0:1, 0:4 * dv], start=True, stop=True, skip_group_check=True)
            waiting = []
            for half, k in steps:
                slot = n % 4
                n += 1
                lo = max(0, k * 128 - half * HALF)
                t = P.pe([ready, banks.get(slot)], nc.tensor.matmul, P.ps[:, slot, lo:HALF], lhsT=K[:, s, k * 128:(k + 1) * 128],
                         rhs=Q[:, s, half * HALF + lo:(half + 1) * HALF], start=True, stop=True)
                src, dst, free = P.ps[:, slot, :], A[:, slot, :], slots.get(slot)
                if k * 128 >= half * HALF:
                    m = [P.dve([t, free], nc.vector.tensor_tensor, dst[:, lo:lo + 128], src[:, lo:lo + 128], C.causal[:], ALU.mult)]
                    if lo + 128 < HALF:
                        m.append(P.dve([], nc.vector.tensor_copy, dst[:, lo + 128:HALF], src[:, lo + 128:HALF]))
                else:
                    m = [P.act([t, free], nc.scalar.copy, dst, src)]
                banks.put(slot, m)
                waiting.append((half, k, slot, m))
                if len(waiting) > 2:
                    last = products(*waiting.pop(0))
            head_in.put(s, [t])
            while waiting:
                last = products(*waiting.pop(0))
            vals.put(s, [last])
            for half in range(2):
                view = P.ps[:, 4 + 2 * s + half, 0:4 * dv].rearrange("p (j d) -> p j d", d=dv)
                accs.put(2 * s + half, finish(s, head, half, view, [last], dens))
        for ring in (banks, slots, accs, head_in, vals, dens):
            ring.close()


def cosformer(P, C, io, X, stack):
    nc = P.nc
    H = 16
    d = io["L1_attn_Wq"].shape[1] // H
    wv = load(P, stack, "wv", io["L1_attn_Wv"])
    bv = load(P, stack, "bv", io["L1_attn_bv_row"])
    wo = load(P, stack, "wo", io["L1_attn_Wo"].rearrange("(k p) n -> p k n", p=128), [128, H * d // 128, D])
    bo = load(P, stack, "bo", io["L1_attn_bo"])
    bqk = tile(P, stack, "bqk", [128, 2, 2])
    cs = load(P, stack, "cs", io["cosformer_table"])
    wts = P.stream("weights").now()
    h, tmp = tile(P, stack, "h", [D, S]), tile(P, stack, "tmp", [D, S])
    V = tile(P, stack, "V", [128, TOK_TILES, H, d + 1])
    O = tile(P, stack, "O", [128, TOK_TILES, H * d])
    den = tile(P, stack, "den", [128, 4, 4])
    n = normalize(P, C, [], X, h, tmp)
    n = values_by_token(P, [n, wts], h, wv, H, d, V, True)
    add_row(P, C, n, V, bv, H, d)
    P.barrier()
    Q, K = (tile(P, stack, n, [128, 2, S]) for n in ("Q", "K"))
    w = tile(P, stack, "w", [128, 2, 2, 2 * d])
    arrive = [P.stream("head0"), P.stream("head1")]

    def make_head(s, head, free, banks):
        for j, name in enumerate(("L1_attn_Wq", "L1_attn_Wk")):
            for c in range(2):
                a = P.sp.dma([free], arrive[s], w[:, s, j, c * d:(c + 1) * d], io[name][:, bass.ds(head * d, d)])
        a = P.sp.dma([], arrive[s], bqk[:, s, :], io["L1_attn_bqk_twice"][bass.ds(head, 1)].rearrange("a p j -> p (a j)"))
        marks = []
        for j, dst in enumerate((Q, K)):
            for sl in halves():
                b = 2 * j + sl.start // HALF
                t = P.pe([a, banks.get(b)], nc.tensor.matmul, P.ps[:, b, :], lhsT=w[:, s, j, :], rhs=h[:, sl], start=True, stop=True)
                r = P.act([t, free], nc.scalar.activation, dst[:, s, sl], P.ps[:, b, :], ACT.Relu, bias=bqk[:, s, j:j + 1])
                banks.put(b, [r])
                marks.append(P.dve([r], nc.vector.tensor_tensor, dst[:, s, sl], dst[:, s, sl], cs[:, sl], ALU.mult))
        return marks

    def finish(s, head, half, view, marks, dens):
        z = 2 * s + half
        r = P.dve([marks, dens.get(z)], nc.vector.tensor_scalar, den[:, z, :], view[:, :, d], 1e-6, None, ALU.max)
        r = P.dve([r], nc.vector.reciprocal, den[:, z, :], den[:, z, :])
        for j in range(4):
            r2 = P.dve([r], nc.vector.tensor_scalar, O[:, half * 4 + j, bass.ds(head * d, d)], view[:, j, 0:d], den[:, z, j:j + 1], None, ALU.mult)
        dens.put(z, [r2])
        return [r2]

    causal_products(P, C, make_head, H, Q, K, V, d + 1, stack, finish)
    P.barrier()
    output_projection(P, C, [], O, lambda k, m: wo[:, k, :], X, stack, bo[:, 0:1])


def add_row(P, C, marks, V, row, H, d):
    nc = P.nc
    out = []
    for c in range(H * d // HALF):
        b = P.bank()
        t = P.pe(marks, nc.tensor.matmul, P.ps[:, b, :], lhsT=C.ones[0:1, :], rhs=row[0:1, c * HALF:(c + 1) * HALF], start=True, stop=True)
        k = HALF // d
        for j in range(V.shape[1]):
            v = V[:, j, c * k:(c + 1) * k, 0:d]
            P.free[b] = P.dve([t], nc.vector.tensor_tensor, v, v, P.ps[:, b, :].rearrange("p (h d) -> p h d", d=d), ALU.add)
        out.append(P.free[b])
    return out


def retention(P, C, io, X, stack):
    nc = P.nc
    H = D // 16
    d = D // H
    names = ("W_Q", "W_Q_turned", "W_K", "W_K_turned", "W_V", "W_G", "W_O")
    w = {n: load(P, stack, n, io["L3_attn_" + n]) for n in names}
    tables = {n: load(P, stack, n, io["retention_" + n]) for n in ("q_cos", "q_sin", "k_cos", "k_sin")}
    gw, gb = (load(P, stack, n, io["L3_attn_" + n]) for n in ("gn_weight", "gn_bias"))
    wts = P.stream("weights").now()
    h, tmp, tmp2 = (tile(P, stack, n, [D, S]) for n in ("h", "tmp", "tmp2"))
    V = tile(P, stack, "V", [128, TOK_TILES, H, d])
    O = tile(P, stack, "O", [128, TOK_TILES, D])
    n = normalize(P, C, [], X, h, tmp)
    v = values_by_token(P, [n, wts], h, w["W_V"], H, d, V, False)
    scratch = nc.dram_tensor("retention_heads", (2, D, S), F32, kind="Internal").ap()
    for j, x in enumerate("QK"):
        write_rotated(P, C, [n, wts], h, w["W_" + x], w["W_" + x + "_turned"], tables["q_cos" if x == "Q" else "k_cos"],
                      tables["q_sin" if x == "Q" else "k_sin"], tmp, tmp2, scratch[j])
    P.barrier()
    Q, K = (tile(P, stack, n, [d, 2, S]) for n in ("Q", "K"))
    arrive = [P.stream("head0"), P.stream("head1")]

    def make_head(s, head, free, banks):
        P.sp.dma([free], arrive[s], Q[:, s, :], scratch[0, bass.ds(head * d, d), :])
        return [P.sp.dma([], arrive[s], K[:, s, :], scratch[1, bass.ds(head * d, d), :])]

    def finish(s, head, half, view, marks, dens):
        return [P.dve(marks, nc.vector.tensor_scalar, O[:, half * 4:half * 4 + 4, bass.ds(head * d, d)], view, 1.0, None, ALU.mult)]

    causal_products(P, C, make_head, H, Q, K, V, d, stack, finish)
    P.barrier()
    G = TOK_TILES * H
    sq = tile(P, stack, "sq", [128, G, d])
    st = tile(P, stack, "st", [128, 2, G])
    Og = O[:].rearrange("p j (h d) -> p (j h) d", d=d)
    spread = lambda t: t.unsqueeze(2).to_broadcast([128, G, d])
    r = P.dve([], nc.vector.tensor_reduce, st[:, 0, :], Og, AX, ALU.add)
    r = P.dve([r], nc.vector.tensor_scalar, st[:, 0, :], st[:, 0, :], 1.0 / d, None, ALU.mult)
    r = P.dve([r], nc.vector.tensor_tensor, Og, Og, spread(st[:, 0, :]), ALU.subtract)
    q = P.dve([r], nc.vector.tensor_tensor, sq[:], Og, Og, ALU.mult)
    q = P.dve([q], nc.vector.tensor_reduce, st[:, 1, :], sq[:], AX, ALU.add)
    q = P.act([q], nc.scalar.activation, st[:, 1, :], st[:, 1, :], ACT.Sqrt, bias=C.eps[:, 0:1], scale=1.0 / d)
    q = P.dve([q], nc.vector.reciprocal, st[:, 1, :], st[:, 1, :])
    q = P.dve([q], nc.vector.tensor_tensor, Og, Og, spread(st[:, 1, :]), ALU.mult)
    y = transpose_back(P, C, [q], O[:], tmp, 128)
    y = P.dve([y], nc.vector.tensor_scalar, tmp[:], tmp[:], gw[:, 0:1], gb[:, 0:1], ALU.mult, ALU.add)
    g = linear(P, [], lambda k, m: w["W_G"][:], [h], 1, lambda m, sl, ps, t: P.act([t], nc.scalar.activation, tmp2[:, sl], ps, ACT.Silu))
    y = P.dve([y, g], nc.vector.tensor_tensor, tmp[:], tmp[:], tmp2[:], ALU.mult)
    linear(P, [y], lambda k, m: w["W_O"][:], [tmp], 1, add_to_x(P, X))


def write_rotated(P, C, marks, h, w, w_turned, cos, sin, a, b, dst):
    nc = P.nc
    stored = P.stream("stored")
    old = [stored.now()]
    done = []
    linear(P, [marks], lambda k, m: w[:], [h], 1, lambda m, sl, ps, t: P.dve([t, old], nc.vector.tensor_tensor, a[:, sl], ps, cos[:, sl], ALU.mult))

    def turned(m, sl, ps, t):
        r = P.dve([t], nc.vector.tensor_tensor, b[:, sl], ps, sin[:, sl], ALU.mult)
        done.append(P.dve([r], nc.vector.tensor_tensor, a[:, sl], a[:, sl], b[:, sl], ALU.add))
        return r
    linear(P, [marks], lambda k, m: w_turned[:], [h], 1, turned)
    return P.sp.dma(done, stored, dst, a[:])


def softmax_heads(P, C, head_in, Q, K, V, dv, O, causal, stack, pairs):
    nc = P.nc
    Pq, PT = tile(P, stack, "Pq", [128, 2, S]), tile(P, stack, "PT", [128, 2, S])
    st = tile(P, stack, "st", [128, 2, 4])

    def one(s, head, rings):
        scores, probs, turned, outs, ins, tbank = rings
        ready = head_in(s, head, ins.get(s))

        def front(q):
            p = q % 2
            n = (q + 1) * 128 if causal else S
            for c in range(0, n, HALF):
                w = min(HALF, n - c)
                t = P.pe([ready, scores.get(p)], nc.tensor.matmul, P.ps[:, 2 * p + c // HALF, 0:w], lhsT=Q[:, s, q * 128:(q + 1) * 128],
                         rhs=K[:, s, c:c + w], start=True, stop=True)
            ps = P.ps[:, 2 * p:2 * p + 2, :].rearrange("p a b -> p (a b)")[:, 0:n]
            if causal:
                t = P.dve([t], nc.vector.tensor_tensor, ps[:, n - 128:n], ps[:, n - 128:n], C.below[:], ALU.add)
            m = P.dve([t, probs.get(p)], nc.vector.tensor_reduce, st[:, p, 0:1], ps, AX, ALU.max, negate=True)
            e = P.act([m, t], nc.scalar.activation, Pq[:, p, 0:n], ps, ACT.Exp, bias=st[:, p, 0:1], accum_out=st[:, p, 1:2])
            scores.put(p, [e])
            return P.dve([e], nc.vector.reciprocal, st[:, p, 2:3], st[:, p, 1:2])

        def back(q, r):
            p = q % 2
            tiles = q + 1 if causal else TOK_TILES
            copies = []
            for c in range(0, tiles, 4):
                k = min(4, tiles - c)
                for j in range(c, c + k):
                    t = P.pe([r, tbank.get(c // 4)], nc.tensor.transpose, P.ps[:, 4 + c // 4, (j - c) * 128:(j - c + 1) * 128],
                             Pq[:, p, j * 128:(j + 1) * 128], C.ident[:])
                eng, op = ((P.act, nc.scalar.copy), (P.dve, nc.vector.tensor_copy))[(c // 4 + q) % 2]
                m = eng([t, turned.get(p)], op, PT[:, p, c * 128:(c + k) * 128], P.ps[:, 4 + c // 4, 0:k * 128])
                copies.append(m)
                tbank.put(c // 4, [m])
            for j in range(tiles):
                t = P.pe([copies, outs.get(p)], nc.tensor.matmul, P.ps[:, 6 + p, 0:dv], lhsT=PT[:, p, j * 128:(j + 1) * 128],
                         rhs=V[:, s, j, :], start=j == 0, stop=j == tiles - 1)
            turned.put(p, [t])
            dst = O[:, q, 0:dv] if pairs is None else O[:, q, bass.ds(head * dv, dv)]
            m = P.dve([t], nc.vector.tensor_scalar, dst, P.ps[:, 6 + p, 0:dv], st[:, p, 2:3], None, ALU.mult)
            outs.put(p, [m])
            probs.put(p, [t, m])
            return t

        r = front(0)
        for q in range(TOK_TILES):
            nxt = front(q + 1) if q + 1 < TOK_TILES else None
            t = back(q, r)
            r = nxt
        ins.put(s, [t])

    rings = lambda: [Ring(P, n, 2) for n in ("scores", "probs", "turned", "outs", "ins", "tbank")]
    if pairs is None:
        one(0, 0, rings())
    else:
        with P.loop(pairs) as pair:
            r = rings()
            for s in range(2):
                one(s, pair * 2 + s, r)
            for x in r:
                x.close()


def causal_attention(P, C, io, X, stack):
    nc = P.nc
    H = 16
    d = D // H
    w = {n: load(P, stack, n, io["L0_attn_" + n]) for n in ("W_Q", "W_Q_turned", "W_K", "W_K_turned", "W_V", "W_O")}
    tables = {n: load(P, stack, n, io["rope_" + n]) for n in ("q_cos", "q_sin", "k_cos", "k_sin")}
    wts = P.stream("weights").now()
    h, tmp, tmp2 = (tile(P, stack, n, [D, S]) for n in ("h", "tmp", "tmp2"))
    V = tile(P, stack, "V", [128, TOK_TILES, H, d])
    O = tile(P, stack, "O", [128, TOK_TILES, D])
    n = normalize(P, C, [], X, h, tmp)
    values_by_token(P, [n, wts], h, w["W_V"], H, d, V, False)
    scratch = nc.dram_tensor("rope_heads", (2, D, S), F32, kind="Internal").ap()
    for j, x in enumerate("QK"):
        write_rotated(P, C, [n, wts], h, w["W_" + x], w["W_" + x + "_turned"], tables["q_cos" if x == "Q" else "k_cos"],
                      tables["q_sin" if x == "Q" else "k_sin"], tmp, tmp2, scratch[j])
    P.barrier()
    Q, K = (tile(P, stack, n, [d, 2, S]) for n in ("Q", "K"))
    Vh = tile(P, stack, "Vh", [128, 2, TOK_TILES, d])
    arrive = [P.stream("head0"), P.stream("head1")]

    def head_in(s, head, free):
        P.sp.dma([free], arrive[s], Q[:, s, :], scratch[0, bass.ds(head * d, d), :])
        a = P.sp.dma([], arrive[s], K[:, s, :], scratch[1, bass.ds(head * d, d), :])
        return [a, P.dve(free, nc.vector.tensor_scalar, Vh[:, s], head_of(V, head), 1.0, None, ALU.mult)]

    softmax_heads(P, C, head_in, Q, K, Vh, d, O, True, stack, H // 2)
    P.barrier()
    output_projection(P, C, [], O, lambda k, m: w["W_O"][:], X, stack)


def attention_of_experts(P, C, io, X, stack):
    nc = P.nc
    E = io["L2_ffn_sim_matrix"].shape[1]
    sim = load(P, stack, "sim", io["L2_ffn_sim_matrix"])
    gates = load(P, stack, "gates", io["L2_ffn_gates_row"])
    wts = P.stream("weights").now()
    w = tile(P, stack, "w", [128, 2, 4, D])
    h, tmp = tile(P, stack, "h", [D, S]), tile(P, stack, "tmp", [D, S])
    wB = tile(P, stack, "wB", [128, E, S])
    xe = tile(P, stack, "xe", [128, 2, S])
    Q, K, Vt = (tile(P, stack, n, [128, 1, S]) for n in ("Q", "K", "Vt"))
    V = tile(P, stack, "V", [128, 1, TOK_TILES, D])
    O = tile(P, stack, "O", [128, TOK_TILES, D])
    sel, wT = tile(P, stack, "sel", [E, E, 128]), tile(P, stack, "wT", [E, S])
    loads = [P.stream("expert0"), P.stream("expert1")]
    sels = one_hot_rows(P, C, [], None, E, sel)
    names = ("q_proj", "k_proj", "v_proj", "o_proj")

    def fetch(e, marks, which):
        for n in which:
            a = P.sp.dma(marks, loads[e % 2], w[:, e % 2, n, :], io["L2_ffn_" + names[n]][e])
        return a
    here = [fetch(0, [], range(3)), fetch(1, [], range(3))]
    n = normalize(P, C, [], X, h, tmp)
    g = tile(P, stack, "g", [128, 4, E])
    r = P.act([wts], nc.scalar.activation, g[:, 0, :], sim[:], ACT.Square)
    b = P.bank()
    t = P.pe([r], nc.tensor.matmul, P.ps[:, b, 0:E], lhsT=C.mean[:], rhs=g[:, 0, :], start=True, stop=True)
    r = P.act([t], nc.scalar.activation, g[:, 1, :], P.ps[:, b, 0:E], ACT.Sqrt, scale=float(D))
    P.free[b] = r
    r = P.dve([r], nc.vector.tensor_scalar, g[:, 1, :], g[:, 1, :], 1e-12, None, ALU.max)
    r = P.dve([r], nc.vector.reciprocal, g[:, 1, :], g[:, 1, :])
    r = P.dve([r], nc.vector.tensor_tensor, g[:, 0, :], sim[:], g[:, 1, :], ALU.mult)
    b = P.bank()
    t = P.pe([], nc.tensor.matmul, P.ps[:, b, 0:E], lhsT=C.ones[0:1, :], rhs=gates[0:1, :], start=True, stop=True)
    s = P.act([t], nc.scalar.activation, g[:, 2, :], P.ps[:, b, 0:E], ACT.Sigmoid)
    P.free[b] = s
    q = P.act([n], nc.scalar.activation, tmp[:], h[:], ACT.Square)
    L = tile(P, stack, "L", [128, TOK_TILES, E])
    M, F = tile(P, stack, "M", [128, TOK_TILES, E]), tile(P, stack, "F", [128, TOK_TILES, E])
    top, which = tile(P, stack, "top", [128, TOK_TILES, 8]), tile(P, stack, "which", [128, TOK_TILES, 8], U32)
    whichf, norm = tile(P, stack, "whichf", [128, TOK_TILES, 8]), tile(P, stack, "norm", [128, TOK_TILES, 4])
    number = tile(P, stack, "number", [128, E])
    iot = P.pool([], nc.gpsimd.iota, number[:], [[1, E]], 0, 0, allow_small_or_imprecise_dtypes=True)
    b = P.bank()
    b2 = P.bank()
    for j in range(TOK_TILES):
        P.pe([q], nc.tensor.matmul, P.ps[:, b, j:j + 1], lhsT=tmp[:, j * 128:(j + 1) * 128], rhs=C.ones_col[:], start=True, stop=True)
        t = P.pe([r], nc.tensor.matmul, P.ps[:, b2, j * E:(j + 1) * E], lhsT=h[:, j * 128:(j + 1) * 128], rhs=g[:, 0, :], start=True, stop=True)
    r = P.act([t], nc.scalar.activation, norm[:, :, 0:1], P.ps[:, b, 0:TOK_TILES].unsqueeze(2), ACT.Sqrt)
    P.free[b] = r
    r = P.dve([r], nc.vector.tensor_scalar, norm[:, :, 0:1], norm[:, :, 0:1], 1e-12, None, ALU.max)
    r = P.dve([r], nc.vector.reciprocal, norm[:, :, 0:1], norm[:, :, 0:1])
    wide = lambda a: a.to_broadcast([128, TOK_TILES, E])
    each = lambda a: a.unsqueeze(1).to_broadcast([128, TOK_TILES, E])
    r = P.dve([r], nc.vector.tensor_tensor, L[:], P.ps[:, b2, 0:TOK_TILES * E].rearrange("p (j e) -> p j e", e=E), wide(norm[:, :, 0:1]), ALU.mult)
    P.free[b2] = r
    logits = P.dve([r, s], nc.vector.tensor_tensor, L[:], L[:], each(g[:, 2, :]), ALU.subtract)
    for j in range(TOK_TILES):
        m = P.dve([logits], nc.vector.max, top[:, j, :], L[:, j, :])
        m = P.dve([m], nc.vector.max_index, which[:, j, :], top[:, j, :], L[:, j, :])
    m = P.dve([m], nc.vector.tensor_copy, whichf[:], which[:])
    k = P.dve([logits], nc.vector.tensor_scalar, M[:], L[:], 0.0, None, ALU.is_gt)
    f = P.dve([m, iot], nc.vector.tensor_tensor, F[:], each(number[:]), wide(whichf[:, :, 0:1]), ALU.is_equal)
    f2 = P.dve([m, iot], nc.vector.tensor_tensor, wB[:, 0, 0:TOK_TILES * E].rearrange("p (j e) -> p j e", e=E), each(number[:]), wide(whichf[:, :, 1:2]), ALU.is_equal)
    f = P.dve([f, f2], nc.vector.tensor_tensor, F[:], F[:], wB[:, 0, 0:TOK_TILES * E].rearrange("p (j e) -> p j e", e=E), ALU.add)
    i = P.dve([m], nc.vector.tensor_scalar, norm[:, :, 1:2], top[:, :, 0:1], 0.0, None, ALU.is_le)
    f = P.dve([f, i], nc.vector.tensor_tensor, F[:], F[:], wide(norm[:, :, 1:2]), ALU.mult)
    k = P.dve([f, k], nc.vector.tensor_tensor, M[:], M[:], F[:], ALU.add)
    r = P.dve([m], nc.vector.tensor_scalar, norm[:, :, 2:3], top[:, :, 0:1], 0.0, None, ALU.max)
    r = P.dve([r, k, f], nc.vector.tensor_scalar, L[:], L[:], 0.0, None, ALU.max)
    r = P.dve([r], nc.vector.tensor_tensor, L[:], L[:], wide(norm[:, :, 2:3]), ALU.subtract)
    r = P.act([r], nc.scalar.activation, L[:], L[:], ACT.Exp)
    r = P.dve([r], nc.vector.tensor_tensor, L[:], L[:], M[:], ALU.mult)
    r2 = P.dve([r], nc.vector.tensor_reduce, norm[:, :, 3:4], L[:], AX, ALU.add)
    r2 = P.dve([r2], nc.vector.reciprocal, norm[:, :, 3:4], norm[:, :, 3:4])
    r2 = P.dve([r2], nc.vector.tensor_tensor, L[:], L[:], wide(norm[:, :, 3:4]), ALU.mult)
    t = transpose_back(P, C, [r2], L, wT, E)
    spread = linear(P, [t, sels, f], lambda k, m: sel[:, m, :], [wT], E, lambda m, sl, ps, t: P.act([t, f], nc.scalar.copy, wB[:, m, sl], ps))
    P.barrier()
    used = [[], []]
    for e in range(E):
        z = e % 2
        m = P.dve([used[z]], nc.vector.tensor_tensor, xe[:, z, :], h[:], wB[:, e, :], ALU.mult)
        for n in range(3):
            for i, sl in enumerate(halves()):
                t = P.pe([m, here[z]], nc.tensor.matmul, P.ps[:, 2 * n + i, :], lhsT=w[:, z, n, :], rhs=xe[:, z, sl], start=e == 0, stop=e == E - 1)
        used[z] = [t]
        if e + 2 < E:
            here[z] = fetch(e + 2, [t], range(3))
    out = []
    for n, dst in enumerate((Q, K, Vt)):
        for i, sl in enumerate(halves()):
            out.append(P.act([t], nc.scalar.activation, dst[:, 0, sl], P.ps[:, 2 * n + i, :], ACT.Copy, scale=1.0 / math.sqrt(D) if n == 0 else 1.0))
    here = [fetch(0, [t], [3]), fetch(1, [t], [3])]
    P.barrier()
    for i in range(2):
        b = P.bank()
        for j in range(4):
            t = P.pe([], nc.tensor.transpose, P.ps[:, b, j * 128:(j + 1) * 128], Vt[:, 0, (4 * i + j) * 128:(4 * i + j + 1) * 128], C.ident[:])
        P.free[b] = P.act([t], nc.scalar.copy, V[:, 0, 4 * i:4 * i + 4, :], P.ps[:, b, :].rearrange("p (j d) -> p j d", d=D))
    P.barrier()
    softmax_heads(P, C, lambda s, head, free: [], Q, K, V, D, O, False, stack, None)
    P.barrier()
    t = transpose_back(P, C, [], O[:], Q[:, 0, :], 128)
    P.barrier()
    used = [[], []]
    for e in range(E):
        z = e % 2
        m = P.dve([used[z]], nc.vector.tensor_tensor, xe[:, z, :], Q[:, 0, :], wB[:, e, :], ALU.mult)
        for i, sl in enumerate(halves()):
            t = P.pe([m, here[z]], nc.tensor.matmul, P.ps[:, i, :], lhsT=w[:, z, 3, :], rhs=xe[:, z, sl], start=e == 0, stop=e == E - 1)
        used[z] = [t]
        if e + 2 < E:
            here[z] = fetch(e + 2, [t], [3])
    for i, sl in enumerate(halves()):
        add_to_x(P, X)(0, sl, P.ps[:, i, :], t)



class Cross:

    def __init__(self, P, name, heads, d, split, softmax, masked):
        nc = P.nc
        self.name, self.H, self.d, self.split, self.softmax, self.masked = name, heads, d, split, softmax, masked
        self.dt = BF16 if split else F32
        self.rows = len(TERMS) * d if split else d
        self.dv = d + 1 if softmax else d
        dram = lambda n, shape, dt: nc.dram_tensor(f"{name}_dram_{n}", shape, dt, kind="Internal").ap()
        self.K = dram("K", (CHUNKS, heads, self.rows, CHUNK), self.dt)
        self.Q = dram("Q", (heads, self.rows, S), self.dt)
        self.V = dram("V", (CHUNKS, heads, 128, TPC * self.dv), F32)
        if softmax and not split:
            self.Kb, self.Qb = dram("Kb", (CHUNKS, heads, d, CHUNK), BF16), dram("Qb", (heads, d, S), BF16)
        if softmax:
            self.mask = dram("mask", (CHUNKS, CHUNK), F32)
            self.mask_parts = dram("mask_parts", (CHUNKS, 2, CHUNK), BF16)


TERMS = [(0, 0), (0, 1), (0, 2), (1, 0), (1, 1), (2, 0)]
CHUNKS = 0


def split_parts(P, marks, src, parts, rest):
    nc = P.nc
    a = P.dve([marks], nc.vector.tensor_copy, parts[:, 0], src)
    b = P.dve([a], nc.vector.tensor_tensor, rest, src, parts[:, 0], ALU.subtract)
    a = P.dve([b], nc.vector.tensor_copy, parts[:, 1], rest)
    b = P.dve([a], nc.vector.tensor_tensor, src, rest, parts[:, 1], ALU.subtract)
    return P.dve([b], nc.vector.tensor_copy, parts[:, 2], src)


def mask_rows(P, X, mask_src, fill, stack):
    nc = P.nc
    n = N_KEYS
    full, rest = n // CHUNK, n % CHUNK
    m = tile(P, stack, X.name + "_mask", [CHUNKS, CHUNK], F32)
    parts, t = tile(P, stack, X.name + "_mask_parts", [CHUNKS, 2, CHUNK], BF16), tile(P, stack, X.name + "_mask_rest", [CHUNKS, CHUNK])
    raw = tile(P, stack, X.name + "_mask_raw", [CHUNKS, CHUNK], I32 if mask_src is None else mask_src.dtype)
    z = P.dve([], nc.vector.memset, raw[:], 0)
    sig = P.stream("mask")
    src = P.io_ones if mask_src is None else mask_src
    if full:
        P.sp.dma([z], sig, raw[0:full, :], src[0:full * CHUNK].rearrange("(c n) -> c n", n=CHUNK))
    if rest:
        P.sp.dma([z], sig, raw[full:full + 1, 0:rest], src[full * CHUNK:n].unsqueeze(0))
    r = P.dve([sig.now()], nc.vector.tensor_copy, m[:], raw[:])
    r = P.dve([r], nc.vector.tensor_scalar, m[:], m[:], 0.0, fill, ALU.is_equal, ALU.mult)
    P.sp.dma([r], sig, X.mask, m[:])
    a = P.dve([r], nc.vector.tensor_copy, parts[:, 0, :], m[:])
    b = P.dve([a], nc.vector.tensor_tensor, t[:], m[:], parts[:, 0, :], ALU.subtract)
    a = P.dve([b], nc.vector.tensor_copy, parts[:, 1, :], t[:])
    P.sp.dma([a], sig, X.mask_parts, parts[:])


def keys_and_values(P, C, io, X, wk, bk, wv):
    nc = P.nc
    H, d, dv = X.H, X.d, X.dv
    F = H * d
    with ExitStack() as stack:
        if X.softmax:
            mask_rows(P, X, X.masked[0], X.masked[1], stack)
        wk_t, wv_t = (load(P, stack, n, w) for n, w in (("wk", wk), ("wv", wv)))
        bk_t = load(P, stack, "bk", bk) if bk is not None else None
        P.barrier()
        ctxt = tile(P, stack, "ctxt", [128, 2, CHUNK])
        valid = load(P, stack, "valid", io["valid_keys"])
        keep = tile(P, stack, "keep", [128, 2, CHUNK]) if X.split and X.softmax else None
        T = F // 128
        Kf = tile(P, stack, "Kf", [128, 2, T, CHUNK])
        Kb = tile(P, stack, "Kb", [128, 2, T, CHUNK], BF16) if not X.split and X.softmax else None
        parts, rest = (tile(P, stack, "parts", [128, 3, CHUNK], BF16), tile(P, stack, "rest", [128, CHUNK])) if X.split else (None, None)
        Vt = tile(P, stack, "Vt", [128, 2, H, TPC, dv])
        width = min(HALF, F)
        arrive, stored = [P.stream("chunk0"), P.stream("chunk1")], [P.stream("stored0"), P.stream("stored1")]
        P.barrier()

        def one(c, z, rings):
            banks, ins, outs, work = rings
            free = ins.get(z)
            a = P.sp.dma([free], arrive[z], ctxt[:, z, :], io["ctx_1024"][:, bass.ds(c * CHUNK, CHUNK)])
            if keep is not None:
                a = P.sp.dma([], arrive[z], keep[:, z, :], X.mask[bass.ds(c, 1), :].to_broadcast([128, CHUNK]))
            stores = []
            old = outs.get(z)
            n = 0
            for f in range(T):
                b = n % 8
                n += 1
                t = P.pe([a, banks.get(b)], nc.tensor.matmul, P.ps[:, b, :], lhsT=wk_t[:, f * 128:(f + 1) * 128], rhs=ctxt[:, z, :], start=True, stop=True)
                if bk_t is None:
                    r = P.act([t, old, work.get(0)], nc.scalar.copy, Kf[:, z, f, :], P.ps[:, b, :])
                else:
                    r = P.act([t, old, work.get(0)], nc.scalar.activation, Kf[:, z, f, :], P.ps[:, b, :], ACT.Identity, bias=bk_t[:, f:f + 1])
                banks.put(b, [r])
                if Kb is not None:
                    q = P.dve([r, old], nc.vector.tensor_copy, Kb[:, z, f, :], Kf[:, z, f, :])
                    stores.append((q, X.Kb[bass.ds(c, 1), f * 128 // d:(f + 1) * 128 // d].rearrange("a h r n -> (a h r) n"), Kb[:, z, f, :]))
                if not X.split:
                    stores.append((r, X.K[bass.ds(c, 1), f * 128 // d:(f + 1) * 128 // d].rearrange("a h r n -> (a h r) n"), Kf[:, z, f, :]))
            if X.split:
                if keep is not None:
                    k = P.dve([a, free], nc.vector.tensor_scalar, keep[:, z, :], keep[:, z, :], 0.0, None, ALU.is_equal)
                    r = P.dve([r, k], nc.vector.tensor_tensor, Kf[:, z, 0, :], Kf[:, z, 0, :], keep[:, z, :], ALU.mult)
                q = split_parts(P, [r, outs.get(2)], Kf[:, z, 0, :], parts, rest[:])
                work.put(0, [q])
                for g, (_, p) in enumerate(TERMS):
                    stores.append((q, X.K[bass.ds(c, 1), :, g * d:(g + 1) * d, :].rearrange("a h r n -> (a h) r n"), parts[:, p, :]))
            for j in range(TPC):
                for w in range(F // width):
                    b = n % 8
                    n += 1
                    t = P.pe([a, banks.get(b)], nc.tensor.matmul, P.ps[:, b, 0:width], lhsT=ctxt[:, z, j * 128:(j + 1) * 128],
                             rhs=wv_t[:, w * width:(w + 1) * width], start=True, stop=True)
                    k = width // d
                    r = P.dve([t, old], nc.vector.tensor_copy, Vt[:, z, w * k:(w + 1) * k, j, 0:d], P.ps[:, b, 0:width].rearrange("p (h d) -> p h d", d=d))
                    banks.put(b, [r])
                if X.softmax:
                    one_col = Vt[:, z, :, j, d:dv].rearrange("p h a -> p (h a)")
                    r = P.dve([old], nc.vector.tensor_scalar, one_col, C.ones16[:, 0:H], valid_chunk[:, z, j:j + 1], None, ALU.mult)
            ins.put(z, [t, r])
            stores.append((r, X.V[bass.ds(c, 1)].rearrange("a h p x -> p (a h) x"), Vt[:, z].rearrange("p h j x -> p h (j x)")))
            for m, dst, src in stores:
                s = P.sp.dma([m], stored[z], dst, src)
            outs.put(z, [s])
            outs.put(2, [s])

        valid_chunk = tile(P, stack, "valid_chunk", [128, 2, TPC])

        def chunk(c, z, rings):
            if X.softmax:
                P.dve([rings[1].get(z)], nc.vector.tensor_scalar, valid_chunk[:, z, :], valid[:, bass.ds(c * TPC, TPC)], 1.0, None, ALU.mult)
                P.dve.wait(P.dve.sig.now())
            one(c, z, rings)

        make = lambda: [Ring(P, n, k) for n, k in (("kv_bank", 8), ("ctx", 2), ("out", 3), ("work", 1))]
        with P.loop(CHUNKS // 2) as pair:
            rings = make()
            for z in range(2):
                chunk(pair * 2 + z, z, rings)
            for r in rings:
                r.close()
        P.barrier()
        if CHUNKS % 2:
            chunk(CHUNKS - 1, 0, make())
        P.barrier()


def queries(P, C, io, X, h, wq, bq, tmp):
    nc = P.nc
    scale = 1.0 / math.sqrt(X.d)
    with ExitStack() as stack:
        wq_t = load(P, stack, "wq", wq)
        bq_t = load(P, stack, "bq", bq) if bq is not None else None
        T = X.H * X.d // 128
        Qf = tile(P, stack, "Qf", [128, T, S])
        Qb = tile(P, stack, "Qb16", [128, T, S], BF16) if not X.split and X.softmax else None
        wts = P.stream("weights").now()
        sig = P.stream("stored0")
        r = linear(P, [wts, C.normed], lambda k, m: wq_t[:, m * 128:(m + 1) * 128], [h], T, lambda m, sl, ps, t: P.dve(
            [t], nc.vector.tensor_scalar, Qf[:, m, sl], ps, bq_t[:, m:m + 1] if bq_t is not None else 0.0, scale, ALU.add, ALU.mult))
        if X.split:
            parts, rest = tile(P, stack, "qparts", [128, 3, S], BF16), tile(P, stack, "qrest", [128, S])
            q = split_parts(P, [r], Qf[:, 0, :], parts, rest[:])
            for g, (p, _) in enumerate(TERMS):
                P.sp.dma([q], sig, X.Q[:, g * X.d:(g + 1) * X.d, :], parts[:, p, :])
        else:
            for f in range(T):
                k = slice(f * 128 // X.d, (f + 1) * 128 // X.d)
                P.sp.dma([r], sig, X.Q[k].rearrange("h r n -> (h r) n"), Qf[:, f, :])
                if Qb is not None:
                    q = P.act([r], nc.scalar.copy, Qb[:, f, :], Qf[:, f, :])
                    P.sp.dma([q], sig, X.Qb[k].rearrange("h r n -> (h r) n"), Qb[:, f, :])
        P.barrier()


def cross_heads(P, C, X, O, stack):
    nc = P.nc
    H, d, dv, rows, dt = X.H, X.d, X.dv, X.rows, X.dt
    wide = d == 128
    aux = {64: 64, 48: 64}.get(rows, 64)
    n_m = 1 if (dt == F32 and not wide) else 2
    total = rows if (wide or not X.softmax) else aux + 2 * n_m
    per_bank = 3 if wide else 4
    acc0 = 5 if wide else 6

    Kc = tile(P, stack, "Kc", [total, 2, CHUNK], dt)
    Vc = tile(P, stack, "Vc", [128, 2, TPC, dv])
    Qc = tile(P, stack, "Qc", [total, S], dt)
    Pr = tile(P, stack, "Pr", [128, TPC, S])
    kd, vd = [P.stream("key_chunk0"), P.stream("key_chunk1")], [P.stream("value_chunk0"), P.stream("value_chunk1")]
    q_in = P.stream("query")
    if X.softmax:
        pdt = BF16
        Kn = tile(P, stack, "Kn", [total, 2, CHUNK], pdt)
        Qn = tile(P, stack, "Qn", [total, S], pdt)
        mx, red = tile(P, stack, "mx", [128, TOK_TILES]), tile(P, stack, "red", [128, 2, TOK_TILES])
        mparts = tile(P, stack, "mparts", [128, 2, TOK_TILES], BF16)
        mneg, mrest = tile(P, stack, "mneg", [128, TOK_TILES]), tile(P, stack, "mrest", [128, TOK_TILES])
        kn = [P.stream("next_chunk0"), P.stream("next_chunk1")]
        if wide:
            Ka, Qa, Qa0 = tile(P, stack, "Ka", [4, 2, CHUNK], BF16), tile(P, stack, "Qa", [4, S], BF16), tile(P, stack, "Qa0", [4, S], BF16)
            z = P.dve([], nc.vector.memset, Ka[:], 1.0)
            z = P.dve([], nc.vector.memset, Qa[:], 1.0)
            z = P.dve([], nc.vector.memset, Qa0[:], 1.0)
            P.dve([z], nc.vector.memset, Qa0[0:2, :], 0.0)
        else:
            for t, v in ((Kc, 1.0), (Kn, 1.0)):
                if aux > rows:
                    P.dve([], nc.vector.memset, t[32:aux], 0.0)
                P.dve([], nc.vector.memset, t[aux:aux + n_m], v)
            for t in (Qc, Qn):
                if aux > rows:
                    P.dve([], nc.vector.memset, t[32:aux], 0.0)
                P.dve([], nc.vector.memset, t[aux:total], 1.0)
            P.barrier()
            P.dve([], nc.vector.memset, Qn[aux:aux + n_m], 0.0)
    P.barrier()

    def mask_into(marks, sig, dst, c):
        if wide:
            return P.sp.dma(marks, sig, dst, X.mask_parts[bass.ds(c, 1)].rearrange("a m n -> (a m) n"))
        if dst.dtype == F32:
            return P.sp.dma(marks, sig, dst, X.mask[bass.ds(c, 1), :])
        return P.sp.dma(marks, sig, dst, X.mask_parts[bass.ds(c, 1), 0:n_m].rearrange("a m n -> (a m) n"))

    def fetch(c, z, now, nxt, free):
        if now is not None:
            P.sp.dma(free, kd[z], Kc[0:rows, z, :], X.K[bass.ds(c, 1), bass.ds(now, 1)].rearrange("a h r n -> (a h r) n"))
            if X.softmax and not wide:
                mask_into([], kd[z], Kc[aux + n_m:total, z, :], c)
            P.name_if(f"keys{z}", kd[z].now())
            P.name_if(f"vals{z}", P.sp.dma([], vd[z], Vc[:, z].rearrange("p j x -> p (j x)"), X.V[bass.ds(c, 1), bass.ds(now, 1)].rearrange("a h p x -> (a h p) x")))
        if nxt is not None:
            src = X.K if X.split else X.Kb
            P.sp.dma(free, kn[z], Kn[0:rows, z, :], src[bass.ds(c, 1), bass.ds(nxt, 1)].rearrange("a h r n -> (a h r) n"))
            if not wide:
                mask_into([], kn[z], Kn[aux + n_m:total, z, :], c)
        if wide:
            mask_into(free, kn[z], Ka[2:4, z, :], c)
        if X.softmax:
            P.name_if(f"next{z}", kn[z].now())

    def chunk(z, now, nxt, rings, arrived):
        banks, probs, slots, nbanks, reds = rings
        keys, vals, nexts = arrived
        exps = {}

        def scores(t):
            b = t % 2
            for half, sl in enumerate(halves()):
                m = P.pe([keys, nexts if wide else None, banks.get(b)], nc.tensor.matmul, P.ps[:, 2 * b + half, :], lhsT=Kc[:, z, t * 128:(t + 1) * 128], rhs=Qc[:, sl],
                         start=True, stop=not wide)
                if wide:
                    m = P.pe([], nc.tensor.matmul, P.ps[:, 2 * b + half, :], lhsT=Ka[:, z, t * 128:(t + 1) * 128], rhs=Qa[:, sl], start=False, stop=True)
            e = P.act([m, probs.get(t)], nc.scalar.activation, Pr[:, t, :], P.ps[:, 2 * b:2 * b + 2, :].rearrange("p a n -> p (a n)"),
                      ACT.Exp if X.softmax else ACT.Sigmoid)
            banks.put(b, [e])
            exps[t] = e

        def products(t):
            for q in range(TOK_TILES):
                b, j = acc0 + q // per_bank, q % per_bank
                m = P.pe([exps[t], vals], nc.tensor.matmul, P.ps[:, b, j * dv:(j + 1) * dv], lhsT=Pr[:, t, q * 128:(q + 1) * 128],
                         rhs=Vc[:, z, t, :], start=False, stop=True, skip_group_check=True)
            probs.put(t, [m])
            return m

        def maxima(q):
            b = q % 2
            m = P.pe([nexts, nbanks.get(b)], nc.tensor.matmul, P.ps[:, 4 + b, :], lhsT=Qn[:, q * 128:(q + 1) * 128], rhs=Kn[:, z, :], start=True, stop=not wide)
            if wide:
                m = P.pe([], nc.tensor.matmul, P.ps[:, 4 + b, :], lhsT=Qa0[:, q * 128:(q + 1) * 128], rhs=Ka[:, z, :], start=False, stop=True)
            r = P.dve([m, reds.get(z)], nc.vector.tensor_reduce, red[:, z, q:q + 1], P.ps[:, 4 + b, :], AX, ALU.max)
            nbanks.put(b, [r])
            return m, r

        order = []
        if now is not None and nxt is not None:
            order = ["s0", "s1", "m0", "m1", "p0", "s2", "m2", "m3", "p1", "s3", "m4", "m5", "p2", "m6", "m7", "p3"]
        elif now is not None:
            order = ["s0", "s1", "p0", "s2", "p1", "s3", "p2", "p3"]
        else:
            order = [f"m{q}" for q in range(TOK_TILES)]
        for o in order:
            k = int(o[1])
            if o[0] == "s":
                scores(k)
            elif o[0] == "p":
                last = products(k)
            else:
                last, r = maxima(k)
        if nxt is not None:
            r = P.dve([r, reds.get(2)], nc.vector.tensor_tensor, mx[:], mx[:], red[:, z, :], ALU.max)
            reds.put(z, [r])
            reds.put(2, [r])
        slots.put(z, [last, P.pe.sig.now()])

    def run(now, nxt):
        make = lambda: [Ring(P, n, k) for n, k in (("banks", 2), ("probs", TPC), ("slots", 2), ("nbanks", 2), ("reds", 3))]
        P.meet()
        if now is not None:
            for b in range(acc0, acc0 + -(-TOK_TILES // per_bank)):
                P.pe([], nc.tensor.matmul, P.ps[:, b, 0:per_bank * dv], lhsT=C.zero[0:1, 0:128], rhs=C.zero[0:1, 0:per_bank * dv], start=True, stop=True, skip_group_check=True)
        if nxt is not None:
            P.dve([], nc.vector.memset, mx[:], -3.0e38)
        fetch(0, 0, now, nxt, [])
        P.meet_engines()
        with P.loop(CHUNKS // 2) as pair:
            rings = make()
            slots = rings[2]
            for z in range(2):
                fetch(pair * 2 + z + 1, 1 - z, now, nxt, slots.get(1 - z))
                if z == 0:
                    arrived = P.lags_of("keys0"), P.lags_of("vals0"), P.lags_of("next0")
                else:
                    arrived = kd[1].now(), vd[1].now(), kn[1].now() if X.softmax else None
                chunk(z, now, nxt, rings, arrived)
            for r in rings:
                r.close()
        P.meet_engines()
        if CHUNKS % 2:
            chunk(0, now, nxt, make(), (kd[0].now(), vd[0].now(), kn[0].now() if X.softmax else None))

    def take_off():
        P.meet()
        r = P.dve([], nc.vector.tensor_scalar, mneg[:], mx[:], -1.0, None, ALU.mult)
        if n_m == 1:
            for q in range(TOK_TILES):
                t = P.pe([r], nc.tensor.matmul, P.ps[aux:aux + 1, q // 4, (q % 4) * 128:(q % 4 + 1) * 128], lhsT=mneg[:, q:q + 1], rhs=C.ident[:], start=True, stop=True)
        else:
            a = P.dve([r], nc.vector.tensor_copy, mparts[:, 0, :], mneg[:])
            b = P.dve([a], nc.vector.tensor_tensor, mrest[:], mneg[:], mparts[:, 0, :], ALU.subtract)
            r = P.dve([b], nc.vector.tensor_copy, mparts[:, 1, :], mrest[:])
            base = 0 if wide else aux
            for q in range(TOK_TILES):
                t = P.pe([r], nc.tensor.matmul, P.ps[base:base + 2, q // 4, (q % 4) * 128:(q % 4 + 1) * 128], lhsT=mparts[:, :, q], rhs=C.ident16[:], start=True, stop=True)
        if wide:
            P.act([t], nc.scalar.copy, Qa[0:2, :], P.ps[0:2, 0:2, :].rearrange("p a n -> p (a n)"))
        else:
            P.act([t], nc.scalar.copy, Qc[aux:aux + n_m, :], P.ps[aux:aux + n_m, 0:2, :].rearrange("p a n -> p (a n)"))

    def next_queries(head):
        if X.split:
            return P.sp.dma([P.all_now()], q_in, Qn[0:rows, :], X.Q[bass.ds(head, 1)].rearrange("a r n -> (a r) n"))
        return P.sp.dma([P.all_now()], q_in, Qn[0:rows, :], X.Qb[bass.ds(head, 1)].rearrange("a r n -> (a r) n"))

    def these_queries(head):
        return P.sp.dma([P.all_now()], q_in, Qc[0:rows, :], X.Q[bass.ds(head, 1)].rearrange("a r n -> (a r) n"))

    den = tile(P, stack, "den8", [128, TOK_TILES])

    def store(head):
        P.meet()
        for b in range(-(-TOK_TILES // per_bank)):
            n = min(per_bank, TOK_TILES - b * per_bank)
            view = P.ps[:, acc0 + b, 0:n * dv].rearrange("p (j x) -> p j x", x=dv)
            if X.softmax:
                r = P.dve([], nc.vector.reciprocal, den[:, b * per_bank:b * per_bank + n], view[:, :, d])
                P.dve([r], nc.vector.tensor_tensor, O[:, b * per_bank:b * per_bank + n, bass.ds(head * d, d)], view[:, :, 0:d],
                      den[:, b * per_bank:b * per_bank + n].unsqueeze(2).to_broadcast([128, n, d]), ALU.mult)
            else:
                P.dve([], nc.vector.tensor_scalar, O[:, b * per_bank:b * per_bank + n, bass.ds(head * d, d)], view, 1.0, None, ALU.mult)

    if not X.softmax:
        with P.loop(H) as head:
            P.meet()
            these_queries(head)
            run(head, None)
            store(head)
        P.barrier()
        return
    next_queries(0)
    run(None, 0)
    these_queries(0)
    take_off()
    if H > 1:
        with P.loop(H - 1) as head:
            P.meet()
            next_queries(head + 1)
            run(head, head + 1)
            store(head)
            these_queries(head + 1)
            take_off()
    run(H - 1, None)
    store(H - 1)
    P.barrier()


def cross_layer(P, C, io, X, stack, name, heads, d, split, softmax, masked, w, bias, out):
    nc = P.nc
    A = Cross(P, name, heads, d, split, softmax, masked)
    bk = io[bias[1]] if bias else None
    keys_and_values(P, C, io, A, io[w[1]], bk, io[w[2]])
    with ExitStack() as inner:
        h, tmp = tile(P, inner, "h", [D, S]), tile(P, inner, "tmp", [D, S])
        C.normed = normalize(P, C, [], X, h, tmp)
        queries(P, C, io, A, h, io[w[0]], io[bias[0]] if bias else None, tmp)
    O = tile(P, stack, "O", [128, TOK_TILES, heads * d])
    with ExitStack() as inner:
        cross_heads(P, C, A, O, inner)
    F = heads * d
    OT = tile(P, stack, "OT", [128, F // 128, S])
    bv = load(P, stack, "bv", io[bias[2]]) if bias else None
    wo = load(P, stack, "wo", io[out[0]].rearrange("(k p) n -> p k n", p=128), [128, F // 128, D]) if out else None
    bo = load(P, stack, "bo", io[out[1]]) if out and out[1] else None
    wts = P.stream("weights").now()
    done = []
    for f in range(F // 128):
        t = transpose_back(P, C, [wts], O[:, :, f * 128:(f + 1) * 128], OT[:, f, :], 128)
        if bv is not None:
            t = [P.dve([t], nc.vector.tensor_scalar, OT[:, f, :], OT[:, f, :], bv[:, f:f + 1], None, ALU.add)]
        done.append(t)
    if out:
        linear(P, [done], lambda k, m: wo[:, k, :], [OT[:, k, :] for k in range(F // 128)], 1, add_to_x(P, X, bo[:, 0:1] if bo is not None else None))
    else:
        P.dve([done], nc.vector.tensor_tensor, X[:], X[:], OT[:, 0, :], ALU.add)


def cross_0(P, C, io, X, stack):
    cross_layer(P, C, io, X, stack, "L0", 16, 64, False, True, (io["mask_BxS2_bf1"], MASKED), ("L0_xattn_Wq", "L0_xattn_Wk", "L0_xattn_Wv"),
                ("L0_xattn_bq", "L0_xattn_bk", "L0_xattn_bv"), ("L0_xattn_Wo", "L0_xattn_bo"))


def cross_1(P, C, io, X, stack):
    cross_layer(P, C, io, X, stack, "L1", 1, 128, False, True, (None, MASKED), ("L1_xattn_Wq", "L1_xattn_Wk", "L1_xattn_Wv"), None, None)


def cross_2(P, C, io, X, stack):
    cross_layer(P, C, io, X, stack, "L2", 16, 8, True, False, None, ("L2_xattn_Wq", "L2_xattn_Wk", "L2_xattn_Wv"), None, ("L2_xattn_Wo", None))


def cross_3(P, C, io, X, stack):
    cross_layer(P, C, io, X, stack, "L3", 16, 8, True, True, (io["mask_Bx1x1xS2_ik0"], -1e9), ("L3_xattn_Wq", "L3_xattn_Wk", "L3_xattn_Wv"),
                ("L3_xattn_bq", "L3_xattn_bk", "L3_xattn_bv"), ("L3_xattn_Wo", "L3_xattn_bo"))


def build(nc, io, counts, layers):
    global CHUNKS, N_KEYS
    N_KEYS = io["ones_keys"].shape[0]
    CHUNKS = io["ctx_1024"].shape[1] // CHUNK
    with ExitStack() as ctx:
        P = Prog(nc, ctx, counts)

        class C:
            pass
        C.mean = tile(P, ctx, "mean", [128, 128])
        C.eps = tile(P, ctx, "eps", [128, 1])
        C.one_eps = tile(P, ctx, "one_eps", [128, 1])
        C.ident = tile(P, ctx, "ident", [128, 128])
        C.zero = tile(P, ctx, "zero", [128, HALF])
        C.ones, C.ones_col = tile(P, ctx, "ones", [1, 128]), tile(P, ctx, "ones_col", [128, 1])
        C.ones16, C.ident16 = tile(P, ctx, "ones16", [128, 16]), tile(P, ctx, "ident16", [128, 128], BF16)
        P.dve([], nc.vector.memset, C.ones16[:], 1.0)
        P.io_ones = io["ones_keys"]
        C.causal, C.below = tile(P, ctx, "causal", [128, 128]), tile(P, ctx, "below", [128, 128])
        X = tile(P, ctx, "X", [D, S])
        P.sp.dma(None, P.stream("x"), X[:], io["x"])
        P.dve([], nc.vector.memset, C.mean[:], 1.0 / D)
        P.dve([], nc.vector.memset, C.eps[:], LN_EPS)
        P.dve([], nc.vector.memset, C.one_eps[:], 1.0 + 1e-6)
        P.dve([], nc.vector.memset, C.zero[:], 0.0)
        z = P.pool([], nc.gpsimd.memset, C.ident[:], 0.0)
        P.pool([z], nc.gpsimd.affine_select, out=C.ident[:], in_=C.ident[:], compare_op=ALU.not_equal, fill=1.0,
               base=0, pattern=[[-1, 128]], channel_multiplier=1)
        P.dve([], nc.vector.memset, C.ones[:], 1.0)
        P.dve([], nc.vector.memset, C.ones_col[:], 1.0)
        z = P.pool([], nc.gpsimd.memset, C.causal[:], 1.0)
        P.pool([z], nc.gpsimd.affine_select, out=C.causal[:], in_=C.causal[:], compare_op=ALU.is_ge, fill=0.0,
               base=0, pattern=[[1, 128]], channel_multiplier=-1)
        z = P.pool([], nc.gpsimd.memset, C.below[:], 0.0)
        P.pool([z], nc.gpsimd.affine_select, out=C.below[:], in_=C.below[:], compare_op=ALU.is_ge, fill=MASKED,
               base=0, pattern=[[-1, 128]], channel_multiplier=1)
        P.barrier()
        P.dve([], nc.vector.tensor_copy, C.ident16[:], C.ident[:])
        P.barrier()
        for n in layers:
            with ExitStack() as stack:
                PARTS[n](P, C, io, X, stack)
                P.barrier()
        P.sp.dma(None, P.stream("out"), io["out"], X[:])
        P.barrier()


PARTS = {2: ffn_ternary_gated, 5: ffn_ternary_gelu, 6: recurrent_block, 11: ffn_experts,
         0: causal_attention, 1: cross_0, 4: cross_1, 7: cross_2, 10: cross_3, 3: cosformer, 8: attention_of_experts, 9: retention}



TRANSPOSED = {"L0_ffn_w1_w", "L0_ffn_w2_w", "L0_ffn_h1_w", "L0_ffn_h2_w", "L0_ffn_w3_w", "L1_ffn_W1", "L1_ffn_W2",
              "L2_attn_W_in", "L2_attn_W_gate", "L2_attn_W_out", "L2_attn_rg_in_w", "L2_attn_rg_gate_w",
              "L2_attn_mlp_gate_w", "L2_attn_mlp_up_w", "L2_attn_mlp_down_w",
              "L0_attn_W_Q", "L0_attn_W_K", "L0_attn_W_V", "L0_attn_W_O",
              "L2_xattn_Wq", "L2_xattn_Wk", "L2_xattn_Wv", "L2_xattn_Wo",
              "L3_xattn_Wq", "L3_xattn_Wk", "L3_xattn_Wv", "L3_xattn_Wo"}


def kernel(**inputs):
    import concourse.bacc as bacc
    from concourse.bass_utils import run_bass_kernel_spmd

    arrays = {}
    for name, a in inputs.items():
        a = np.asarray(a)
        if name in TRANSPOSED:
            a = a.T
        if name == "x":
            a = a[0].T
        if name == "ctx_1024":
            n_keys = a.shape[1]
            padded = -(-n_keys // CHUNK) * CHUNK
            a = np.pad(a[0], ((0, padded - n_keys), (0, 0))).T
        if name.startswith("mask"):
            a = a.reshape(-1)
        if a.ndim == 1 and not name.startswith("mask"):
            a = a.reshape(-1, 96 if a.size == 192 else min(128, a.size)).T
        if a.dtype == np.bool_:
            a = a.view(np.uint8)
        arrays[name] = np.ascontiguousarray(a)
    arrays.update(layout(inputs))
    arrays["ones_keys"] = np.ones(n_keys, np.int32)
    valid = (np.arange(padded) < n_keys).astype(np.float32)
    arrays["valid_keys"] = np.ascontiguousarray(valid.reshape(-1, 128).T)

    def program(counts):
        nc = bacc.Bacc("TRN2", target_bir_lowering=False, num_devices=1)
        io = {n: nc.dram_tensor(n + "_dram", a.shape, mybir.dt.from_np(a.dtype), kind="ExternalInput").ap()
              for n, a in arrays.items()}
        io["out"] = nc.dram_tensor("out_dram", (D, S), F32, kind="ExternalOutput").ap()
        build(nc, io, counts, LAYERS)
        return nc

    counts = {}
    program(counts)
    nc = program(counts)
    r = run_bass_kernel_spmd(nc, [{n + "_dram": a for n, a in arrays.items()}], core_ids=[0])
    return np.ascontiguousarray(r.results[0]["out_dram"].T)[None]


def exchanged(a):
    return a.reshape(a.shape[0], -1, 2)[:, :, ::-1].reshape(a.shape)


def block_diagonal(w):
    h, d, _ = w.shape
    out = np.zeros((h * d, h * d), w.dtype)
    for n in range(h):
        out[n * d:(n + 1) * d, n * d:(n + 1) * d] = w[n]
    return out


def tables():
    pos = np.arange(S, dtype=np.float64)
    out = {}

    def table(d, cos, sin, factor):
        c = np.repeat(cos, 2, axis=1).T
        s = np.stack([-sin, sin], axis=2).reshape(S, d).T
        n = D // d
        return [np.ascontiguousarray((np.tile(t, (n, 1)) * factor).astype(np.float32)) for t in (c, s)]

    d = D // 16
    inv = 10000.0 ** (-2.0 * np.arange(d // 2) / d)
    ang = (np.float32(1) * pos[:, None].astype(np.float32) * inv.astype(np.float32)).astype(np.float64)
    out["rope_q_cos"], out["rope_q_sin"] = table(d, np.cos(ang), np.sin(ang), 1.0 / math.sqrt(d))
    out["rope_k_cos"], out["rope_k_sin"] = table(d, np.cos(ang), np.sin(ang), 1.0)

    H, d = 8, 16
    gamma = (1.0 - np.exp(np.linspace(math.log(1.0 / 32.0), math.log(1.0 / 512.0), H))).astype(np.float32).astype(np.float64)
    scale = (np.arange(0, d, 2) + 0.4 * d) / (1.4 * d)
    sc = scale[None, :] ** (pos / 512.0)[:, None]
    inv = (1.0 / 10000.0 ** (np.arange(d // 2) / (d // 2))).astype(np.float32)
    ang = (pos[:, None].astype(np.float32) * inv).astype(np.float64)
    decay = np.repeat(gamma[:, None] ** pos[None, :], d, axis=0)
    out["retention_q_cos"], out["retention_q_sin"] = table(d, np.cos(ang) * sc, np.sin(ang) * sc, decay)
    out["retention_k_cos"], out["retention_k_sin"] = table(d, np.cos(ang) / sc, np.sin(ang) / sc, 1.0 / decay)

    ang = (np.float32(math.pi / (2.0 * S)) * pos.astype(np.float32)).astype(np.float64)
    out["cosformer_table"] = np.repeat(np.stack([np.cos(ang), np.sin(ang)]), 64, axis=0).astype(np.float32)
    return out


def layout(inputs):
    out = tables()
    get = lambda n: np.asarray(inputs[n])
    for x in ("Q", "K"):
        out[f"L0_attn_W_{x}_turned"] = exchanged(get(f"L0_attn_W_{x}").T)
        out[f"L3_attn_W_{x}"] = block_diagonal(get(f"L3_attn_W_{x}"))
        out[f"L3_attn_W_{x}_turned"] = exchanged(out[f"L3_attn_W_{x}"])
    out["L3_attn_W_V"] = block_diagonal(get("L3_attn_W_V"))
    heads = lambda n: np.tile(get(n).reshape(16, 64).T, (2, 1))
    out["L1_attn_bqk_twice"] = np.stack([heads("L1_attn_bq"), heads("L1_attn_bk")], axis=2).transpose(1, 0, 2)
    for n in ("L1_attn_bv", "L0_xattn_bv", "L3_xattn_bv", "L2_ffn_gates"):
        out[n + "_row"] = get(n)[None]
    out["L1_xattn_Wk"], out["L1_xattn_Wv"] = np.split(get("L1_xattn_Wkv"), 2, axis=1)
    return {n: np.ascontiguousarray(a) for n, a in out.items()}
```

```python
from contextlib import ExitStack, contextmanager
import math

import numpy as np

import concourse.bass as bass
from concourse import mybir

F32 = mybir.dt.float32
BF16 = mybir.dt.bfloat16
I32 = mybir.dt.int32
U32 = mybir.dt.uint32
U8 = mybir.dt.uint8
ALU = mybir.AluOpType
ACT = mybir.ActivationFunctionType
AX = mybir.AxisListType.X

D = 128
S = 1024
HALF = 512
TOK_TILES = S // 128
CHUNK = 512
TPC = CHUNK // 128
LN_EPS = 1e-5
MASKED = -1e15
START = 512
LAYERS = list(range(12))
UNROLL = 4


class Signal:

    def __init__(self, prog, name):
        self.prog, self.sem, self.n = prog, prog.ctx.enter_context(prog.nc.semaphore(name)), 0
        prog.counted.append(self)

    def now(self):
        return Mark(self, self.n, list(self.prog.frames))

    def count(self, instruction, by=1):
        instruction.then_inc(self.sem, by)
        self.n += by
        return self.now()


class Mark:

    def __init__(self, sig, n, frames):
        self.sig, self.n, self.frames = sig, n, frames

    def key(self):
        return len(self.frames), self.n

    def value(self, engine):
        loops = [f for f in self.frames if f.per.get(self.sig, 0)]
        if not loops:
            return self.n
        here = engine.prog.frames[-1]
        key = (engine, self.sig, len(loops))
        if key not in here.added:
            added = 0
            for f in loops:
                added = f.reg * f.per[self.sig] + added
            here.added[key] = engine.e.snap(added)
        return here.added[key] + self.n


class Ring:

    def __init__(self, prog, label, n):
        self.prog, self.label, self.n, self.marks = prog, label, n, {}

    def get(self, slot):
        if slot in self.marks:
            return self.marks[slot]
        if not self.prog.frames:
            return []
        return self.prog.lags(f"{self.label}{slot}")

    def put(self, slot, marks):
        self.marks[slot] = marks

    def enter(self):
        self.outside, self.marks = self.marks, {}

    def leave(self):
        inside = {slot: self.prog.lasts(f"{self.label}{slot}") for slot in range(self.n)}
        self.marks = {**self.outside, **{slot: marks for slot, marks in inside.items() if marks}}

    def close(self):
        for slot, marks in self.marks.items():
            for k, m in enumerate(marks):
                self.prog.name(f"{self.label}{slot}.{k}", m)


class Frame:

    def __init__(self, reg, per, base):
        self.reg, self.per, self.base, self.names, self.added = reg, per, base, {}, {}


class Engine:
    def __init__(self, prog, e, name):
        self.prog, self.e, self.sig, self.waited = prog, e, Signal(prog, name), {}

    def wait(self, *marks):
        need = {}

        def gather(m):
            if isinstance(m, Mark):
                have = need.get(m.sig)
                if have is None or m.key() > have.key():
                    need[m.sig] = m
            elif m is not None:
                for x in m:
                    gather(x)
        gather(marks)
        for sig, m in need.items():
            if (m.n <= START and not m.frames) or self.waited.get(sig, (0, 0)) >= m.key():
                continue
            self.waited[sig] = m.key()
            v = m.value(self)
            assert m.n >= 0
            self.e.wait_ge(sig.sem, v)
            if self is self.prog.sp and not isinstance(v, int):
                self.prog.settle(self)

    def __call__(self, marks, op, *a, **k):
        self.wait(marks)
        return self.sig.count(op(*a, **k))

    def quiet(self, marks, op, *a, **k):
        self.wait(marks)
        op(*a, **k)

    def dma(self, marks, sig, out, in_):
        self.wait(marks)
        return sig.count(self.e.dma_start(out, in_), 16)


class Prog:
    def __init__(self, nc, ctx, counts):
        self.nc, self.ctx, self.counts, self.seen = nc, ctx, counts, []
        self.frames, self.counted, self.tiles = [], [], 0
        self.pe = Engine(self, nc.tensor, "pe_done")
        self.act = Engine(self, nc.scalar, "act_done")
        self.dve = Engine(self, nc.vector, "dve_done")
        self.pool = Engine(self, nc.gpsimd, "pool_done")
        self.sp = Engine(self, nc.sync, "sp_done")
        self.engines = (self.pe, self.act, self.dve, self.pool, self.sp)
        self.ps = ctx.enter_context(nc.psum_tensor("ps", [128, 8, HALF], F32))
        self.free = [None] * 8
        self.turn = 0
        self.banks = list(range(8))
        self.loads = {}
        for e in self.engines:
            e.e.sem_inc(e.sig.sem, START)
            e.sig.n = START
        self.barrier()

    def stream(self, name):
        if name not in self.loads:
            assert not self.frames
            sig = self.loads[name] = Signal(self, name)
            self.sp.e.sem_inc(sig.sem, START)
            sig.n = START
        return self.loads[name]

    def barrier(self):
        for e in self.engines:
            if e is not self.sp:
                e.wait(e.sig.now())
        for sig in self.loads.values():
            self.sp.wait(sig.now())
        self.nc.all_engine_barrier()
        for e in self.engines:
            for sig in self.counted:
                e.waited[sig] = (len(self.frames), sig.n)
        self.free = [None] * 8

    def settle(self, e):
        e.e.sem_inc(e.sig.sem, 1)
        e.sig.n += 1

    def meet(self):
        marks = self.all_now()
        for e in self.engines:
            e.wait(marks)
            if e is not self.sp:
                self.settle(e)

    def meet_engines(self):
        marks = [e.sig.now() for e in self.engines]
        for e in self.engines:
            e.wait(marks)
            if e is not self.sp:
                self.settle(e)

    def all_now(self):
        return [s.now() for s in self.counted]

    def name_if(self, label, mark):
        if self.frames:
            self.name(label, mark)

    def lags_of(self, label):
        return [self.lag(label)] if label in self.frames[-1].known else []

    @contextmanager
    def loop(self, count):
        key = len(self.seen)
        self.seen.append(None)
        known = self.counts.get(key)
        with self.nc.Fori(0, count) as reg:
            per = {s: known[0][n] for n, s in enumerate(self.counted)} if known else {}
            f = Frame(reg, per, {s: s.n for s in self.counted})
            f.known = known[1] if known else {}
            self.frames.append(f)
            for e in self.engines:
                e.waited = {}
            yield reg
            self.frames.pop()
            grown = [s.n - f.base.get(s, 0) for s in self.counted]
        self.counts[key] = (grown, f.names)
        self.ended = f, grown, count
        for s, g in zip(self.counted, grown):
            s.n = f.base.get(s, 0) + g * count
        for e in self.engines:
            e.waited = {}

    def name(self, label, mark):
        f = self.frames[-1]
        f.names[label] = (self.counted.index(mark.sig), mark.n - f.base.get(mark.sig, 0))
        return mark

    def lag(self, label):
        f = self.frames[-1]
        index, off = f.known.get(label, (0, 0))
        sig = self.counted[index]
        per = f.per.get(sig, 0)
        return Mark(sig, f.base.get(sig, 0) + off - per, list(self.frames))

    def lags(self, label):
        names = [n for n in self.frames[-1].known if n.rsplit(".", 1)[0] == label]
        return [self.lag(n) for n in names]

    def lasts(self, label):
        f, grown, count = self.ended
        marks = []
        for n, (index, off) in f.names.items():
            if n.rsplit(".", 1)[0] == label:
                sig = self.counted[index]
                marks.append(Mark(sig, f.base.get(sig, 0) + off + grown[index] * (count - 1), list(self.frames)))
        return marks

    def bank(self):
        b = self.banks[self.turn % len(self.banks)]
        self.turn += 1
        self.pe.wait(self.free[b])
        return b



def halves():
    return [slice(h * HALF, (h + 1) * HALF) for h in range(S // HALF)]


def load(P, stack, name, src, shape=None, dt=F32, dst=None):
    shape = list(shape or src.shape)
    t = tile(P, stack, name, shape, dt)
    P.sp.dma(None, P.stream("weights"), t[:] if dst is None else dst(t), src)
    return t


def tile(P, stack, name, shape, dt=F32):
    P.tiles += 1
    return stack.enter_context(P.nc.sbuf_tensor(f"{name}_{P.tiles}", list(shape), dt))


def linear(P, marks, weights, inputs, n_out, evacuate, width=None):
    out = []
    cols = [slice(0, width)] if width else halves()
    for m in range(n_out):
        for h, sl in enumerate(cols):
            b = P.bank()
            n = len(inputs)
            for k in range(n):
                w = weights(k, m)
                ps = P.ps[0:w.shape[-1], b, 0:sl.stop - sl.start]
                mark = P.pe(marks, P.nc.tensor.matmul, ps, lhsT=w, rhs=inputs[k][:, sl], start=k == 0, stop=k == n - 1)
            P.free[b] = evacuate(m, sl, ps, mark)
            out.append(P.free[b])
    return out


def normalize(P, C, marks, src, dst, tmp, center=True, weight=None):
    nc = P.nc
    done = []
    for sl in halves():
        base = src
        m = marks
        if center:
            b = P.bank()
            t = P.pe(marks, nc.tensor.matmul, P.ps[:, b, :], lhsT=C.mean[:], rhs=src[:, sl], start=True, stop=True)
            m = P.dve([t, marks], nc.vector.tensor_tensor, dst[:, sl], src[:, sl], P.ps[:, b, :], ALU.subtract)
            P.free[b] = m
            base = dst
        q = P.act([m, marks], nc.scalar.activation, tmp[:, sl], base[:, sl], ACT.Square)
        b = P.bank()
        t = P.pe([q], nc.tensor.matmul, P.ps[:, b, :], lhsT=C.mean[:], rhs=tmp[:, sl], start=True, stop=True)
        r = P.act([t], nc.scalar.activation, tmp[:, sl], P.ps[:, b, :], ACT.Sqrt, bias=C.eps[:, 0:1])
        P.free[b] = r
        r = P.dve([r], nc.vector.reciprocal, tmp[:, sl], tmp[:, sl])
        if weight is None:
            r = P.dve([r], nc.vector.tensor_tensor, dst[:, sl], base[:, sl], tmp[:, sl], ALU.mult)
        else:
            r = P.dve([r], nc.vector.scalar_tensor_tensor, dst[:, sl], base[:, sl], weight, tmp[:, sl], ALU.mult, ALU.mult)
        done.append(r)
    return done


def add_to_x(P, X, bias=None):
    def evacuate(m, sl, ps, mark):
        if bias is None:
            return P.dve([mark], P.nc.vector.tensor_tensor, X[:, sl], X[:, sl], ps, ALU.add)
        return P.dve([mark], P.nc.vector.scalar_tensor_tensor, X[:, sl], ps, bias, X[:, sl], ALU.add, ALU.add)
    return evacuate


def ffn_ternary_gated(P, C, io, X, stack):
    nc = P.nc
    F = io["L0_ffn_w1_w"].shape[1]
    T = F // 128
    w1, w2 = (load(P, stack, n, io[n]) for n in ("L0_ffn_w1_w", "L0_ffn_w2_w"))
    h1, h2 = (load(P, stack, n, io[n].rearrange("(k p) n -> p k n", p=128), [128, T, F])
              for n in ("L0_ffn_h1_w", "L0_ffn_h2_w"))
    w3 = load(P, stack, "w3", io["L0_ffn_w3_w"].rearrange("(k p) n -> p k n", p=128), [128, T, D])
    s1, s2, t1, t2 = (load(P, stack, n, io[n])
                      for n in ("L0_ffn_w1_s", "L0_ffn_w2_s", "L0_ffn_h1_s", "L0_ffn_h2_s"))
    s3 = load(P, stack, "s3", io["L0_ffn_w3_s"])
    wts = P.stream("weights").now()
    h, tmp = tile(P, stack, "h", [D, S]), tile(P, stack, "tmp", [D, S])
    a, b = tile(P, stack, "a", [128, T, S]), tile(P, stack, "b", [128, T, S])
    n = normalize(P, C, [], X, h, tmp)
    gates = linear(P, [n, wts], lambda k, m: w1[:, m * 128:(m + 1) * 128], [h], T, lambda m, sl, ps, t: P.act(
        [t], nc.scalar.activation, a[:, m, sl], ps, ACT.Silu, scale=s1[:, m:m + 1]))
    up = linear(P, [], lambda k, m: w2[:, m * 128:(m + 1) * 128], [h], T, lambda m, sl, ps, t: P.dve(
        [t, gates], nc.vector.scalar_tensor_tensor, a[:, m, sl], ps, s2[:, m:m + 1], a[:, m, sl], ALU.mult, ALU.mult))
    one = linear(P, [up], lambda k, m: h1[:, k, m * 128:(m + 1) * 128], [a[:, k, :] for k in range(T)], T,
                 lambda m, sl, ps, t: P.act([t], nc.scalar.activation, b[:, m, sl], ps, ACT.Gelu, scale=t1[:, m:m + 1]))
    two = linear(P, [one], lambda k, m: h2[:, k, m * 128:(m + 1) * 128], [b[:, k, :] for k in range(T)], T,
                 lambda m, sl, ps, t: P.act([t], nc.scalar.activation, a[:, m, sl], ps, ACT.Gelu, scale=t2[:, m:m + 1]))
    linear(P, [two], lambda k, m: w3[:, k, :], [a[:, k, :] for k in range(T)], 1, lambda m, sl, ps, t: P.dve(
        [t], nc.vector.scalar_tensor_tensor, X[:, sl], ps, s3[:, 0:1], X[:, sl], ALU.mult, ALU.add))


def ternary(P, C, marks, w, work, stack, name):
    nc = P.nc
    n = w.shape[-1]
    s = tile(P, stack, name, [128, 4])
    r = P.dve([marks], nc.vector.tensor_reduce, s[:, 0:1], w, AX, ALU.add, apply_absolute_value=True)
    b = P.bank()
    t = P.pe([r], nc.tensor.matmul, P.ps[:, b, 0:1], lhsT=C.mean[:], rhs=s[:, 0:1], start=True, stop=True)
    r = P.dve([t], nc.vector.tensor_scalar, s[:, 1:2], P.ps[:, b, 0:1], 1.0 / n, 1e-8, ALU.mult, ALU.max)
    P.free[b] = r
    r1 = P.dve([r], nc.vector.tensor_scalar, s[:, 2:3], s[:, 1:2], 0.5, None, ALU.mult)
    r2 = P.dve([r], nc.vector.tensor_scalar, s[:, 3:4], s[:, 1:2], -0.5, None, ALU.mult)
    r = P.dve([r1, r2], nc.vector.tensor_scalar, work, w, s[:, 3:4], None, ALU.is_lt)
    r = P.dve([r], nc.vector.scalar_tensor_tensor, work, w, s[:, 2:3], work, ALU.is_gt, ALU.subtract)
    r = P.dve([r], nc.vector.tensor_tensor, work, work, w, ALU.subtract)
    return P.dve([r], nc.vector.tensor_tensor, w, w, work, ALU.add)


def ffn_ternary_gelu(P, C, io, X, stack):
    nc = P.nc
    F = io["L1_ffn_W1"].shape[1]
    T = F // 128
    w1 = load(P, stack, "w1", io["L1_ffn_W1"])
    w2 = load(P, stack, "w2", io["L1_ffn_W2"].rearrange("(k p) n -> p k n", p=128), [128, T, D])
    b1 = load(P, stack, "b1", io["L1_ffn_b1"])
    b2 = load(P, stack, "b2", io["L1_ffn_b2"])
    wts = P.stream("weights").now()
    h, tmp = tile(P, stack, "h", [D, S]), tile(P, stack, "tmp", [D, S])
    work, a = tile(P, stack, "work", [128, F]), tile(P, stack, "a", [128, T, S])
    flat2 = w2[:].rearrange("p k n -> p (k n)")
    m1 = ternary(P, C, [wts], w1[:], work[:], stack, "scale1")
    m2 = ternary(P, C, [wts, m1], flat2, work[:], stack, "scale2")
    n = normalize(P, C, [], X, h, tmp)
    hid = linear(P, [n, m1], lambda k, m: w1[:, m * 128:(m + 1) * 128], [h], T, lambda m, sl, ps, t: P.act(
        [t], nc.scalar.activation, a[:, m, sl], ps, ACT.Gelu, bias=b1[:, m:m + 1]))
    linear(P, [hid, m2], lambda k, m: w2[:, k, :], [a[:, k, :] for k in range(T)], 1, add_to_x(P, X, b2[:, 0:1]))


def recurrent_block(P, C, io, X, stack):
    nc = P.nc
    HID = io["L2_attn_W_in"].shape[1]
    R, T = HID // 2, 2
    K = io["L2_attn_conv_w"].shape[-1]
    col = lambda n: load(P, stack, n, io[n])
    w_in, w_gate, m_gate, m_up = (load(P, stack, n, io["L2_attn_" + n]) for n in ("W_in", "W_gate", "mlp_gate_w", "mlp_up_w"))
    rg_in, rg_gate, w_out, m_down = (load(P, stack, n, io["L2_attn_" + n].rearrange("(t p) n -> p t n", p=R),
                                          [R, T, io["L2_attn_" + n].shape[1]]) for n in ("rg_in_w", "rg_gate_w", "W_out", "mlp_down_w"))
    conv_w = load(P, stack, "conv_w", io["L2_attn_conv_w"].rearrange("(t p) a k -> p t (a k)", p=R), [R, T, K])
    conv_b, in_b, gate_b, lam = (col("L2_attn_" + n) for n in ("conv_b", "rg_in_b", "rg_gate_b", "forget_lambda"))
    n1, n2 = (load(P, stack, n, io["L2_attn_" + n]) for n in ("norm1_w", "norm2_w"))
    wts = P.stream("weights").now()
    x, h, tmp = (tile(P, stack, n, [D, S]) for n in ("x", "h", "tmp"))
    u_pad = tile(P, stack, "u_pad", [R, T, K - 1 + S])
    gate, u, ig, rg, t1 = (tile(P, stack, n, [R, T, S]) for n in ("gate", "u", "ig", "rg", "t1"))
    c = tile(P, stack, "c", [R, 2, T])
    r = P.act([wts], nc.scalar.activation, c[:, 0, :], lam[:], ACT.Abs)
    r = P.act([r], nc.scalar.activation, c[:, 0, :], c[:, 0, :], ACT.Exp, scale=-1.0)
    r = P.act([r], nc.scalar.activation, c[:, 0, :], c[:, 0, :], ACT.Ln, bias=1.0)
    r = P.dve([r, wts], nc.vector.scalar_tensor_tensor, c[:, 1, :], lam[:], 0.0, c[:, 0, :], ALU.max, ALU.add)
    decay = P.dve([r], nc.vector.tensor_scalar, c[:, 1, :], c[:, 1, :], -8.0, None, ALU.mult)
    zero = P.dve([], nc.vector.memset, u_pad[:, :, 0:K - 1], 0.0)

    n = normalize(P, C, [], X, x, tmp)
    n = normalize(P, C, [n, wts], x, h, tmp, center=False, weight=n1[:, 0:1])
    tiles = lambda w: (lambda k, m: w[:, m * R:(m + 1) * R])
    deep = lambda w: (lambda k, m: w[:, k, m * R:(m + 1) * R])
    gates = linear(P, [n], tiles(w_gate), [h], T, lambda m, sl, ps, t: P.act([t], nc.scalar.activation, gate[:, m, sl], ps, ACT.Gelu))
    us = linear(P, [n], tiles(w_in), [h], T, lambda m, sl, ps, t: P.act(
        [t], nc.scalar.copy, u_pad[:, m, K - 1 + sl.start:K - 1 + sl.stop], ps))
    conv = []
    for m in range(T):
        r = P.dve([us, zero], nc.vector.tensor_scalar, u[:, m, :], u_pad[:, m, 0:S], conv_w[:, m, 0:1], conv_b[:, m:m + 1], ALU.mult, ALU.add)
        for k in range(1, K):
            r = P.dve([r], nc.vector.scalar_tensor_tensor, u[:, m, :], u_pad[:, m, k:k + S], conv_w[:, m, k:k + 1], u[:, m, :], ALU.mult, ALU.add)
        conv.append(r)
    us = [u[:, k, :] for k in range(T)]
    igs = linear(P, [conv], deep(rg_in), us, T, lambda m, sl, ps, t: P.act([t], nc.scalar.activation, ig[:, m, sl], ps, ACT.Sigmoid, bias=in_b[:, m:m + 1]))
    rgs = linear(P, [conv], deep(rg_gate), us, T, lambda m, sl, ps, t: P.act([t], nc.scalar.activation, rg[:, m, sl], ps, ACT.Sigmoid, bias=gate_b[:, m:m + 1]))
    recs = []
    for m in range(T):
        a = P.act([rgs, decay], nc.scalar.activation, rg[:, m, :], rg[:, m, :], ACT.Exp, scale=c[:, 1, m:m + 1])
        b = P.act([a], nc.scalar.activation, t1[:, m, :], rg[:, m, :], ACT.Square)
        b = P.act([b], nc.scalar.activation, t1[:, m, :], t1[:, m, :], ACT.Sqrt, scale=-1.0, bias=C.one_eps[0:R, 0:1])
        b = P.dve([b, igs], nc.vector.tensor_tensor, t1[:, m, :], t1[:, m, :], ig[:, m, :], ALU.mult)
        b = P.dve([b], nc.vector.tensor_tensor, t1[:, m, :], t1[:, m, :], u[:, m, :], ALU.mult)
        b = P.dve([a, b], nc.vector.tensor_tensor_scan, ig[:, m, :], rg[:, m, :], t1[:, m, :], 0.0, ALU.mult, ALU.add)
        recs.append(P.dve([b, gates], nc.vector.tensor_tensor, ig[:, m, :], ig[:, m, :], gate[:, m, :], ALU.mult))
    mix = linear(P, [recs], lambda k, m: w_out[:, k, :], [ig[:, k, :] for k in range(T)], 1, add_to_x(P, x))
    n = normalize(P, C, [mix], x, h, tmp, center=False, weight=n2[:, 0:1])
    gs = linear(P, [n], tiles(m_gate), [h], T, lambda m, sl, ps, t: P.act([t], nc.scalar.activation, gate[:, m, sl], ps, ACT.Gelu))
    gs = linear(P, [n], tiles(m_up), [h], T, lambda m, sl, ps, t: P.dve([t, gs], nc.vector.tensor_tensor, gate[:, m, sl], ps, gate[:, m, sl], ALU.mult))
    outs = linear(P, [gs], lambda k, m: m_down[:, k, :], [gate[:, k, :] for k in range(T)], 1, add_to_x(P, x))
    for sl in halves():
        P.dve([outs], nc.vector.tensor_tensor, X[:, sl], X[:, sl], x[:, sl], ALU.add)


def transpose_back(P, C, marks, src, dst, parts):
    nc = P.nc
    out = []
    for h, sl in enumerate(halves()):
        b = P.bank()
        for j in range(4):
            t = P.pe(marks, nc.tensor.transpose, P.ps[0:parts, b, j * 128:(j + 1) * 128], src[:, 4 * h + j, :], C.ident[:])
        P.free[b] = P.act([t], nc.scalar.copy, dst[:, sl], P.ps[0:parts, b, :])
        out.append(P.free[b])
    return out


def one_hot_rows(P, C, marks, rows, n, sel):
    z = P.pool(marks, P.nc.gpsimd.memset, sel[:], 0.0)
    return P.pool([z], P.nc.gpsimd.affine_select, out=sel[:], in_=sel[:], compare_op=ALU.not_equal, fill=1.0, base=0,
                  pattern=[[-1, n], [0, 128]], channel_multiplier=1)


def ffn_experts(P, C, io, X, stack):
    nc = P.nc
    E, F = io["L3_ffn_experts_w1"].shape[0], io["L3_ffn_experts_w1"].shape[2]
    T = F // 128
    gate = load(P, stack, "gate", io["L3_ffn_gate"])
    w1, w3 = (tile(P, stack, n, [128, 2, F]) for n in ("w1", "w3"))
    w2 = tile(P, stack, "w2", [128, 2, T, D])
    wts = P.stream("weights").now()
    h, tmp, acc = (tile(P, stack, n, [D, S]) for n in ("h", "tmp", "acc"))
    a = tile(P, stack, "a", [128, T, S])
    logits, w, hot = (tile(P, stack, n, [128, TOK_TILES, E]) for n in ("logits", "w", "hot"))
    top, both = tile(P, stack, "top", [128, TOK_TILES, 8]), tile(P, stack, "both", [128, TOK_TILES, 2])
    which, whichf = tile(P, stack, "which", [128, TOK_TILES, 8], U32), tile(P, stack, "whichf", [128, TOK_TILES, 8])
    number = tile(P, stack, "number", [128, E])
    wT, wB = tile(P, stack, "wT", [E, S]), tile(P, stack, "wB", [128, E, S])
    sel = tile(P, stack, "sel", [E, E, 128])
    sels = one_hot_rows(P, C, [], None, E, sel)
    iot = P.pool([], nc.gpsimd.iota, number[:], [[1, E]], 0, 0, allow_small_or_imprecise_dtypes=True)
    loads = [P.stream("expert0"), P.stream("expert1")]

    def fetch(e, marks):
        for t, n in ((w1, "w1"), (w3, "w3")):
            P.sp.dma(marks, loads[e % 2], t[:, e % 2, :], io["L3_ffn_experts_" + n][e])
        return P.sp.dma(marks, loads[e % 2], w2[:, e % 2], io["L3_ffn_experts_w2"][e].rearrange("(k p) n -> p k n", p=128))

    here = [fetch(0, []), fetch(1, [])]
    n = normalize(P, C, [], X, h, tmp)
    b = P.bank()
    for j in range(TOK_TILES):
        t = P.pe([n, wts], nc.tensor.matmul, P.ps[:, b, j * E:(j + 1) * E], lhsT=h[:, j * 128:(j + 1) * 128], rhs=gate[:], start=True, stop=True)
    r = P.dve([t], nc.vector.tensor_copy, logits[:], P.ps[:, b, 0:TOK_TILES * E].rearrange("p (j e) -> p j e", e=E))
    P.free[b] = r
    for j in range(TOK_TILES):
        m = P.dve([r], nc.vector.max, top[:, j, :], logits[:, j, :])
        m = P.dve([m], nc.vector.max_index, which[:, j, :], top[:, j, :], logits[:, j, :])
    m = P.dve([m], nc.vector.tensor_copy, whichf[:], which[:])
    r = P.dve([m], nc.vector.tensor_tensor, both[:, :, 1:2], top[:, :, 1:2], top[:, :, 0:1], ALU.subtract)
    r = P.act([r], nc.scalar.activation, both[:, :, 1:2], both[:, :, 1:2], ACT.Exp)
    r = P.dve([r], nc.vector.tensor_scalar, both[:, :, 0:1], both[:, :, 1:2], 1.0, None, ALU.add)
    r = P.dve([r], nc.vector.reciprocal, both[:, :, 0:1], both[:, :, 0:1])
    r = P.dve([r], nc.vector.tensor_tensor, both[:, :, 1:2], both[:, :, 1:2], both[:, :, 0:1], ALU.mult)
    for j in range(TOK_TILES):
        q = P.dve([r, m, iot], nc.vector.tensor_scalar, w[:, j, :], number[:], whichf[:, j, 0:1], both[:, j, 0:1], ALU.is_equal, ALU.mult)
        p = P.dve([r], nc.vector.tensor_scalar, hot[:, j, :], number[:], whichf[:, j, 1:2], both[:, j, 1:2], ALU.is_equal, ALU.mult)
        q = P.dve([p, q], nc.vector.tensor_tensor, w[:, j, :], w[:, j, :], hot[:, j, :], ALU.add)
    t = transpose_back(P, C, [q], w, wT, E)
    spread = linear(P, [t, sels], lambda k, m: sel[:, m, :], [wT], E, lambda m, sl, ps, t: P.act([t], nc.scalar.copy, wB[:, m, sl], ps))
    zero = P.dve([], nc.vector.memset, acc[:], 0.0)
    last = [zero, spread]
    down = []
    for e in range(E):
        s = e % 2
        g = linear(P, [n, here[s], down], lambda k, m: w1[:, s, m * 128:(m + 1) * 128], [h], T, lambda m, sl, ps, t: P.act(
            [t, down], nc.scalar.activation, a[:, m, sl], ps, ACT.Silu))
        u = linear(P, [], lambda k, m: w3[:, s, m * 128:(m + 1) * 128], [h], T, lambda m, sl, ps, t: P.dve(
            [t, g], nc.vector.tensor_tensor, a[:, m, sl], ps, a[:, m, sl], ALU.mult))

        def weigh(m, sl, ps, t):
            q = P.dve([t, last], nc.vector.tensor_tensor, tmp[:, sl], ps, wB[:, e, sl], ALU.mult)
            P.dve([q], nc.vector.tensor_tensor, acc[:, sl], acc[:, sl], tmp[:, sl], ALU.add)
            return q
        down = linear(P, [u], lambda k, m: w2[:, s, k, :], [a[:, k, :] for k in range(T)], 1, weigh)
        last = [P.dve.sig.now()]
        if e + 2 < E:
            here[s] = fetch(e + 2, [P.pe.sig.now()])
    for sl in halves():
        P.dve(last, nc.vector.tensor_tensor, X[:, sl], X[:, sl], acc[:, sl], ALU.add)



def output_projection(P, C, marks, O, weight, X, stack, bias=None):
    parts = O.shape[-1] // 128
    OT = tile(P, stack, "OT", [128, parts, S])
    done = [transpose_back(P, C, marks, O[:, :, f * 128:(f + 1) * 128], OT[:, f, :], 128) for f in range(parts)]
    return linear(P, [done], weight, [OT[:, f, :] for f in range(parts)], 1, add_to_x(P, X, bias))


def values_by_token(P, marks, h, w, heads, dv, V, ones):
    nc = P.nc
    out = []
    width = min(HALF, heads * dv)
    if ones:
        out.append(P.pool([], nc.gpsimd.memset, V[:, :, :, dv:dv + 1], 1.0))
    for j in range(TOK_TILES):
        for c in range(heads * dv // width):
            b = P.bank()
            t = P.pe(marks, nc.tensor.matmul, P.ps[:, b, 0:width], lhsT=h[:, j * 128:(j + 1) * 128],
                     rhs=w[:, c * width:(c + 1) * width], start=True, stop=True)
            k = width // dv
            P.free[b] = P.act([t], nc.scalar.copy, V[:, j, c * k:(c + 1) * k, 0:dv], P.ps[:, b, 0:width].rearrange("p (h d) -> p h d", d=dv))
            out.append(P.free[b])
    return out


def head_of(V, head):
    n, d = V.shape[2], V.shape[3]
    return V[:].rearrange("p j h d -> p j (h d)")[:, :, bass.ds(head * d, d)]


def causal_products(P, C, make_head, heads, Q, K, V, dv, stack, finish):
    nc = P.nc
    Vh = tile(P, stack, "Vh", [128, 2, TOK_TILES, dv])
    A = tile(P, stack, "A", [128, 4, HALF])
    steps = [(half, k) for half in range(2) for k in range(TOK_TILES) if k * 128 < (half + 1) * HALF]
    with P.loop(heads // 2) as pair:
        banks, slots = Ring(P, "score_bank", 4), Ring(P, "A_slot", 4)
        dens = Ring(P, "denominator", 4)
        accs, head_in, vals = Ring(P, "accumulator", 4), Ring(P, "head", 2), Ring(P, "values", 2)
        n = 0
        for s in range(2):
            head = pair * 2 + s
            ready = make_head(s, head, head_in.get(s), banks)
            v = P.dve(vals.get(s), nc.vector.tensor_scalar, Vh[:, s], head_of(V, head), 1.0, None, ALU.mult)

            def products(half, k, slot, m):
                for j in range(4):
                    if half * 4 + j >= k:
                        t = P.pe([m, v], nc.tensor.matmul, P.ps[:, 4 + 2 * s + half, j * dv:(j + 1) * dv],
                                 lhsT=A[:, slot, j * 128:(j + 1) * 128], rhs=Vh[:, s, k, :], start=False, stop=True,
                                 skip_group_check=True)
                slots.put(slot, [t])
                return t

            for half in range(2):
                P.pe(accs.get(2 * s + half), nc.tensor.matmul, P.ps[:, 4 + 2 * s + half, 0:4 * dv], lhsT=C.zero[0:1, 0:128],
                     rhs=C.zero[0:1, 0:4 * dv], start=True, stop=True, skip_group_check=True)
            waiting = []
            for half, k in steps:
                slot = n % 4
                n += 1
                lo = max(0, k * 128 - half * HALF)
                t = P.pe([ready, banks.get(slot)], nc.tensor.matmul, P.ps[:, slot, lo:HALF], lhsT=K[:, s, k * 128:(k + 1) * 128],
                         rhs=Q[:, s, half * HALF + lo:(half + 1) * HALF], start=True, stop=True)
                src, dst, free = P.ps[:, slot, :], A[:, slot, :], slots.get(slot)
                if k * 128 >= half * HALF:
                    m = [P.dve([t, free], nc.vector.tensor_tensor, dst[:, lo:lo + 128], src[:, lo:lo + 128], C.causal[:], ALU.mult)]
                    if lo + 128 < HALF:
                        m.append(P.dve([], nc.vector.tensor_copy, dst[:, lo + 128:HALF], src[:, lo + 128:HALF]))
                else:
                    m = [P.act([t, free], nc.scalar.copy, dst, src)]
                banks.put(slot, m)
                waiting.append((half, k, slot, m))
                if len(waiting) > 2:
                    last = products(*waiting.pop(0))
            head_in.put(s, [t])
            while waiting:
                last = products(*waiting.pop(0))
            vals.put(s, [last])
            for half in range(2):
                view = P.ps[:, 4 + 2 * s + half, 0:4 * dv].rearrange("p (j d) -> p j d", d=dv)
                accs.put(2 * s + half, finish(s, head, half, view, [last], dens))
        for ring in (banks, slots, accs, head_in, vals, dens):
            ring.close()


def cosformer(P, C, io, X, stack):
    nc = P.nc
    H = 16
    d = io["L1_attn_Wq"].shape[1] // H
    wv = load(P, stack, "wv", io["L1_attn_Wv"])
    bv = load(P, stack, "bv", io["L1_attn_bv_row"])
    wo = load(P, stack, "wo", io["L1_attn_Wo"].rearrange("(k p) n -> p k n", p=128), [128, H * d // 128, D])
    bo = load(P, stack, "bo", io["L1_attn_bo"])
    bqk = tile(P, stack, "bqk", [128, 2, 2])
    cs = load(P, stack, "cs", io["cosformer_table"])
    wts = P.stream("weights").now()
    h, tmp = tile(P, stack, "h", [D, S]), tile(P, stack, "tmp", [D, S])
    V = tile(P, stack, "V", [128, TOK_TILES, H, d + 1])
    O = tile(P, stack, "O", [128, TOK_TILES, H * d])
    den = tile(P, stack, "den", [128, 4, 4])
    n = normalize(P, C, [], X, h, tmp)
    n = values_by_token(P, [n, wts], h, wv, H, d, V, True)
    add_row(P, C, n, V, bv, H, d)
    P.barrier()
    Q, K = (tile(P, stack, n, [128, 2, S]) for n in ("Q", "K"))
    w = tile(P, stack, "w", [128, 2, 2, 2 * d])
    arrive = [P.stream("head0"), P.stream("head1")]

    def make_head(s, head, free, banks):
        for j, name in enumerate(("L1_attn_Wq", "L1_attn_Wk")):
            for c in range(2):
                a = P.sp.dma([free], arrive[s], w[:, s, j, c * d:(c + 1) * d], io[name][:, bass.ds(head * d, d)])
        a = P.sp.dma([], arrive[s], bqk[:, s, :], io["L1_attn_bqk_twice"][bass.ds(head, 1)].rearrange("a p j -> p (a j)"))
        marks = []
        for j, dst in enumerate((Q, K)):
            for sl in halves():
                b = 2 * j + sl.start // HALF
                t = P.pe([a, banks.get(b)], nc.tensor.matmul, P.ps[:, b, :], lhsT=w[:, s, j, :], rhs=h[:, sl], start=True, stop=True)
                r = P.act([t, free], nc.scalar.activation, dst[:, s, sl], P.ps[:, b, :], ACT.Relu, bias=bqk[:, s, j:j + 1])
                banks.put(b, [r])
                marks.append(P.dve([r], nc.vector.tensor_tensor, dst[:, s, sl], dst[:, s, sl], cs[:, sl], ALU.mult))
        return marks

    def finish(s, head, half, view, marks, dens):
        z = 2 * s + half
        r = P.dve([marks, dens.get(z)], nc.vector.tensor_scalar, den[:, z, :], view[:, :, d], 1e-6, None, ALU.max)
        r = P.dve([r], nc.vector.reciprocal, den[:, z, :], den[:, z, :])
        for j in range(4):
            r2 = P.dve([r], nc.vector.tensor_scalar, O[:, half * 4 + j, bass.ds(head * d, d)], view[:, j, 0:d], den[:, z, j:j + 1], None, ALU.mult)
        dens.put(z, [r2])
        return [r2]

    causal_products(P, C, make_head, H, Q, K, V, d + 1, stack, finish)
    P.barrier()
    output_projection(P, C, [], O, lambda k, m: wo[:, k, :], X, stack, bo[:, 0:1])


def add_row(P, C, marks, V, row, H, d):
    nc = P.nc
    out = []
    for c in range(H * d // HALF):
        b = P.bank()
        t = P.pe(marks, nc.tensor.matmul, P.ps[:, b, :], lhsT=C.ones[0:1, :], rhs=row[0:1, c * HALF:(c + 1) * HALF], start=True, stop=True)
        k = HALF // d
        for j in range(V.shape[1]):
            v = V[:, j, c * k:(c + 1) * k, 0:d]
            P.free[b] = P.dve([t], nc.vector.tensor_tensor, v, v, P.ps[:, b, :].rearrange("p (h d) -> p h d", d=d), ALU.add)
        out.append(P.free[b])
    return out


def retention(P, C, io, X, stack):
    nc = P.nc
    H = D // 16
    d = D // H
    names = ("W_Q", "W_Q_turned", "W_K", "W_K_turned", "W_V", "W_G", "W_O")
    w = {n: load(P, stack, n, io["L3_attn_" + n]) for n in names}
    tables = {n: load(P, stack, n, io["retention_" + n]) for n in ("q_cos", "q_sin", "k_cos", "k_sin")}
    gw, gb = (load(P, stack, n, io["L3_attn_" + n]) for n in ("gn_weight", "gn_bias"))
    wts = P.stream("weights").now()
    h, tmp, tmp2 = (tile(P, stack, n, [D, S]) for n in ("h", "tmp", "tmp2"))
    V = tile(P, stack, "V", [128, TOK_TILES, H, d])
    O = tile(P, stack, "O", [128, TOK_TILES, D])
    n = normalize(P, C, [], X, h, tmp)
    v = values_by_token(P, [n, wts], h, w["W_V"], H, d, V, False)
    scratch = nc.dram_tensor("retention_heads", (2, D, S), F32, kind="Internal").ap()
    for j, x in enumerate("QK"):
        write_rotated(P, C, [n, wts], h, w["W_" + x], w["W_" + x + "_turned"], tables["q_cos" if x == "Q" else "k_cos"],
                      tables["q_sin" if x == "Q" else "k_sin"], tmp, tmp2, scratch[j])
    P.barrier()
    Q, K = (tile(P, stack, n, [d, 2, S]) for n in ("Q", "K"))
    arrive = [P.stream("head0"), P.stream("head1")]

    def make_head(s, head, free, banks):
        P.sp.dma([free], arrive[s], Q[:, s, :], scratch[0, bass.ds(head * d, d), :])
        return [P.sp.dma([], arrive[s], K[:, s, :], scratch[1, bass.ds(head * d, d), :])]

    def finish(s, head, half, view, marks, dens):
        return [P.dve(marks, nc.vector.tensor_scalar, O[:, half * 4:half * 4 + 4, bass.ds(head * d, d)], view, 1.0, None, ALU.mult)]

    causal_products(P, C, make_head, H, Q, K, V, d, stack, finish)
    P.barrier()
    G = TOK_TILES * H
    sq = tile(P, stack, "sq", [128, G, d])
    st = tile(P, stack, "st", [128, 2, G])
    Og = O[:].rearrange("p j (h d) -> p (j h) d", d=d)
    spread = lambda t: t.unsqueeze(2).to_broadcast([128, G, d])
    r = P.dve([], nc.vector.tensor_reduce, st[:, 0, :], Og, AX, ALU.add)
    r = P.dve([r], nc.vector.tensor_scalar, st[:, 0, :], st[:, 0, :], 1.0 / d, None, ALU.mult)
    r = P.dve([r], nc.vector.tensor_tensor, Og, Og, spread(st[:, 0, :]), ALU.subtract)
    q = P.dve([r], nc.vector.tensor_tensor, sq[:], Og, Og, ALU.mult)
    q = P.dve([q], nc.vector.tensor_reduce, st[:, 1, :], sq[:], AX, ALU.add)
    q = P.act([q], nc.scalar.activation, st[:, 1, :], st[:, 1, :], ACT.Sqrt, bias=C.eps[:, 0:1], scale=1.0 / d)
    q = P.dve([q], nc.vector.reciprocal, st[:, 1, :], st[:, 1, :])
    q = P.dve([q], nc.vector.tensor_tensor, Og, Og, spread(st[:, 1, :]), ALU.mult)
    y = transpose_back(P, C, [q], O[:], tmp, 128)
    y = P.dve([y], nc.vector.tensor_scalar, tmp[:], tmp[:], gw[:, 0:1], gb[:, 0:1], ALU.mult, ALU.add)
    g = linear(P, [], lambda k, m: w["W_G"][:], [h], 1, lambda m, sl, ps, t: P.act([t], nc.scalar.activation, tmp2[:, sl], ps, ACT.Silu))
    y = P.dve([y, g], nc.vector.tensor_tensor, tmp[:], tmp[:], tmp2[:], ALU.mult)
    linear(P, [y], lambda k, m: w["W_O"][:], [tmp], 1, add_to_x(P, X))


def write_rotated(P, C, marks, h, w, w_turned, cos, sin, a, b, dst):
    nc = P.nc
    stored = P.stream("stored")
    old = [stored.now()]
    done = []
    linear(P, [marks], lambda k, m: w[:], [h], 1, lambda m, sl, ps, t: P.dve([t, old], nc.vector.tensor_tensor, a[:, sl], ps, cos[:, sl], ALU.mult))

    def turned(m, sl, ps, t):
        r = P.dve([t], nc.vector.tensor_tensor, b[:, sl], ps, sin[:, sl], ALU.mult)
        done.append(P.dve([r], nc.vector.tensor_tensor, a[:, sl], a[:, sl], b[:, sl], ALU.add))
        return r
    linear(P, [marks], lambda k, m: w_turned[:], [h], 1, turned)
    return P.sp.dma(done, stored, dst, a[:])


def softmax_heads(P, C, head_in, Q, K, V, dv, O, causal, stack, pairs):
    nc = P.nc
    Pq, PT = tile(P, stack, "Pq", [128, 2, S]), tile(P, stack, "PT", [128, 2, S])
    st = tile(P, stack, "st", [128, 2, 4])

    def one(s, head, rings):
        scores, probs, turned, outs, ins, tbank = rings
        ready = head_in(s, head, ins.get(s))

        def front(q):
            p = q % 2
            n = (q + 1) * 128 if causal else S
            for c in range(0, n, HALF):
                w = min(HALF, n - c)
                t = P.pe([ready, scores.get(p)], nc.tensor.matmul, P.ps[:, 2 * p + c // HALF, 0:w], lhsT=Q[:, s, q * 128:(q + 1) * 128],
                         rhs=K[:, s, c:c + w], start=True, stop=True)
            ps = P.ps[:, 2 * p:2 * p + 2, :].rearrange("p a b -> p (a b)")[:, 0:n]
            if causal:
                t = P.dve([t], nc.vector.tensor_tensor, ps[:, n - 128:n], ps[:, n - 128:n], C.below[:], ALU.add)
            m = P.dve([t, probs.get(p)], nc.vector.tensor_reduce, st[:, p, 0:1], ps, AX, ALU.max, negate=True)
            e = P.act([m, t], nc.scalar.activation, Pq[:, p, 0:n], ps, ACT.Exp, bias=st[:, p, 0:1], accum_out=st[:, p, 1:2])
            scores.put(p, [e])
            return P.dve([e], nc.vector.reciprocal, st[:, p, 2:3], st[:, p, 1:2])

        def back(q, r):
            p = q % 2
            tiles = q + 1 if causal else TOK_TILES
            copies = []
            for c in range(0, tiles, 4):
                k = min(4, tiles - c)
                for j in range(c, c + k):
                    t = P.pe([r, tbank.get(c // 4)], nc.tensor.transpose, P.ps[:, 4 + c // 4, (j - c) * 128:(j - c + 1) * 128],
                             Pq[:, p, j * 128:(j + 1) * 128], C.ident[:])
                eng, op = ((P.act, nc.scalar.copy), (P.dve, nc.vector.tensor_copy))[(c // 4 + q) % 2]
                m = eng([t, turned.get(p)], op, PT[:, p, c * 128:(c + k) * 128], P.ps[:, 4 + c // 4, 0:k * 128])
                copies.append(m)
                tbank.put(c // 4, [m])
            for j in range(tiles):
                t = P.pe([copies, outs.get(p)], nc.tensor.matmul, P.ps[:, 6 + p, 0:dv], lhsT=PT[:, p, j * 128:(j + 1) * 128],
                         rhs=V[:, s, j, :], start=j == 0, stop=j == tiles - 1)
            turned.put(p, [t])
            dst = O[:, q, 0:dv] if pairs is None else O[:, q, bass.ds(head * dv, dv)]
            m = P.dve([t], nc.vector.tensor_scalar, dst, P.ps[:, 6 + p, 0:dv], st[:, p, 2:3], None, ALU.mult)
            outs.put(p, [m])
            probs.put(p, [t, m])
            return t

        r = front(0)
        for q in range(TOK_TILES):
            nxt = front(q + 1) if q + 1 < TOK_TILES else None
            t = back(q, r)
            r = nxt
        ins.put(s, [t])

    rings = lambda: [Ring(P, n, 2) for n in ("scores", "probs", "turned", "outs", "ins", "tbank")]
    if pairs is None:
        one(0, 0, rings())
    else:
        with P.loop(pairs) as pair:
            r = rings()
            for s in range(2):
                one(s, pair * 2 + s, r)
            for x in r:
                x.close()


def causal_attention(P, C, io, X, stack):
    nc = P.nc
    H = 16
    d = D // H
    w = {n: load(P, stack, n, io["L0_attn_" + n]) for n in ("W_Q", "W_Q_turned", "W_K", "W_K_turned", "W_V", "W_O")}
    tables = {n: load(P, stack, n, io["rope_" + n]) for n in ("q_cos", "q_sin", "k_cos", "k_sin")}
    wts = P.stream("weights").now()
    h, tmp, tmp2 = (tile(P, stack, n, [D, S]) for n in ("h", "tmp", "tmp2"))
    V = tile(P, stack, "V", [128, TOK_TILES, H, d])
    O = tile(P, stack, "O", [128, TOK_TILES, D])
    n = normalize(P, C, [], X, h, tmp)
    values_by_token(P, [n, wts], h, w["W_V"], H, d, V, False)
    scratch = nc.dram_tensor("rope_heads", (2, D, S), F32, kind="Internal").ap()
    for j, x in enumerate("QK"):
        write_rotated(P, C, [n, wts], h, w["W_" + x], w["W_" + x + "_turned"], tables["q_cos" if x == "Q" else "k_cos"],
                      tables["q_sin" if x == "Q" else "k_sin"], tmp, tmp2, scratch[j])
    P.barrier()
    Q, K = (tile(P, stack, n, [d, 2, S]) for n in ("Q", "K"))
    Vh = tile(P, stack, "Vh", [128, 2, TOK_TILES, d])
    arrive = [P.stream("head0"), P.stream("head1")]

    def head_in(s, head, free):
        P.sp.dma([free], arrive[s], Q[:, s, :], scratch[0, bass.ds(head * d, d), :])
        a = P.sp.dma([], arrive[s], K[:, s, :], scratch[1, bass.ds(head * d, d), :])
        return [a, P.dve(free, nc.vector.tensor_scalar, Vh[:, s], head_of(V, head), 1.0, None, ALU.mult)]

    softmax_heads(P, C, head_in, Q, K, Vh, d, O, True, stack, H // 2)
    P.barrier()
    output_projection(P, C, [], O, lambda k, m: w["W_O"][:], X, stack)


def attention_of_experts(P, C, io, X, stack):
    nc = P.nc
    E = io["L2_ffn_sim_matrix"].shape[1]
    sim = load(P, stack, "sim", io["L2_ffn_sim_matrix"])
    gates = load(P, stack, "gates", io["L2_ffn_gates_row"])
    wts = P.stream("weights").now()
    w = tile(P, stack, "w", [128, 2, 4, D])
    h, tmp = tile(P, stack, "h", [D, S]), tile(P, stack, "tmp", [D, S])
    wB = tile(P, stack, "wB", [128, E, S])
    xe = tile(P, stack, "xe", [128, 2, S])
    Q, K, Vt = (tile(P, stack, n, [128, 1, S]) for n in ("Q", "K", "Vt"))
    V = tile(P, stack, "V", [128, 1, TOK_TILES, D])
    O = tile(P, stack, "O", [128, TOK_TILES, D])
    sel, wT = tile(P, stack, "sel", [E, E, 128]), tile(P, stack, "wT", [E, S])
    loads = [P.stream("expert0"), P.stream("expert1")]
    sels = one_hot_rows(P, C, [], None, E, sel)
    names = ("q_proj", "k_proj", "v_proj", "o_proj")

    def fetch(e, marks, which):
        for n in which:
            a = P.sp.dma(marks, loads[e % 2], w[:, e % 2, n, :], io["L2_ffn_" + names[n]][e])
        return a
    here = [fetch(0, [], range(3)), fetch(1, [], range(3))]
    n = normalize(P, C, [], X, h, tmp)
    g = tile(P, stack, "g", [128, 4, E])
    r = P.act([wts], nc.scalar.activation, g[:, 0, :], sim[:], ACT.Square)
    b = P.bank()
    t = P.pe([r], nc.tensor.matmul, P.ps[:, b, 0:E], lhsT=C.mean[:], rhs=g[:, 0, :], start=True, stop=True)
    r = P.act([t], nc.scalar.activation, g[:, 1, :], P.ps[:, b, 0:E], ACT.Sqrt, scale=float(D))
    P.free[b] = r
    r = P.dve([r], nc.vector.tensor_scalar, g[:, 1, :], g[:, 1, :], 1e-12, None, ALU.max)
    r = P.dve([r], nc.vector.reciprocal, g[:, 1, :], g[:, 1, :])
    r = P.dve([r], nc.vector.tensor_tensor, g[:, 0, :], sim[:], g[:, 1, :], ALU.mult)
    b = P.bank()
    t = P.pe([], nc.tensor.matmul, P.ps[:, b, 0:E], lhsT=C.ones[0:1, :], rhs=gates[0:1, :], start=True, stop=True)
    s = P.act([t], nc.scalar.activation, g[:, 2, :], P.ps[:, b, 0:E], ACT.Sigmoid)
    P.free[b] = s
    q = P.act([n], nc.scalar.activation, tmp[:], h[:], ACT.Square)
    L = tile(P, stack, "L", [128, TOK_TILES, E])
    M, F = tile(P, stack, "M", [128, TOK_TILES, E]), tile(P, stack, "F", [128, TOK_TILES, E])
    top, which = tile(P, stack, "top", [128, TOK_TILES, 8]), tile(P, stack, "which", [128, TOK_TILES, 8], U32)
    whichf, norm = tile(P, stack, "whichf", [128, TOK_TILES, 8]), tile(P, stack, "norm", [128, TOK_TILES, 4])
    number = tile(P, stack, "number", [128, E])
    iot = P.pool([], nc.gpsimd.iota, number[:], [[1, E]], 0, 0, allow_small_or_imprecise_dtypes=True)
    b = P.bank()
    b2 = P.bank()
    for j in range(TOK_TILES):
        P.pe([q], nc.tensor.matmul, P.ps[:, b, j:j + 1], lhsT=tmp[:, j * 128:(j + 1) * 128], rhs=C.ones_col[:], start=True, stop=True)
        t = P.pe([r], nc.tensor.matmul, P.ps[:, b2, j * E:(j + 1) * E], lhsT=h[:, j * 128:(j + 1) * 128], rhs=g[:, 0, :], start=True, stop=True)
    r = P.act([t], nc.scalar.activation, norm[:, :, 0:1], P.ps[:, b, 0:TOK_TILES].unsqueeze(2), ACT.Sqrt)
    P.free[b] = r
    r = P.dve([r], nc.vector.tensor_scalar, norm[:, :, 0:1], norm[:, :, 0:1], 1e-12, None, ALU.max)
    r = P.dve([r], nc.vector.reciprocal, norm[:, :, 0:1], norm[:, :, 0:1])
    wide = lambda a: a.to_broadcast([128, TOK_TILES, E])
    each = lambda a: a.unsqueeze(1).to_broadcast([128, TOK_TILES, E])
    r = P.dve([r], nc.vector.tensor_tensor, L[:], P.ps[:, b2, 0:TOK_TILES * E].rearrange("p (j e) -> p j e", e=E), wide(norm[:, :, 0:1]), ALU.mult)
    P.free[b2] = r
    logits = P.dve([r, s], nc.vector.tensor_tensor, L[:], L[:], each(g[:, 2, :]), ALU.subtract)
    for j in range(TOK_TILES):
        m = P.dve([logits], nc.vector.max, top[:, j, :], L[:, j, :])
        m = P.dve([m], nc.vector.max_index, which[:, j, :], top[:, j, :], L[:, j, :])
    m = P.dve([m], nc.vector.tensor_copy, whichf[:], which[:])
    k = P.dve([logits], nc.vector.tensor_scalar, M[:], L[:], 0.0, None, ALU.is_gt)
    f = P.dve([m, iot], nc.vector.tensor_tensor, F[:], each(number[:]), wide(whichf[:, :, 0:1]), ALU.is_equal)
    f2 = P.dve([m, iot], nc.vector.tensor_tensor, wB[:, 0, 0:TOK_TILES * E].rearrange("p (j e) -> p j e", e=E), each(number[:]), wide(whichf[:, :, 1:2]), ALU.is_equal)
    f = P.dve([f, f2], nc.vector.tensor_tensor, F[:], F[:], wB[:, 0, 0:TOK_TILES * E].rearrange("p (j e) -> p j e", e=E), ALU.add)
    i = P.dve([m], nc.vector.tensor_scalar, norm[:, :, 1:2], top[:, :, 0:1], 0.0, None, ALU.is_le)
    f = P.dve([f, i], nc.vector.tensor_tensor, F[:], F[:], wide(norm[:, :, 1:2]), ALU.mult)
    k = P.dve([f, k], nc.vector.tensor_tensor, M[:], M[:], F[:], ALU.add)
    r = P.dve([m], nc.vector.tensor_scalar, norm[:, :, 2:3], top[:, :, 0:1], 0.0, None, ALU.max)
    r = P.dve([r, k, f], nc.vector.tensor_scalar, L[:], L[:], 0.0, None, ALU.max)
    r = P.dve([r], nc.vector.tensor_tensor, L[:], L[:], wide(norm[:, :, 2:3]), ALU.subtract)
    r = P.act([r], nc.scalar.activation, L[:], L[:], ACT.Exp)
    r = P.dve([r], nc.vector.tensor_tensor, L[:], L[:], M[:], ALU.mult)
    r2 = P.dve([r], nc.vector.tensor_reduce, norm[:, :, 3:4], L[:], AX, ALU.add)
    r2 = P.dve([r2], nc.vector.reciprocal, norm[:, :, 3:4], norm[:, :, 3:4])
    r2 = P.dve([r2], nc.vector.tensor_tensor, L[:], L[:], wide(norm[:, :, 3:4]), ALU.mult)
    t = transpose_back(P, C, [r2], L, wT, E)
    spread = linear(P, [t, sels, f], lambda k, m: sel[:, m, :], [wT], E, lambda m, sl, ps, t: P.act([t, f], nc.scalar.copy, wB[:, m, sl], ps))
    P.barrier()
    used = [[], []]
    for e in range(E):
        z = e % 2
        m = P.dve([used[z]], nc.vector.tensor_tensor, xe[:, z, :], h[:], wB[:, e, :], ALU.mult)
        for n in range(3):
            for i, sl in enumerate(halves()):
                t = P.pe([m, here[z]], nc.tensor.matmul, P.ps[:, 2 * n + i, :], lhsT=w[:, z, n, :], rhs=xe[:, z, sl], start=e == 0, stop=e == E - 1)
        used[z] = [t]
        if e + 2 < E:
            here[z] = fetch(e + 2, [t], range(3))
    out = []
    for n, dst in enumerate((Q, K, Vt)):
        for i, sl in enumerate(halves()):
            out.append(P.act([t], nc.scalar.activation, dst[:, 0, sl], P.ps[:, 2 * n + i, :], ACT.Copy, scale=1.0 / math.sqrt(D) if n == 0 else 1.0))
    here = [fetch(0, [t], [3]), fetch(1, [t], [3])]
    P.barrier()
    for i in range(2):
        b = P.bank()
        for j in range(4):
            t = P.pe([], nc.tensor.transpose, P.ps[:, b, j * 128:(j + 1) * 128], Vt[:, 0, (4 * i + j) * 128:(4 * i + j + 1) * 128], C.ident[:])
        P.free[b] = P.act([t], nc.scalar.copy, V[:, 0, 4 * i:4 * i + 4, :], P.ps[:, b, :].rearrange("p (j d) -> p j d", d=D))
    P.barrier()
    softmax_heads(P, C, lambda s, head, free: [], Q, K, V, D, O, False, stack, None)
    P.barrier()
    t = transpose_back(P, C, [], O[:], Q[:, 0, :], 128)
    P.barrier()
    used = [[], []]
    for e in range(E):
        z = e % 2
        m = P.dve([used[z]], nc.vector.tensor_tensor, xe[:, z, :], Q[:, 0, :], wB[:, e, :], ALU.mult)
        for i, sl in enumerate(halves()):
            t = P.pe([m, here[z]], nc.tensor.matmul, P.ps[:, i, :], lhsT=w[:, z, 3, :], rhs=xe[:, z, sl], start=e == 0, stop=e == E - 1)
        used[z] = [t]
        if e + 2 < E:
            here[z] = fetch(e + 2, [t], [3])
    for i, sl in enumerate(halves()):
        add_to_x(P, X)(0, sl, P.ps[:, i, :], t)



class Cross:

    def __init__(self, P, name, heads, d, split, softmax, masked):
        nc = P.nc
        self.name, self.H, self.d, self.split, self.softmax, self.masked = name, heads, d, split, softmax, masked
        self.dt = BF16 if split else F32
        self.rows = len(TERMS) * d if split else d
        self.dv = d + 1 if softmax else d
        self.groups = {8: 4, 64: 2, 128: 1}[d]
        more = self.more = 2 if heads > 1 else 0
        dram = lambda n, shape, dt: nc.dram_tensor(f"{name}_dram_{n}", shape, dt, kind="Internal").ap()
        self.K = dram("K", (CHUNKS, heads + more, self.rows, CHUNK), self.dt)
        self.Q = dram("Q", (heads + more, self.rows, S), self.dt)
        self.V = dram("V", (CHUNKS, heads + more, 128, TPC * self.dv), F32)
        self.O = dram("O", (heads, 128, S), F32)
        if softmax and not split:
            self.Kb, self.Qb = dram("Kb", (CHUNKS, heads + more, d, CHUNK), BF16), dram("Qb", (heads + more, d, S), BF16)
        if softmax:
            self.den = dram("den", (heads, S), F32)
            self.mask = dram("mask", (CHUNKS, CHUNK), F32)
            self.mask_parts = dram("mask_parts", (CHUNKS, 2, CHUNK), BF16)


TERMS = [(0, 0), (0, 1), (0, 2), (1, 0), (1, 1), (2, 0)]
CHUNKS = 0


def split_parts(P, marks, src, parts, rest):
    nc = P.nc
    a = P.dve([marks], nc.vector.tensor_copy, parts[:, 0], src)
    b = P.dve([a], nc.vector.tensor_tensor, rest, src, parts[:, 0], ALU.subtract)
    a = P.dve([b], nc.vector.tensor_copy, parts[:, 1], rest)
    b = P.dve([a], nc.vector.tensor_tensor, src, rest, parts[:, 1], ALU.subtract)
    return P.dve([b], nc.vector.tensor_copy, parts[:, 2], src)


def mask_rows(P, X, mask_src, fill, stack):
    nc = P.nc
    n = N_KEYS
    full, rest = n // CHUNK, n % CHUNK
    m = tile(P, stack, X.name + "_mask", [CHUNKS, CHUNK], F32)
    parts, t = tile(P, stack, X.name + "_mask_parts", [CHUNKS, 2, CHUNK], BF16), tile(P, stack, X.name + "_mask_rest", [CHUNKS, CHUNK])
    raw = tile(P, stack, X.name + "_mask_raw", [CHUNKS, CHUNK], I32 if mask_src is None else mask_src.dtype)
    z = P.dve([], nc.vector.memset, raw[:], 0)
    sig = P.stream("mask")
    src = P.io_ones if mask_src is None else mask_src
    if full:
        P.sp.dma([z], sig, raw[0:full, :], src[0:full * CHUNK].rearrange("(c n) -> c n", n=CHUNK))
    if rest:
        P.sp.dma([z], sig, raw[full:full + 1, 0:rest], src[full * CHUNK:n].unsqueeze(0))
    r = P.dve([sig.now()], nc.vector.tensor_copy, m[:], raw[:])
    r = P.dve([r], nc.vector.tensor_scalar, m[:], m[:], 0.0, fill, ALU.is_equal, ALU.mult)
    P.sp.dma([r], sig, X.mask, m[:])
    a = P.dve([r], nc.vector.tensor_copy, parts[:, 0, :], m[:])
    b = P.dve([a], nc.vector.tensor_tensor, t[:], m[:], parts[:, 0, :], ALU.subtract)
    a = P.dve([b], nc.vector.tensor_copy, parts[:, 1, :], t[:])
    P.sp.dma([a], sig, X.mask_parts, parts[:])


def keys_and_values(P, C, io, X, wk, bk, wv):
    nc = P.nc
    H, d, dv = X.H, X.d, X.dv
    F = H * d
    with ExitStack() as stack:
        if X.softmax:
            mask_rows(P, X, X.masked[0], X.masked[1], stack)
        wk_t, wv_t = (load(P, stack, n, w) for n, w in (("wk", wk), ("wv", wv)))
        bk_t = load(P, stack, "bk", bk) if bk is not None else None
        P.barrier()
        ctxt = tile(P, stack, "ctxt", [128, 2, CHUNK])
        valid = load(P, stack, "valid", io["valid_keys"])
        keep = tile(P, stack, "keep", [128, 2, CHUNK]) if X.split and X.softmax else None
        T = F // 128
        Kf = tile(P, stack, "Kf", [128, 2, T, CHUNK])
        Kb = tile(P, stack, "Kb", [128, 2, T, CHUNK], BF16) if not X.split and X.softmax else None
        parts, rest = (tile(P, stack, "parts", [128, 3, CHUNK], BF16), tile(P, stack, "rest", [128, CHUNK])) if X.split else (None, None)
        Vt = tile(P, stack, "Vt", [128, 2, H, TPC, dv])
        width = min(HALF, F)
        arrive, stored = [P.stream("chunk0"), P.stream("chunk1")], [P.stream("stored0"), P.stream("stored1")]
        P.barrier()

        def one(c, z, rings):
            banks, ins, outs, work = rings
            free = ins.get(z)
            a = P.sp.dma([free], arrive[z], ctxt[:, z, :], io["ctx_1024"][:, bass.ds(c * CHUNK, CHUNK)])
            if keep is not None:
                a = P.sp.dma([], arrive[z], keep[:, z, :], X.mask[bass.ds(c, 1), :].to_broadcast([128, CHUNK]))
            stores = []
            old = outs.get(z)
            n = 0
            for f in range(T):
                b = n % 8
                n += 1
                t = P.pe([a, banks.get(b)], nc.tensor.matmul, P.ps[:, b, :], lhsT=wk_t[:, f * 128:(f + 1) * 128], rhs=ctxt[:, z, :], start=True, stop=True)
                if bk_t is None:
                    r = P.act([t, old, work.get(0)], nc.scalar.copy, Kf[:, z, f, :], P.ps[:, b, :])
                else:
                    r = P.act([t, old, work.get(0)], nc.scalar.activation, Kf[:, z, f, :], P.ps[:, b, :], ACT.Identity, bias=bk_t[:, f:f + 1])
                banks.put(b, [r])
                if Kb is not None:
                    q = P.dve([r, old], nc.vector.tensor_copy, Kb[:, z, f, :], Kf[:, z, f, :])
                    stores.append((q, X.Kb[bass.ds(c, 1), f * 128 // d:(f + 1) * 128 // d].rearrange("a h r n -> (a h r) n"), Kb[:, z, f, :]))
                    if f == 0 and X.more:
                        stores.append((q, X.Kb[bass.ds(c, 1), H:H + 2].rearrange("a h r n -> (a h r) n"), Kb[0:2 * d, z, 0, :]))
                if not X.split:
                    stores.append((r, X.K[bass.ds(c, 1), f * 128 // d:(f + 1) * 128 // d].rearrange("a h r n -> (a h r) n"), Kf[:, z, f, :]))
                    if f == 0 and X.more:
                        stores.append((r, X.K[bass.ds(c, 1), H:H + 2].rearrange("a h r n -> (a h r) n"), Kf[0:2 * d, z, 0, :]))
            if X.split:
                if keep is not None:
                    k = P.dve([a, free], nc.vector.tensor_scalar, keep[:, z, :], keep[:, z, :], 0.0, None, ALU.is_equal)
                    r = P.dve([r, k], nc.vector.tensor_tensor, Kf[:, z, 0, :], Kf[:, z, 0, :], keep[:, z, :], ALU.mult)
                q = split_parts(P, [r, outs.get(2)], Kf[:, z, 0, :], parts, rest[:])
                work.put(0, [q])
                for g, (_, p) in enumerate(TERMS):
                    stores.append((q, X.K[bass.ds(c, 1), 0:H, g * d:(g + 1) * d, :].rearrange("a h r n -> (a h) r n"), parts[:, p, :]))
                    stores.append((q, X.K[bass.ds(c, 1), H:H + 2, g * d:(g + 1) * d, :].rearrange("a h r n -> (a h) r n"), parts[0:2 * d, p, :]))
            for j in range(TPC):
                for w in range(F // width):
                    b = n % 8
                    n += 1
                    t = P.pe([a, banks.get(b)], nc.tensor.matmul, P.ps[:, b, 0:width], lhsT=ctxt[:, z, j * 128:(j + 1) * 128],
                             rhs=wv_t[:, w * width:(w + 1) * width], start=True, stop=True)
                    k = width // d
                    r = P.dve([t, old], nc.vector.tensor_copy, Vt[:, z, w * k:(w + 1) * k, j, 0:d], P.ps[:, b, 0:width].rearrange("p (h d) -> p h d", d=d))
                    banks.put(b, [r])
                if X.softmax:
                    one_col = Vt[:, z, :, j, d:dv].rearrange("p h a -> p (h a)")
                    r = P.dve([old], nc.vector.tensor_scalar, one_col, C.ones16[:, 0:H], valid_chunk[:, z, j:j + 1], None, ALU.mult)
            ins.put(z, [t, r])
            stores.append((r, X.V[bass.ds(c, 1), 0:H].rearrange("a h p x -> p (a h) x"), Vt[:, z].rearrange("p h j x -> p h (j x)")))
            if X.more:
                stores.append((r, X.V[bass.ds(c, 1), H:H + 2].rearrange("a h p x -> p (a h) x"), Vt[:, z, 0:2].rearrange("p h j x -> p h (j x)")))
            for m, dst, src in stores:
                s = P.sp.dma([m], stored[z], dst, src)
            outs.put(z, [s])
            outs.put(2, [s])

        valid_chunk = tile(P, stack, "valid_chunk", [128, 2, TPC])

        def chunk(c, z, rings):
            if X.softmax:
                P.dve([rings[1].get(z)], nc.vector.tensor_scalar, valid_chunk[:, z, :], valid[:, bass.ds(c * TPC, TPC)], 1.0, None, ALU.mult)
                P.dve.wait(P.dve.sig.now())
            one(c, z, rings)

        make = lambda: [Ring(P, n, k) for n, k in (("kv_bank", 8), ("ctx", 2), ("out", 3), ("work", 1))]
        with P.loop(CHUNKS // 2) as pair:
            rings = make()
            for z in range(2):
                chunk(pair * 2 + z, z, rings)
            for r in rings:
                r.close()
        P.barrier()
        if CHUNKS % 2:
            chunk(CHUNKS - 1, 0, make())
        P.barrier()


def queries(P, C, io, X, h, wq, bq, tmp):
    nc = P.nc
    scale = 1.0 / math.sqrt(X.d)
    with ExitStack() as stack:
        wq_t = load(P, stack, "wq", wq)
        bq_t = load(P, stack, "bq", bq) if bq is not None else None
        T = X.H * X.d // 128
        Qf = tile(P, stack, "Qf", [128, T, S])
        Qb = tile(P, stack, "Qb16", [128, T, S], BF16) if not X.split and X.softmax else None
        wts = P.stream("weights").now()
        sig = P.stream("stored0")
        r = linear(P, [wts, C.normed], lambda k, m: wq_t[:, m * 128:(m + 1) * 128], [h], T, lambda m, sl, ps, t: P.dve(
            [t], nc.vector.tensor_scalar, Qf[:, m, sl], ps, bq_t[:, m:m + 1] if bq_t is not None else 0.0, scale, ALU.add, ALU.mult))
        if X.split:
            parts, rest = tile(P, stack, "qparts", [128, 3, S], BF16), tile(P, stack, "qrest", [128, S])
            q = split_parts(P, [r], Qf[:, 0, :], parts, rest[:])
            for g, (p, _) in enumerate(TERMS):
                P.sp.dma([q], sig, X.Q[0:X.H, g * X.d:(g + 1) * X.d, :], parts[:, p, :])
                P.sp.dma([q], sig, X.Q[X.H:X.H + 2, g * X.d:(g + 1) * X.d, :], parts[0:2 * X.d, p, :])
        else:
            for f in range(T):
                k = slice(f * 128 // X.d, (f + 1) * 128 // X.d)
                P.sp.dma([r], sig, X.Q[k].rearrange("h r n -> (h r) n"), Qf[:, f, :])
                if f == 0 and X.more:
                    P.sp.dma([r], sig, X.Q[X.H:].rearrange("h r n -> (h r) n"), Qf[0:2 * X.d, 0, :])
                if Qb is not None:
                    q = P.act([r], nc.scalar.copy, Qb[:, f, :], Qf[:, f, :])
                    P.sp.dma([q], sig, X.Qb[k].rearrange("h r n -> (h r) n"), Qb[:, f, :])
                    if f == 0 and X.more:
                        P.sp.dma([q], sig, X.Qb[X.H:].rearrange("h r n -> (h r) n"), Qb[0:2 * X.d, 0, :])
        P.barrier()


def cross_heads(P, C, X, stack):
    nc = P.nc
    H, d, dv, rows, dt, G = X.H, X.d, X.dv, X.rows, X.dt, X.groups
    wide = d == 128
    aux = 64
    n_m = 1 if (dt == F32 and not wide) else 2
    total = rows if wide else aux + 2 * max(n_m, 2 if dt == BF16 else 1)
    width = 128 // G
    own_sum = X.softmax and d > 32
    spread_v = dv if not own_sum else d

    Kc = tile(P, stack, "Kc", [total, 2, CHUNK], dt)
    Vc = tile(P, stack, "Vc", [128, 2, TPC, dv])
    Qc = tile(P, stack, "Qc", [total, S], dt)
    Pr = tile(P, stack, "Pr", [128, 2 * TPC, S])
    Oc = tile(P, stack, "Oc", [128, S])
    kd = [P.stream(f"key_chunk{n}") for n in range(2)]
    vd = [P.stream(f"value_chunk{n}") for n in range(2)]
    kn = [P.stream(f"next_chunk{n}") for n in range(2)]
    q_in, q_next, stored = P.stream("query"), P.stream("next_query"), P.stream("head_stored")
    if own_sum:
        Ps, Dc = tile(P, stack, "Ps", [128, S]), tile(P, stack, "Dc", [1, S])
        sum_stored = P.stream("sum_stored")
    if not wide and total > rows:
        for t in (Kc, Qc):
            if aux > rows:
                P.dve([], nc.vector.memset, t[32:aux], 0.0)
            P.dve([], nc.vector.memset, t[aux:total], 0.0)
        P.barrier()
    if X.softmax:
        Kn = tile(P, stack, "Kn", [total, 2, CHUNK], BF16)
        Qn = tile(P, stack, "Qn", [total, S], BF16)
        mx, red = tile(P, stack, "mx", [128, TOK_TILES]), tile(P, stack, "red", [128, 2, TOK_TILES])
        mparts = tile(P, stack, "mparts", [128, 2, TOK_TILES], BF16)
        mneg, mrest = tile(P, stack, "mneg", [128, TOK_TILES]), tile(P, stack, "mrest", [128, TOK_TILES])
        if wide:
            Ka, Qa, Qa0 = tile(P, stack, "Ka", [68, 2, CHUNK], BF16), tile(P, stack, "Qa", [68, S], BF16), tile(P, stack, "Qa0", [68, S], BF16)
            for t in (Ka, Qa, Qa0):
                P.dve([], nc.vector.memset, t[:], 0.0)
            P.barrier()
            P.dve([], nc.vector.memset, Ka[0:2], 1.0)
            P.dve([], nc.vector.memset, Qa[0:4], 1.0)
            P.dve([], nc.vector.memset, Qa0[0:4], 1.0)
            P.barrier()
            P.dve([], nc.vector.memset, Qa0[0:2], 0.0)
        else:
            for t in (Kn, Qn):
                if aux > rows:
                    P.dve([], nc.vector.memset, t[32:aux], 0.0)
            for t in (Kc, Kn):
                P.dve([], nc.vector.memset, t[aux:aux + n_m], 1.0)
            for t in (Qc, Qn):
                P.dve([], nc.vector.memset, t[aux:total], 1.0)
            P.barrier()
            P.dve([], nc.vector.memset, Qn[aux:aux + n_m], 0.0)
    P.barrier()

    def mask_into(marks, sig, dst, c):
        if dst.dtype == F32:
            return P.sp.dma(marks, sig, dst, X.mask[bass.ds(c, 1), :])
        return P.sp.dma(marks, sig, dst, X.mask_parts[bass.ds(c, 1), 0:n_m].rearrange("a m n -> (a m) n"))

    def fetch_keys(c, z, now, nxt, free):
        if now is not None:
            P.sp.dma(free, kd[z], Kc[0:rows, z, :], X.K[bass.ds(c, 1), bass.ds(now, 1)].rearrange("a h r n -> (a h r) n"))
            if X.softmax and not wide:
                mask_into([], kd[z], Kc[aux + n_m:total, z, :], c)
        if nxt is not None:
            src = X.K if X.split else X.Kb
            P.sp.dma(free, kn[z], Kn[0:rows, z, :], src[bass.ds(c, 1), bass.ds(nxt, 1)].rearrange("a h r n -> (a h r) n"))
            if not wide:
                mask_into([], kn[z], Kn[aux + n_m:total, z, :], c)
        if wide:
            mask_into(free, kn[z], Ka[2:4, z, :], c)
        P.name_if(f"keys{z}", kd[z].now())
        P.name_if(f"next{z}", kn[z].now())

    def fetch_values(c, z, now, R):
        free = [R["value_readers"].get(z), R["sum_readers"].get(z)]
        a = P.sp.dma(free, vd[z], Vc[:, z].rearrange("p j x -> p (j x)"), X.V[bass.ds(c, 1), bass.ds(now, 1)].rearrange("a h p x -> (a h p) x"))
        P.name_if(f"vals{z}", a)

    def arrived(z, label, sig):
        frame = P.frames[-1] if P.frames else None
        if frame is not None and sig.n == frame.base.get(sig, 0):
            return P.lags_of(f"{label}{z}")
        return [sig.now()]

    units = [(g, half) for g in range(TPC // G) for half in range(2)]

    def step(z, now, nxt, R, first):
        keys = arrived(z, "keys", kd[z]) if now is not None else []
        nexts = arrived(z, "next", kn[z]) if nxt is not None or wide else []

        def scores(t):
            b, slot = t % 2, z * TPC + t
            for half, sl in enumerate(halves()):
                m = P.pe([keys, nexts if wide else None, R["banks"].get(b), R["rows"].get(0)], nc.tensor.matmul, P.ps[:, 2 * b + half, :],
                         lhsT=Kc[:, z, t * 128:(t + 1) * 128], rhs=Qc[:, sl], start=True, stop=not wide)
                if wide:
                    m = P.pe([], nc.tensor.matmul, P.ps[:, 2 * b + half, :], lhsT=Ka[:, z, t * 128:(t + 1) * 128], rhs=Qa[:, sl], start=False, stop=True)
            e = P.act([m, R["probs"].get(slot), R["sums"].get(slot)], nc.scalar.activation, Pr[:, slot, :], P.ps[:, 2 * b:2 * b + 2, :].rearrange("p a n -> p (a n)"),
                      ACT.Exp if X.softmax else ACT.Sigmoid)
            R["banks"].put(b, [e])
            R["exps"].put(slot, [e])
            if own_sum:
                vals = arrived(z, "vals", vd[z])
                valid = Vc[:, z, t, d:dv]
                if first and t == 0:
                    s = P.dve([e, vals, R["sum_read"].get(0)], nc.vector.tensor_scalar, Ps[:], Pr[:, slot, :], valid, None, ALU.mult)
                else:
                    s = P.dve([e, vals, R["sum"].get(0)], nc.vector.scalar_tensor_tensor, Ps[:], Pr[:, slot, :], valid, Ps[:], ALU.mult, ALU.add)
                R["sums"].put(slot, [s])
                R["sum"].put(0, [s])
                R["sum_readers"].put(z, [s])

        def maxima(q):
            b = q % 2
            m = P.pe([nexts, R["nbanks"].get(b), R["next_query"].get(0)], nc.tensor.matmul, P.ps[:, 4 + b, :], lhsT=Qn[:, q * 128:(q + 1) * 128], rhs=Kn[:, z, :], start=True, stop=not wide)
            if wide:
                m = P.pe([], nc.tensor.matmul, P.ps[:, 4 + b, :], lhsT=Qa0[:, q * 128:(q + 1) * 128], rhs=Ka[:, z, :], start=False, stop=True)
            r = P.dve([m, R["reds"].get(z)], nc.vector.tensor_reduce, red[:, z, q:q + 1], P.ps[:, 4 + b, :], AX, ALU.max)
            R["nbanks"].put(b, [r])
            return r

        for t in range(TPC):
            if now is not None:
                scores(t)
            if nxt is not None:
                for q in range(2 * t, 2 * t + 2):
                    r = maxima(q)
            if now is not None and not first:
                for unit in units[t * len(units) // TPC:(t + 1) * len(units) // TPC]:
                    weigh(1 - z, unit, R)
        if nxt is not None:
            r = P.dve([r, R["mx"].get(0)], nc.vector.tensor_tensor, mx[:], mx[:], red[:, z, :], ALU.max)
            R["reds"].put(z, [r])
            R["mx"].put(0, [r])
        R["key_readers"].put(z, [P.pe.sig.now()])
        R["query_readers"].put(0, [P.pe.sig.now()])

    def weigh(z, unit, R):
        g, half = unit
        vals = arrived(z, "vals", vd[z])
        for n in range(G):
            t = g * G + n
            slot = z * TPC + t
            m = P.pe([R["exps"].get(slot), vals, R["accs"].get(half)], nc.tensor.matmul, P.ps[n * width:n * width + spread_v, 6 + half, :],
                     lhsT=Vc[:, z, t, 0:spread_v], rhs=Pr[:, slot, half * HALF:(half + 1) * HALF], start=False, stop=True, skip_group_check=True)
            R["probs"].put(slot, [m])
        R["value_readers"].put(z, [m])

    RINGS = {"banks": 2, "nbanks": 2, "probs": 2 * TPC, "sums": 2 * TPC, "exps": 2 * TPC, "reds": 2, "mx": 1, "mx_read": 1, "sum": 1,
             "sum_read": 1, "sum_stored": 1, "key_readers": 2, "value_readers": 2, "sum_readers": 2, "accs": 2, "rows": 1,
             "rows_read": 1, "next_query": 1, "query_readers": 1, "stored": 1}

    def rings():
        return {n: Ring(P, n, k) for n, k in RINGS.items()}

    assert CHUNKS % 2 == 1
    unroll = UNROLL if (CHUNKS - 1) % UNROLL == 0 else 2
    groups = (CHUNKS - 1) // unroll

    def run(now, nxt, R):
        if nxt is not None:
            R["mx"].put(0, [P.dve([R["mx"].get(0), R["mx_read"].get(0)], nc.vector.memset, mx[:], -3.0e38)])

        def one(c, z, first, more):
            if more:
                fetch_keys(c + 1, 1 - z, now, nxt, R["key_readers"].get(1 - z))
            step(z, now, nxt, R, first)
            if more and now is not None:
                fetch_values(c + 1, 1 - z, now, R)
        one(0, 1, True, True)
        if now is not None:
            for half in range(2):
                R["accs"].put(half, [P.pe([R["accs"].get(half)], nc.tensor.matmul, P.ps[:, 6 + half, :], lhsT=C.zero[0:1, 0:128],
                                          rhs=C.zero[0:1, :], start=True, stop=True, skip_group_check=True)])
        if groups > 1:
            P.meet_engines()
            for r in R.values():
                r.enter()
            with P.loop(groups - 1) as i:
                for k in range(unroll):
                    one(i * unroll + (1 + k), k % 2, False, True)
                for r in R.values():
                    r.close()
            for r in R.values():
                r.leave()
        for k in range(unroll):
            one(CHUNKS - unroll + k, k % 2, False, k < unroll - 1)

    def drain(R):
        for unit in units:
            weigh(1, unit, R)

    def take_off(R):
        r = P.dve([R["mx"].get(0), R["rows_read"].get(0)], nc.vector.tensor_scalar, mneg[:], mx[:], -1.0, None, ALU.mult)
        R["mx_read"].put(0, [r])
        free_banks = R["banks"].get(0)
        if n_m == 1:
            for q in range(TOK_TILES):
                t = P.pe([r, free_banks], nc.tensor.matmul, P.ps[aux:aux + 1, q // 4, (q % 4) * 128:(q % 4 + 1) * 128], lhsT=mneg[:, q:q + 1], rhs=C.ident[:], start=True, stop=True)
        else:
            a = P.dve([r], nc.vector.tensor_copy, mparts[:, 0, :], mneg[:])
            b = P.dve([a], nc.vector.tensor_tensor, mrest[:], mneg[:], mparts[:, 0, :], ALU.subtract)
            r = P.dve([b], nc.vector.tensor_copy, mparts[:, 1, :], mrest[:])
            base = 0 if wide else aux
            for q in range(TOK_TILES):
                t = P.pe([r, free_banks], nc.tensor.matmul, P.ps[base:base + 2, q // 4, (q % 4) * 128:(q % 4 + 1) * 128], lhsT=mparts[:, :, q], rhs=C.ident16[:], start=True, stop=True)
        R["rows_read"].put(0, [t])
        if wide:
            r = P.act([t], nc.scalar.copy, Qa[0:2, :], P.ps[0:2, 0:2, :].rearrange("p a n -> p (a n)"))
        else:
            r = P.act([t], nc.scalar.copy, Qc[aux:aux + n_m, :], P.ps[aux:aux + n_m, 0:2, :].rearrange("p a n -> p (a n)"))
        R["rows"].put(0, [r] + ([q_in.now()]))
        R["banks"].put(0, [r])

    def next_queries(head, R):
        src = X.Q if X.split else X.Qb
        a = P.sp.dma([R["query_readers"].get(0)], q_next, Qn[0:rows, :], src[bass.ds(head, 1)].rearrange("a r n -> (a r) n"))
        R["next_query"].put(0, [a])

    def these_queries(head, R):
        a = P.sp.dma([R["query_readers"].get(0)], q_in, Qc[0:rows, :], X.Q[bass.ds(head, 1)].rearrange("a r n -> (a r) n"))
        R["rows"].put(0, [a])

    def store(head, R):
        last = [R["probs"].get(n) for n in range(2 * TPC)]
        if own_sum:
            for half, sl in enumerate(halves()):
                t = P.pe([R["sum"].get(0), R["nbanks"].get(half)], nc.tensor.matmul, P.ps[0:1, 4 + half, :], lhsT=C.ones_col[:], rhs=Ps[:, sl], start=True, stop=True)
            r = P.act([t, R["sum_stored"].get(0)], nc.scalar.copy, Dc[:], P.ps[0:1, 4:6, :].rearrange("p a n -> p (a n)"))
            for half in range(2):
                R["nbanks"].put(half, [r])
            R["sum_read"].put(0, [t])
            R["sum_stored"].put(0, [P.sp.dma([r], sum_stored, X.den[bass.ds(head, 1), :], Dc[:])])
        r = P.act([last, R["stored"].get(0)], nc.scalar.copy, Oc[:], P.ps[:, 6:8, :].rearrange("p a n -> p (a n)"))
        for half in range(2):
            R["accs"].put(half, [r])
        R["stored"].put(0, [P.sp.dma([r], stored, X.O[bass.ds(head, 1)].rearrange("a p n -> (a p) n"), Oc[:])])

    R = rings()
    follow = lambda n: n if X.softmax and H > 1 else None
    if X.softmax:
        next_queries(0, R)
        fetch_keys(0, 1, None, 0, [])
        run(None, 0, R)
        P.barrier()
        take_off(rings())
    R = rings()
    these_queries(0, R)
    if follow(1):
        next_queries(1, R)
    fetch_keys(0, 1, 0, follow(1), [])
    fetch_values(0, 1, 0, R)
    P.barrier()
    if H == 1:
        R = rings()
        run(0, None, R)
        drain(R)
        store(0, R)
        P.barrier()
        return
    with P.loop(H) as head:
        R = rings()
        run(head, follow(head + 1), R)
        fetch_keys(0, 1, head + 1, follow(head + 2), R["key_readers"].get(1))
        these_queries(head + 1, R)
        if X.softmax:
            next_queries(head + 2, R)
        drain(R)
        fetch_values(0, 1, head + 1, R)
        store(head, R)
        if X.softmax:
            take_off(R)
        for r in R.values():
            r.close()
    P.barrier()


def cross_layer(P, C, io, X, stack, name, heads, d, split, softmax, masked, w, bias, out):
    nc = P.nc
    A = Cross(P, name, heads, d, split, softmax, masked)
    bk = io[bias[1]] if bias else None
    keys_and_values(P, C, io, A, io[w[1]], bk, io[w[2]])
    with ExitStack() as inner:
        h, tmp = tile(P, inner, "h", [D, S]), tile(P, inner, "tmp", [D, S])
        C.normed = normalize(P, C, [], X, h, tmp)
        queries(P, C, io, A, h, io[w[0]], io[bias[0]] if bias else None, tmp)
    with ExitStack() as inner:
        cross_heads(P, C, A, inner)
    bring_together(P, C, io, A, X, stack, bias, out)


def bring_together(P, C, io, A, X, stack, bias, out):
    nc = P.nc
    H, d, G = A.H, A.d, A.groups
    T, per_tile, width = H * d // 128, 128 // d, 128 // G
    U = tile(P, stack, "U", [128, G, T, S])
    bv = load(P, stack, "bv", io[bias[2]]) if bias else None
    wo = load(P, stack, "wo", io[out[0]].rearrange("(k p) n -> p k n", p=128), [128, T, D]) if out else None
    bo = load(P, stack, "bo", io[out[1]]) if out and out[1] else None
    if A.softmax:
        own_sum = d > 32
        n = 1 if own_sum else G
        sums = tile(P, stack, "sums", [H, n, S])
        for g in range(n):
            P.sp.dma(None, P.stream("sums"), sums[:, g, :], A.den if own_sum else A.O[:, g * width + d, :])
    loads = P.stream("heads")
    for t in range(T):
        for g in range(G):
            P.sp.dma(None, loads, U[:, g, t, :], A.O[t * per_tile:(t + 1) * per_tile, g * width:g * width + d, :])
    r = None
    if A.softmax:
        r = P.stream("sums").now()
        for g in range(1, n):
            r = P.dve([r], nc.vector.tensor_tensor, sums[:, 0, :], sums[:, 0, :], sums[:, g, :], ALU.add)
        r = P.dve([r], nc.vector.reciprocal, sums[:, 0, :], sums[:, 0, :])
        a = P.sp.dma([r], P.stream("sums"), A.den, sums[:, 0, :])
        over = tile(P, stack, "over", [128, T, S])
        for t in range(T):
            r = P.sp.dma([a], P.stream("sums"), over[:, t, :], A.den[t * per_tile:(t + 1) * per_tile].unsqueeze(1).to_broadcast([per_tile, d, S]))
    wts = P.stream("weights").now()
    done = []
    for t in range(T):
        m = loads.now()
        for g in range(1, G):
            m = P.dve([m], nc.vector.tensor_tensor, U[:, 0, t, :], U[:, 0, t, :], U[:, g, t, :], ALU.add)
        if A.softmax:
            m = P.dve([m, r], nc.vector.tensor_tensor, U[:, 0, t, :], U[:, 0, t, :], over[:, t, :], ALU.mult)
        if bv is not None:
            m = P.dve([m, wts], nc.vector.tensor_scalar, U[:, 0, t, :], U[:, 0, t, :], bv[:, t:t + 1], None, ALU.add)
        done.append(m)
    if out:
        linear(P, [done, wts], lambda k, m: wo[:, k, :], [U[:, 0, t, :] for t in range(T)], 1, add_to_x(P, X, bo[:, 0:1] if bo is not None else None))
    else:
        P.dve([done], nc.vector.tensor_tensor, X[:], X[:], U[:, 0, 0, :], ALU.add)


def cross_0(P, C, io, X, stack):
    cross_layer(P, C, io, X, stack, "L0", 16, 64, False, True, (io["mask_BxS2_bf1"], MASKED), ("L0_xattn_Wq", "L0_xattn_Wk", "L0_xattn_Wv"),
                ("L0_xattn_bq", "L0_xattn_bk", "L0_xattn_bv"), ("L0_xattn_Wo", "L0_xattn_bo"))


def cross_1(P, C, io, X, stack):
    cross_layer(P, C, io, X, stack, "L1", 1, 128, False, True, (None, MASKED), ("L1_xattn_Wq", "L1_xattn_Wk", "L1_xattn_Wv"), None, None)


def cross_2(P, C, io, X, stack):
    cross_layer(P, C, io, X, stack, "L2", 16, 8, True, False, None, ("L2_xattn_Wq", "L2_xattn_Wk", "L2_xattn_Wv"), None, ("L2_xattn_Wo", None))


def cross_3(P, C, io, X, stack):
    cross_layer(P, C, io, X, stack, "L3", 16, 8, True, True, (io["mask_Bx1x1xS2_ik0"], -1e9), ("L3_xattn_Wq", "L3_xattn_Wk", "L3_xattn_Wv"),
                ("L3_xattn_bq", "L3_xattn_bk", "L3_xattn_bv"), ("L3_xattn_Wo", "L3_xattn_bo"))


def build(nc, io, counts, layers):
    global CHUNKS, N_KEYS
    N_KEYS = io["ones_keys"].shape[0]
    CHUNKS = io["ctx_1024"].shape[1] // CHUNK
    with ExitStack() as ctx:
        P = Prog(nc, ctx, counts)

        class C:
            pass
        C.mean = tile(P, ctx, "mean", [128, 128])
        C.eps = tile(P, ctx, "eps", [128, 1])
        C.one_eps = tile(P, ctx, "one_eps", [128, 1])
        C.ident = tile(P, ctx, "ident", [128, 128])
        C.zero = tile(P, ctx, "zero", [128, HALF])
        C.ones, C.ones_col = tile(P, ctx, "ones", [1, 128]), tile(P, ctx, "ones_col", [128, 1])
        C.ones16, C.ident16 = tile(P, ctx, "ones16", [128, 16]), tile(P, ctx, "ident16", [128, 128], BF16)
        P.dve([], nc.vector.memset, C.ones16[:], 1.0)
        P.io_ones = io["ones_keys"]
        C.causal, C.below = tile(P, ctx, "causal", [128, 128]), tile(P, ctx, "below", [128, 128])
        X = tile(P, ctx, "X", [D, S])
        P.sp.dma(None, P.stream("x"), X[:], io["x"])
        P.dve([], nc.vector.memset, C.mean[:], 1.0 / D)
        P.dve([], nc.vector.memset, C.eps[:], LN_EPS)
        P.dve([], nc.vector.memset, C.one_eps[:], 1.0 + 1e-6)
        P.dve([], nc.vector.memset, C.zero[:], 0.0)
        z = P.pool([], nc.gpsimd.memset, C.ident[:], 0.0)
        P.pool([z], nc.gpsimd.affine_select, out=C.ident[:], in_=C.ident[:], compare_op=ALU.not_equal, fill=1.0,
               base=0, pattern=[[-1, 128]], channel_multiplier=1)
        P.dve([], nc.vector.memset, C.ones[:], 1.0)
        P.dve([], nc.vector.memset, C.ones_col[:], 1.0)
        z = P.pool([], nc.gpsimd.memset, C.causal[:], 1.0)
        P.pool([z], nc.gpsimd.affine_select, out=C.causal[:], in_=C.causal[:], compare_op=ALU.is_ge, fill=0.0,
               base=0, pattern=[[1, 128]], channel_multiplier=-1)
        z = P.pool([], nc.gpsimd.memset, C.below[:], 0.0)
        P.pool([z], nc.gpsimd.affine_select, out=C.below[:], in_=C.below[:], compare_op=ALU.is_ge, fill=MASKED,
               base=0, pattern=[[-1, 128]], channel_multiplier=1)
        P.barrier()
        P.dve([], nc.vector.tensor_copy, C.ident16[:], C.ident[:])
        P.barrier()
        for n in layers:
            with ExitStack() as stack:
                PARTS[n](P, C, io, X, stack)
                P.barrier()
        P.sp.dma(None, P.stream("out"), io["out"], X[:])
        P.barrier()


PARTS = {2: ffn_ternary_gated, 5: ffn_ternary_gelu, 6: recurrent_block, 11: ffn_experts,
         0: causal_attention, 1: cross_0, 4: cross_1, 7: cross_2, 10: cross_3, 3: cosformer, 8: attention_of_experts, 9: retention}



TRANSPOSED = {"L0_ffn_w1_w", "L0_ffn_w2_w", "L0_ffn_h1_w", "L0_ffn_h2_w", "L0_ffn_w3_w", "L1_ffn_W1", "L1_ffn_W2",
              "L2_attn_W_in", "L2_attn_W_gate", "L2_attn_W_out", "L2_attn_rg_in_w", "L2_attn_rg_gate_w",
              "L2_attn_mlp_gate_w", "L2_attn_mlp_up_w", "L2_attn_mlp_down_w",
              "L0_attn_W_Q", "L0_attn_W_K", "L0_attn_W_V", "L0_attn_W_O",
              "L2_xattn_Wq", "L2_xattn_Wk", "L2_xattn_Wv", "L2_xattn_Wo",
              "L3_xattn_Wq", "L3_xattn_Wk", "L3_xattn_Wv", "L3_xattn_Wo"}


def kernel(**inputs):
    import concourse.bacc as bacc
    from concourse.bass_utils import run_bass_kernel_spmd

    arrays = {}
    for name, a in inputs.items():
        a = np.asarray(a)
        if name in TRANSPOSED:
            a = a.T
        if name == "x":
            a = a[0].T
        if name == "ctx_1024":
            n_keys = a.shape[1]
            padded = -(-n_keys // CHUNK) * CHUNK
            a = np.pad(a[0], ((0, padded - n_keys), (0, 0))).T
        if name.startswith("mask"):
            a = a.reshape(-1)
        if a.ndim == 1 and not name.startswith("mask"):
            a = a.reshape(-1, 96 if a.size == 192 else min(128, a.size)).T
        if a.dtype == np.bool_:
            a = a.view(np.uint8)
        arrays[name] = np.ascontiguousarray(a)
    arrays.update(layout(inputs))
    arrays["ones_keys"] = np.ones(n_keys, np.int32)
    valid = (np.arange(padded) < n_keys).astype(np.float32)
    arrays["valid_keys"] = np.ascontiguousarray(valid.reshape(-1, 128).T)

    def program(counts):
        nc = bacc.Bacc("TRN2", target_bir_lowering=False, num_devices=1)
        io = {n: nc.dram_tensor(n + "_dram", a.shape, mybir.dt.from_np(a.dtype), kind="ExternalInput").ap()
              for n, a in arrays.items()}
        io["out"] = nc.dram_tensor("out_dram", (D, S), F32, kind="ExternalOutput").ap()
        build(nc, io, counts, LAYERS)
        return nc

    counts = {}
    program(counts)
    nc = program(counts)
    r = run_bass_kernel_spmd(nc, [{n + "_dram": a for n, a in arrays.items()}], core_ids=[0])
    return np.ascontiguousarray(r.results[0]["out_dram"].T)[None]


def exchanged(a):
    return a.reshape(a.shape[0], -1, 2)[:, :, ::-1].reshape(a.shape)


def block_diagonal(w):
    h, d, _ = w.shape
    out = np.zeros((h * d, h * d), w.dtype)
    for n in range(h):
        out[n * d:(n + 1) * d, n * d:(n + 1) * d] = w[n]
    return out


def tables():
    pos = np.arange(S, dtype=np.float64)
    out = {}

    def table(d, cos, sin, factor):
        c = np.repeat(cos, 2, axis=1).T
        s = np.stack([-sin, sin], axis=2).reshape(S, d).T
        n = D // d
        return [np.ascontiguousarray((np.tile(t, (n, 1)) * factor).astype(np.float32)) for t in (c, s)]

    d = D // 16
    inv = 10000.0 ** (-2.0 * np.arange(d // 2) / d)
    ang = (np.float32(1) * pos[:, None].astype(np.float32) * inv.astype(np.float32)).astype(np.float64)
    out["rope_q_cos"], out["rope_q_sin"] = table(d, np.cos(ang), np.sin(ang), 1.0 / math.sqrt(d))
    out["rope_k_cos"], out["rope_k_sin"] = table(d, np.cos(ang), np.sin(ang), 1.0)

    H, d = 8, 16
    gamma = (1.0 - np.exp(np.linspace(math.log(1.0 / 32.0), math.log(1.0 / 512.0), H))).astype(np.float32).astype(np.float64)
    scale = (np.arange(0, d, 2) + 0.4 * d) / (1.4 * d)
    sc = scale[None, :] ** (pos / 512.0)[:, None]
    inv = (1.0 / 10000.0 ** (np.arange(d // 2) / (d // 2))).astype(np.float32)
    ang = (pos[:, None].astype(np.float32) * inv).astype(np.float64)
    decay = np.repeat(gamma[:, None] ** pos[None, :], d, axis=0)
    out["retention_q_cos"], out["retention_q_sin"] = table(d, np.cos(ang) * sc, np.sin(ang) * sc, decay)
    out["retention_k_cos"], out["retention_k_sin"] = table(d, np.cos(ang) / sc, np.sin(ang) / sc, 1.0 / decay)

    ang = (np.float32(math.pi / (2.0 * S)) * pos.astype(np.float32)).astype(np.float64)
    out["cosformer_table"] = np.repeat(np.stack([np.cos(ang), np.sin(ang)]), 64, axis=0).astype(np.float32)
    return out


def layout(inputs):
    out = tables()
    get = lambda n: np.asarray(inputs[n])
    for x in ("Q", "K"):
        out[f"L0_attn_W_{x}_turned"] = exchanged(get(f"L0_attn_W_{x}").T)
        out[f"L3_attn_W_{x}"] = block_diagonal(get(f"L3_attn_W_{x}"))
        out[f"L3_attn_W_{x}_turned"] = exchanged(out[f"L3_attn_W_{x}"])
    out["L3_attn_W_V"] = block_diagonal(get("L3_attn_W_V"))
    heads = lambda n: np.tile(get(n).reshape(16, 64).T, (2, 1))
    out["L1_attn_bqk_twice"] = np.stack([heads("L1_attn_bq"), heads("L1_attn_bk")], axis=2).transpose(1, 0, 2)
    for n in ("L1_attn_bv", "L0_xattn_bv", "L3_xattn_bv", "L2_ffn_gates"):
        out[n + "_row"] = get(n)[None]
    out["L1_xattn_Wk"], out["L1_xattn_Wv"] = np.split(get("L1_xattn_Wkv"), 2, axis=1)
    return {n: np.ascontiguousarray(a) for n, a in out.items()}
```

```python
from contextlib import ExitStack, contextmanager
import math

import numpy as np

import concourse.bass as bass
from concourse import mybir

F32 = mybir.dt.float32
BF16 = mybir.dt.bfloat16
I32 = mybir.dt.int32
U32 = mybir.dt.uint32
U8 = mybir.dt.uint8
ALU = mybir.AluOpType
ACT = mybir.ActivationFunctionType
AX = mybir.AxisListType.X

D = 128
S = 1024
HALF = 512
TOK_TILES = S // 128
CHUNK = 512
TPC = CHUNK // 128
LN_EPS = 1e-5
MASKED = -1e15
START = 512
LAYERS = list(range(12))
UNROLL = 4


class Signal:

    def __init__(self, prog, name):
        self.prog, self.sem, self.n = prog, prog.ctx.enter_context(prog.nc.semaphore(name)), 0
        prog.counted.append(self)

    def now(self):
        return Mark(self, self.n, list(self.prog.frames))

    def count(self, instruction, by=1):
        instruction.then_inc(self.sem, by)
        self.n += by
        return self.now()


class Mark:

    def __init__(self, sig, n, frames):
        self.sig, self.n, self.frames = sig, n, frames

    def key(self):
        return len(self.frames), self.n

    def value(self, engine):
        loops = [f for f in self.frames if f.per.get(self.sig, 0)]
        if not loops:
            return self.n
        here = engine.prog.frames[-1]
        key = (engine, self.sig, len(loops))
        if key not in here.added:
            added = 0
            for f in loops:
                added = f.reg * f.per[self.sig] + added
            here.added[key] = engine.e.snap(added)
        return here.added[key] + self.n


class Ring:

    def __init__(self, prog, label, n):
        self.prog, self.label, self.n, self.marks = prog, label, n, {}

    def get(self, slot):
        if slot in self.marks:
            return self.marks[slot]
        if not self.prog.frames:
            return []
        return self.prog.lags(f"{self.label}{slot}")

    def put(self, slot, marks):
        self.marks[slot] = marks

    def enter(self):
        self.outside, self.marks = self.marks, {}

    def leave(self):
        inside = {slot: self.prog.lasts(f"{self.label}{slot}") for slot in range(self.n)}
        self.marks = {**self.outside, **{slot: marks for slot, marks in inside.items() if marks}}

    def close(self):
        for slot, marks in self.marks.items():
            for k, m in enumerate(marks):
                self.prog.name(f"{self.label}{slot}.{k}", m)


class Frame:

    def __init__(self, reg, per, base):
        self.reg, self.per, self.base, self.names, self.added = reg, per, base, {}, {}


class Engine:
    def __init__(self, prog, e, name):
        self.prog, self.e, self.sig, self.waited = prog, e, Signal(prog, name), {}

    def wait(self, *marks):
        need = {}

        def gather(m):
            if isinstance(m, Mark):
                have = need.get(m.sig)
                if have is None or m.key() > have.key():
                    need[m.sig] = m
            elif m is not None:
                for x in m:
                    gather(x)
        gather(marks)
        for sig, m in need.items():
            if (m.n <= START and not m.frames) or self.waited.get(sig, (0, 0)) >= m.key():
                continue
            self.waited[sig] = m.key()
            v = m.value(self)
            assert m.n > 0
            self.e.wait_ge(sig.sem, v)
            if self is self.prog.sp and not isinstance(v, int):
                self.prog.settle(self)

    def __call__(self, marks, op, *a, **k):
        self.wait(marks)
        return self.sig.count(op(*a, **k))

    def dma(self, marks, sig, out, in_):
        self.wait(marks)
        return sig.count(self.e.dma_start(out, in_), 16)


class Prog:
    def __init__(self, nc, ctx, counts):
        self.nc, self.ctx, self.counts, self.seen = nc, ctx, counts, []
        self.frames, self.counted, self.tiles = [], [], 0
        self.pe = Engine(self, nc.tensor, "pe_done")
        self.act = Engine(self, nc.scalar, "act_done")
        self.dve = Engine(self, nc.vector, "dve_done")
        self.pool = Engine(self, nc.gpsimd, "pool_done")
        self.sp = Engine(self, nc.sync, "sp_done")
        self.engines = (self.pe, self.act, self.dve, self.pool, self.sp)
        self.ps = ctx.enter_context(nc.psum_tensor("ps", [128, 8, HALF], F32))
        self.free = [None] * 8
        self.turn = 0
        self.banks = list(range(8))
        self.loads = {}
        for e in self.engines:
            e.e.sem_inc(e.sig.sem, START)
            e.sig.n = START
        self.barrier()

    def stream(self, name):
        if name not in self.loads:
            assert not self.frames
            sig = self.loads[name] = Signal(self, name)
            self.sp.e.sem_inc(sig.sem, START)
            sig.n = START
        return self.loads[name]

    def barrier(self):
        for e in self.engines:
            if e is not self.sp:
                e.wait(e.sig.now())
        for sig in self.loads.values():
            self.sp.wait(sig.now())
        self.nc.all_engine_barrier()
        for e in self.engines:
            for sig in self.counted:
                e.waited[sig] = (len(self.frames), sig.n)
        self.free = [None] * 8

    def settle(self, e):
        e.e.sem_inc(e.sig.sem, 1)
        e.sig.n += 1

    def meet_engines(self):
        marks = [e.sig.now() for e in self.engines]
        for e in self.engines:
            e.wait(marks)
            if e is not self.sp:
                self.settle(e)

    def name_if(self, label, mark):
        if self.frames:
            self.name(label, mark)

    def lags_of(self, label):
        return [self.lag(label)] if label in self.frames[-1].known else []

    @contextmanager
    def loop(self, count):
        key = len(self.seen)
        self.seen.append(None)
        known = self.counts.get(key)
        with self.nc.Fori(0, count) as reg:
            per = {s: known[0][n] for n, s in enumerate(self.counted)} if known else {}
            f = Frame(reg, per, {s: s.n for s in self.counted})
            f.known = known[1] if known else {}
            self.frames.append(f)
            for e in self.engines:
                e.waited = {}
            yield reg
            self.frames.pop()
            grown = [s.n - f.base.get(s, 0) for s in self.counted]
        self.counts[key] = (grown, f.names)
        self.ended = f, grown, count
        for s, g in zip(self.counted, grown):
            s.n = f.base.get(s, 0) + g * count
        for e in self.engines:
            e.waited = {}

    def name(self, label, mark):
        f = self.frames[-1]
        f.names[label] = (self.counted.index(mark.sig), mark.n - f.base.get(mark.sig, 0))
        return mark

    def lag(self, label):
        f = self.frames[-1]
        index, off = f.known.get(label, (0, 0))
        sig = self.counted[index]
        per = f.per.get(sig, 0)
        return Mark(sig, f.base.get(sig, 0) + off - per, list(self.frames))

    def lags(self, label):
        names = [n for n in self.frames[-1].known if n.rsplit(".", 1)[0] == label]
        return [self.lag(n) for n in names]

    def lasts(self, label):
        f, grown, count = self.ended
        marks = []
        for n, (index, off) in f.names.items():
            if n.rsplit(".", 1)[0] == label:
                sig = self.counted[index]
                marks.append(Mark(sig, f.base.get(sig, 0) + off + grown[index] * (count - 1), list(self.frames)))
        return marks

    def bank(self):
        b = self.banks[self.turn % len(self.banks)]
        self.turn += 1
        self.pe.wait(self.free[b])
        return b



def halves():
    return [slice(h * HALF, (h + 1) * HALF) for h in range(S // HALF)]


def load(P, stack, name, src, shape=None, dt=F32, dst=None):
    shape = list(shape or src.shape)
    t = tile(P, stack, name, shape, dt)
    P.sp.dma(None, P.stream("weights"), t[:] if dst is None else dst(t), src)
    return t


def tile(P, stack, name, shape, dt=F32):
    P.tiles += 1
    return stack.enter_context(P.nc.sbuf_tensor(f"{name}_{P.tiles}", list(shape), dt))


def linear(P, marks, weights, inputs, n_out, evacuate, width=None):
    out = []
    cols = [slice(0, width)] if width else halves()
    for m in range(n_out):
        for h, sl in enumerate(cols):
            b = P.bank()
            n = len(inputs)
            for k in range(n):
                w = weights(k, m)
                ps = P.ps[0:w.shape[-1], b, 0:sl.stop - sl.start]
                mark = P.pe(marks, P.nc.tensor.matmul, ps, lhsT=w, rhs=inputs[k][:, sl], start=k == 0, stop=k == n - 1)
            P.free[b] = evacuate(m, sl, ps, mark)
            out.append(P.free[b])
    return out


def normalize(P, C, marks, src, dst, tmp, center=True, weight=None):
    nc = P.nc
    done = []
    for sl in halves():
        base = src
        m = marks
        if center:
            b = P.bank()
            t = P.pe(marks, nc.tensor.matmul, P.ps[:, b, :], lhsT=C.mean[:], rhs=src[:, sl], start=True, stop=True)
            m = P.dve([t, marks], nc.vector.tensor_tensor, dst[:, sl], src[:, sl], P.ps[:, b, :], ALU.subtract)
            P.free[b] = m
            base = dst
        q = P.act([m, marks], nc.scalar.activation, tmp[:, sl], base[:, sl], ACT.Square)
        b = P.bank()
        t = P.pe([q], nc.tensor.matmul, P.ps[:, b, :], lhsT=C.mean[:], rhs=tmp[:, sl], start=True, stop=True)
        r = P.act([t], nc.scalar.activation, tmp[:, sl], P.ps[:, b, :], ACT.Sqrt, bias=C.eps[:, 0:1])
        P.free[b] = r
        r = P.dve([r], nc.vector.reciprocal, tmp[:, sl], tmp[:, sl])
        if weight is None:
            r = P.dve([r], nc.vector.tensor_tensor, dst[:, sl], base[:, sl], tmp[:, sl], ALU.mult)
        else:
            r = P.dve([r], nc.vector.scalar_tensor_tensor, dst[:, sl], base[:, sl], weight, tmp[:, sl], ALU.mult, ALU.mult)
        done.append(r)
    return done


def add_to_x(P, X, bias=None):
    def evacuate(m, sl, ps, mark):
        if bias is None:
            return P.dve([mark], P.nc.vector.tensor_tensor, X[:, sl], X[:, sl], ps, ALU.add)
        return P.dve([mark], P.nc.vector.scalar_tensor_tensor, X[:, sl], ps, bias, X[:, sl], ALU.add, ALU.add)
    return evacuate


def ffn_ternary_gated(P, C, io, X, stack):
    nc = P.nc
    F = io["L0_ffn_w1_w"].shape[1]
    T = F // 128
    w1, w2 = (load(P, stack, n, io[n]) for n in ("L0_ffn_w1_w", "L0_ffn_w2_w"))
    h1, h2 = (load(P, stack, n, io[n].rearrange("(k p) n -> p k n", p=128), [128, T, F])
              for n in ("L0_ffn_h1_w", "L0_ffn_h2_w"))
    w3 = load(P, stack, "w3", io["L0_ffn_w3_w"].rearrange("(k p) n -> p k n", p=128), [128, T, D])
    s1, s2, t1, t2 = (load(P, stack, n, io[n])
                      for n in ("L0_ffn_w1_s", "L0_ffn_w2_s", "L0_ffn_h1_s", "L0_ffn_h2_s"))
    s3 = load(P, stack, "s3", io["L0_ffn_w3_s"])
    wts = P.stream("weights").now()
    h, tmp = tile(P, stack, "h", [D, S]), tile(P, stack, "tmp", [D, S])
    a, b = tile(P, stack, "a", [128, T, S]), tile(P, stack, "b", [128, T, S])
    n = normalize(P, C, [], X, h, tmp)
    gates = linear(P, [n, wts], lambda k, m: w1[:, m * 128:(m + 1) * 128], [h], T, lambda m, sl, ps, t: P.act(
        [t], nc.scalar.activation, a[:, m, sl], ps, ACT.Silu, scale=s1[:, m:m + 1]))
    up = linear(P, [], lambda k, m: w2[:, m * 128:(m + 1) * 128], [h], T, lambda m, sl, ps, t: P.dve(
        [t, gates], nc.vector.scalar_tensor_tensor, a[:, m, sl], ps, s2[:, m:m + 1], a[:, m, sl], ALU.mult, ALU.mult))
    one = linear(P, [up], lambda k, m: h1[:, k, m * 128:(m + 1) * 128], [a[:, k, :] for k in range(T)], T,
                 lambda m, sl, ps, t: P.act([t], nc.scalar.activation, b[:, m, sl], ps, ACT.Gelu, scale=t1[:, m:m + 1]))
    two = linear(P, [one], lambda k, m: h2[:, k, m * 128:(m + 1) * 128], [b[:, k, :] for k in range(T)], T,
                 lambda m, sl, ps, t: P.act([t], nc.scalar.activation, a[:, m, sl], ps, ACT.Gelu, scale=t2[:, m:m + 1]))
    linear(P, [two], lambda k, m: w3[:, k, :], [a[:, k, :] for k in range(T)], 1, lambda m, sl, ps, t: P.dve(
        [t], nc.vector.scalar_tensor_tensor, X[:, sl], ps, s3[:, 0:1], X[:, sl], ALU.mult, ALU.add))


def ternary(P, C, marks, w, work, stack, name):
    nc = P.nc
    n = w.shape[-1]
    s = tile(P, stack, name, [128, 4])
    r = P.dve([marks], nc.vector.tensor_reduce, s[:, 0:1], w, AX, ALU.add, apply_absolute_value=True)
    b = P.bank()
    t = P.pe([r], nc.tensor.matmul, P.ps[:, b, 0:1], lhsT=C.mean[:], rhs=s[:, 0:1], start=True, stop=True)
    r = P.dve([t], nc.vector.tensor_scalar, s[:, 1:2], P.ps[:, b, 0:1], 1.0 / n, 1e-8, ALU.mult, ALU.max)
    P.free[b] = r
    r1 = P.dve([r], nc.vector.tensor_scalar, s[:, 2:3], s[:, 1:2], 0.5, None, ALU.mult)
    r2 = P.dve([r], nc.vector.tensor_scalar, s[:, 3:4], s[:, 1:2], -0.5, None, ALU.mult)
    r = P.dve([r1, r2], nc.vector.tensor_scalar, work, w, s[:, 3:4], None, ALU.is_lt)
    r = P.dve([r], nc.vector.scalar_tensor_tensor, work, w, s[:, 2:3], work, ALU.is_gt, ALU.subtract)
    r = P.dve([r], nc.vector.tensor_tensor, work, work, w, ALU.subtract)
    return P.dve([r], nc.vector.tensor_tensor, w, w, work, ALU.add)


def ffn_ternary_gelu(P, C, io, X, stack):
    nc = P.nc
    F = io["L1_ffn_W1"].shape[1]
    T = F // 128
    w1 = load(P, stack, "w1", io["L1_ffn_W1"])
    w2 = load(P, stack, "w2", io["L1_ffn_W2"].rearrange("(k p) n -> p k n", p=128), [128, T, D])
    b1 = load(P, stack, "b1", io["L1_ffn_b1"])
    b2 = load(P, stack, "b2", io["L1_ffn_b2"])
    wts = P.stream("weights").now()
    h, tmp = tile(P, stack, "h", [D, S]), tile(P, stack, "tmp", [D, S])
    work, a = tile(P, stack, "work", [128, F]), tile(P, stack, "a", [128, T, S])
    flat2 = w2[:].rearrange("p k n -> p (k n)")
    m1 = ternary(P, C, [wts], w1[:], work[:], stack, "scale1")
    m2 = ternary(P, C, [wts, m1], flat2, work[:], stack, "scale2")
    n = normalize(P, C, [], X, h, tmp)
    hid = linear(P, [n, m1], lambda k, m: w1[:, m * 128:(m + 1) * 128], [h], T, lambda m, sl, ps, t: P.act(
        [t], nc.scalar.activation, a[:, m, sl], ps, ACT.Gelu, bias=b1[:, m:m + 1]))
    linear(P, [hid, m2], lambda k, m: w2[:, k, :], [a[:, k, :] for k in range(T)], 1, add_to_x(P, X, b2[:, 0:1]))


def recurrent_block(P, C, io, X, stack):
    nc = P.nc
    HID = io["L2_attn_W_in"].shape[1]
    R, T = HID // 2, 2
    K = io["L2_attn_conv_w"].shape[-1]
    col = lambda n: load(P, stack, n, io[n])
    w_in, w_gate, m_gate, m_up = (load(P, stack, n, io["L2_attn_" + n]) for n in ("W_in", "W_gate", "mlp_gate_w", "mlp_up_w"))
    rg_in, rg_gate, w_out, m_down = (load(P, stack, n, io["L2_attn_" + n].rearrange("(t p) n -> p t n", p=R),
                                          [R, T, io["L2_attn_" + n].shape[1]]) for n in ("rg_in_w", "rg_gate_w", "W_out", "mlp_down_w"))
    conv_w = load(P, stack, "conv_w", io["L2_attn_conv_w"].rearrange("(t p) a k -> p t (a k)", p=R), [R, T, K])
    conv_b, in_b, gate_b, lam = (col("L2_attn_" + n) for n in ("conv_b", "rg_in_b", "rg_gate_b", "forget_lambda"))
    n1, n2 = (load(P, stack, n, io["L2_attn_" + n]) for n in ("norm1_w", "norm2_w"))
    wts = P.stream("weights").now()
    x, h, tmp = (tile(P, stack, n, [D, S]) for n in ("x", "h", "tmp"))
    u_pad = tile(P, stack, "u_pad", [R, T, K - 1 + S])
    gate, u, ig, rg, t1 = (tile(P, stack, n, [R, T, S]) for n in ("gate", "u", "ig", "rg", "t1"))
    c = tile(P, stack, "c", [R, 2, T])
    r = P.act([wts], nc.scalar.activation, c[:, 0, :], lam[:], ACT.Abs)
    r = P.act([r], nc.scalar.activation, c[:, 0, :], c[:, 0, :], ACT.Exp, scale=-1.0)
    r = P.act([r], nc.scalar.activation, c[:, 0, :], c[:, 0, :], ACT.Ln, bias=1.0)
    r = P.dve([r, wts], nc.vector.scalar_tensor_tensor, c[:, 1, :], lam[:], 0.0, c[:, 0, :], ALU.max, ALU.add)
    decay = P.dve([r], nc.vector.tensor_scalar, c[:, 1, :], c[:, 1, :], -8.0, None, ALU.mult)
    zero = P.dve([], nc.vector.memset, u_pad[:, :, 0:K - 1], 0.0)

    n = normalize(P, C, [], X, x, tmp)
    n = normalize(P, C, [n, wts], x, h, tmp, center=False, weight=n1[:, 0:1])
    tiles = lambda w: (lambda k, m: w[:, m * R:(m + 1) * R])
    deep = lambda w: (lambda k, m: w[:, k, m * R:(m + 1) * R])
    gates = linear(P, [n], tiles(w_gate), [h], T, lambda m, sl, ps, t: P.act([t], nc.scalar.activation, gate[:, m, sl], ps, ACT.Gelu))
    us = linear(P, [n], tiles(w_in), [h], T, lambda m, sl, ps, t: P.act(
        [t], nc.scalar.copy, u_pad[:, m, K - 1 + sl.start:K - 1 + sl.stop], ps))
    conv = []
    for m in range(T):
        r = P.dve([us, zero], nc.vector.tensor_scalar, u[:, m, :], u_pad[:, m, 0:S], conv_w[:, m, 0:1], conv_b[:, m:m + 1], ALU.mult, ALU.add)
        for k in range(1, K):
            r = P.dve([r], nc.vector.scalar_tensor_tensor, u[:, m, :], u_pad[:, m, k:k + S], conv_w[:, m, k:k + 1], u[:, m, :], ALU.mult, ALU.add)
        conv.append(r)
    us = [u[:, k, :] for k in range(T)]
    igs = linear(P, [conv], deep(rg_in), us, T, lambda m, sl, ps, t: P.act([t], nc.scalar.activation, ig[:, m, sl], ps, ACT.Sigmoid, bias=in_b[:, m:m + 1]))
    rgs = linear(P, [conv], deep(rg_gate), us, T, lambda m, sl, ps, t: P.act([t], nc.scalar.activation, rg[:, m, sl], ps, ACT.Sigmoid, bias=gate_b[:, m:m + 1]))
    recs = []
    for m in range(T):
        a = P.act([rgs, decay], nc.scalar.activation, rg[:, m, :], rg[:, m, :], ACT.Exp, scale=c[:, 1, m:m + 1])
        b = P.act([a], nc.scalar.activation, t1[:, m, :], rg[:, m, :], ACT.Square)
        b = P.act([b], nc.scalar.activation, t1[:, m, :], t1[:, m, :], ACT.Sqrt, scale=-1.0, bias=C.one_eps[0:R, 0:1])
        b = P.dve([b, igs], nc.vector.tensor_tensor, t1[:, m, :], t1[:, m, :], ig[:, m, :], ALU.mult)
        b = P.dve([b], nc.vector.tensor_tensor, t1[:, m, :], t1[:, m, :], u[:, m, :], ALU.mult)
        b = P.dve([a, b], nc.vector.tensor_tensor_scan, ig[:, m, :], rg[:, m, :], t1[:, m, :], 0.0, ALU.mult, ALU.add)
        recs.append(P.dve([b, gates], nc.vector.tensor_tensor, ig[:, m, :], ig[:, m, :], gate[:, m, :], ALU.mult))
    mix = linear(P, [recs], lambda k, m: w_out[:, k, :], [ig[:, k, :] for k in range(T)], 1, add_to_x(P, x))
    n = normalize(P, C, [mix], x, h, tmp, center=False, weight=n2[:, 0:1])
    gs = linear(P, [n], tiles(m_gate), [h], T, lambda m, sl, ps, t: P.act([t], nc.scalar.activation, gate[:, m, sl], ps, ACT.Gelu))
    gs = linear(P, [n], tiles(m_up), [h], T, lambda m, sl, ps, t: P.dve([t, gs], nc.vector.tensor_tensor, gate[:, m, sl], ps, gate[:, m, sl], ALU.mult))
    outs = linear(P, [gs], lambda k, m: m_down[:, k, :], [gate[:, k, :] for k in range(T)], 1, add_to_x(P, x))
    for sl in halves():
        P.dve([outs], nc.vector.tensor_tensor, X[:, sl], X[:, sl], x[:, sl], ALU.add)


def transpose_back(P, C, marks, src, dst, parts):
    nc = P.nc
    out = []
    for h, sl in enumerate(halves()):
        b = P.bank()
        for j in range(4):
            t = P.pe(marks, nc.tensor.transpose, P.ps[0:parts, b, j * 128:(j + 1) * 128], src[:, 4 * h + j, :], C.ident[:])
        P.free[b] = P.act([t], nc.scalar.copy, dst[:, sl], P.ps[0:parts, b, :])
        out.append(P.free[b])
    return out


def one_hot_rows(P, C, marks, rows, n, sel):
    z = P.pool(marks, P.nc.gpsimd.memset, sel[:], 0.0)
    return P.pool([z], P.nc.gpsimd.affine_select, out=sel[:], in_=sel[:], compare_op=ALU.not_equal, fill=1.0, base=0,
                  pattern=[[-1, n], [0, 128]], channel_multiplier=1)


def ffn_experts(P, C, io, X, stack):
    nc = P.nc
    E, F = io["L3_ffn_experts_w1"].shape[0], io["L3_ffn_experts_w1"].shape[2]
    T = F // 128
    gate = load(P, stack, "gate", io["L3_ffn_gate"])
    w1, w3 = (tile(P, stack, n, [128, 2, F]) for n in ("w1", "w3"))
    w2 = tile(P, stack, "w2", [128, 2, T, D])
    wts = P.stream("weights").now()
    h, tmp, acc = (tile(P, stack, n, [D, S]) for n in ("h", "tmp", "acc"))
    a = tile(P, stack, "a", [128, T, S])
    logits, w, hot = (tile(P, stack, n, [128, TOK_TILES, E]) for n in ("logits", "w", "hot"))
    top, both = tile(P, stack, "top", [128, TOK_TILES, 8]), tile(P, stack, "both", [128, TOK_TILES, 2])
    which, whichf = tile(P, stack, "which", [128, TOK_TILES, 8], U32), tile(P, stack, "whichf", [128, TOK_TILES, 8])
    number = tile(P, stack, "number", [128, E])
    wT, wB = tile(P, stack, "wT", [E, S]), tile(P, stack, "wB", [128, E, S])
    sel = tile(P, stack, "sel", [E, E, 128])
    sels = one_hot_rows(P, C, [], None, E, sel)
    iot = P.pool([], nc.gpsimd.iota, number[:], [[1, E]], 0, 0, allow_small_or_imprecise_dtypes=True)
    loads = [P.stream("expert0"), P.stream("expert1")]

    def fetch(e, marks):
        for t, n in ((w1, "w1"), (w3, "w3")):
            P.sp.dma(marks, loads[e % 2], t[:, e % 2, :], io["L3_ffn_experts_" + n][e])
        return P.sp.dma(marks, loads[e % 2], w2[:, e % 2], io["L3_ffn_experts_w2"][e].rearrange("(k p) n -> p k n", p=128))

    here = [fetch(0, []), fetch(1, [])]
    n = normalize(P, C, [], X, h, tmp)
    b = P.bank()
    for j in range(TOK_TILES):
        t = P.pe([n, wts], nc.tensor.matmul, P.ps[:, b, j * E:(j + 1) * E], lhsT=h[:, j * 128:(j + 1) * 128], rhs=gate[:], start=True, stop=True)
    r = P.dve([t], nc.vector.tensor_copy, logits[:], P.ps[:, b, 0:TOK_TILES * E].rearrange("p (j e) -> p j e", e=E))
    P.free[b] = r
    for j in range(TOK_TILES):
        m = P.dve([r], nc.vector.max, top[:, j, :], logits[:, j, :])
        m = P.dve([m], nc.vector.max_index, which[:, j, :], top[:, j, :], logits[:, j, :])
    m = P.dve([m], nc.vector.tensor_copy, whichf[:], which[:])
    r = P.dve([m], nc.vector.tensor_tensor, both[:, :, 1:2], top[:, :, 1:2], top[:, :, 0:1], ALU.subtract)
    r = P.act([r], nc.scalar.activation, both[:, :, 1:2], both[:, :, 1:2], ACT.Exp)
    r = P.dve([r], nc.vector.tensor_scalar, both[:, :, 0:1], both[:, :, 1:2], 1.0, None, ALU.add)
    r = P.dve([r], nc.vector.reciprocal, both[:, :, 0:1], both[:, :, 0:1])
    r = P.dve([r], nc.vector.tensor_tensor, both[:, :, 1:2], both[:, :, 1:2], both[:, :, 0:1], ALU.mult)
    for j in range(TOK_TILES):
        q = P.dve([r, m, iot], nc.vector.tensor_scalar, w[:, j, :], number[:], whichf[:, j, 0:1], both[:, j, 0:1], ALU.is_equal, ALU.mult)
        p = P.dve([r], nc.vector.tensor_scalar, hot[:, j, :], number[:], whichf[:, j, 1:2], both[:, j, 1:2], ALU.is_equal, ALU.mult)
        q = P.dve([p, q], nc.vector.tensor_tensor, w[:, j, :], w[:, j, :], hot[:, j, :], ALU.add)
    t = transpose_back(P, C, [q], w, wT, E)
    spread = linear(P, [t, sels], lambda k, m: sel[:, m, :], [wT], E, lambda m, sl, ps, t: P.act([t], nc.scalar.copy, wB[:, m, sl], ps))
    zero = P.dve([], nc.vector.memset, acc[:], 0.0)
    last = [zero, spread]
    down = []
    for e in range(E):
        s = e % 2
        g = linear(P, [n, here[s], down], lambda k, m: w1[:, s, m * 128:(m + 1) * 128], [h], T, lambda m, sl, ps, t: P.act(
            [t, down], nc.scalar.activation, a[:, m, sl], ps, ACT.Silu))
        u = linear(P, [], lambda k, m: w3[:, s, m * 128:(m + 1) * 128], [h], T, lambda m, sl, ps, t: P.dve(
            [t, g], nc.vector.tensor_tensor, a[:, m, sl], ps, a[:, m, sl], ALU.mult))

        def weigh(m, sl, ps, t):
            q = P.dve([t, last], nc.vector.tensor_tensor, tmp[:, sl], ps, wB[:, e, sl], ALU.mult)
            P.dve([q], nc.vector.tensor_tensor, acc[:, sl], acc[:, sl], tmp[:, sl], ALU.add)
            return q
        down = linear(P, [u], lambda k, m: w2[:, s, k, :], [a[:, k, :] for k in range(T)], 1, weigh)
        last = [P.dve.sig.now()]
        if e + 2 < E:
            here[s] = fetch(e + 2, [P.pe.sig.now()])
    for sl in halves():
        P.dve(last, nc.vector.tensor_tensor, X[:, sl], X[:, sl], acc[:, sl], ALU.add)



def output_projection(P, C, marks, O, weight, X, stack, bias=None):
    parts = O.shape[-1] // 128
    OT = tile(P, stack, "OT", [128, parts, S])
    done = [transpose_back(P, C, marks, O[:, :, f * 128:(f + 1) * 128], OT[:, f, :], 128) for f in range(parts)]
    return linear(P, [done], weight, [OT[:, f, :] for f in range(parts)], 1, add_to_x(P, X, bias))


def values_by_token(P, marks, h, w, heads, dv, V, ones):
    nc = P.nc
    out = []
    width = min(HALF, heads * dv)
    if ones:
        out.append(P.pool([], nc.gpsimd.memset, V[:, :, :, dv:dv + 1], 1.0))
    for j in range(TOK_TILES):
        for c in range(heads * dv // width):
            b = P.bank()
            t = P.pe(marks, nc.tensor.matmul, P.ps[:, b, 0:width], lhsT=h[:, j * 128:(j + 1) * 128],
                     rhs=w[:, c * width:(c + 1) * width], start=True, stop=True)
            k = width // dv
            P.free[b] = P.act([t], nc.scalar.copy, V[:, j, c * k:(c + 1) * k, 0:dv], P.ps[:, b, 0:width].rearrange("p (h d) -> p h d", d=dv))
            out.append(P.free[b])
    return out


def head_of(V, head):
    n, d = V.shape[2], V.shape[3]
    return V[:].rearrange("p j h d -> p j (h d)")[:, :, bass.ds(head * d, d)]


def causal_products(P, C, make_head, heads, Q, K, V, dv, stack, finish):
    nc = P.nc
    Vh = tile(P, stack, "Vh", [128, 2, TOK_TILES, dv])
    A = tile(P, stack, "A", [128, 4, HALF])
    steps = [(half, k) for half in range(2) for k in range(TOK_TILES) if k * 128 < (half + 1) * HALF]
    with P.loop(heads // 2) as pair:
        banks, slots = Ring(P, "score_bank", 4), Ring(P, "A_slot", 4)
        dens = Ring(P, "denominator", 4)
        accs, head_in, vals = Ring(P, "accumulator", 4), Ring(P, "head", 2), Ring(P, "values", 2)
        n = 0
        for s in range(2):
            head = pair * 2 + s
            ready = make_head(s, head, head_in.get(s), banks)
            v = P.dve(vals.get(s), nc.vector.tensor_scalar, Vh[:, s], head_of(V, head), 1.0, None, ALU.mult)

            def products(half, k, slot, m):
                for j in range(4):
                    if half * 4 + j >= k:
                        t = P.pe([m, v], nc.tensor.matmul, P.ps[:, 4 + 2 * s + half, j * dv:(j + 1) * dv],
                                 lhsT=A[:, slot, j * 128:(j + 1) * 128], rhs=Vh[:, s, k, :], start=False, stop=True,
                                 skip_group_check=True)
                slots.put(slot, [t])
                return t

            for half in range(2):
                P.pe(accs.get(2 * s + half), nc.tensor.matmul, P.ps[:, 4 + 2 * s + half, 0:4 * dv], lhsT=C.zero[0:1, 0:128],
                     rhs=C.zero[0:1, 0:4 * dv], start=True, stop=True, skip_group_check=True)
            waiting = []
            for half, k in steps:
                slot = n % 4
                n += 1
                lo = max(0, k * 128 - half * HALF)
                t = P.pe([ready, banks.get(slot)], nc.tensor.matmul, P.ps[:, slot, lo:HALF], lhsT=K[:, s, k * 128:(k + 1) * 128],
                         rhs=Q[:, s, half * HALF + lo:(half + 1) * HALF], start=True, stop=True)
                src, dst, free = P.ps[:, slot, :], A[:, slot, :], slots.get(slot)
                if k * 128 >= half * HALF:
                    m = [P.dve([t, free], nc.vector.tensor_tensor, dst[:, lo:lo + 128], src[:, lo:lo + 128], C.causal[:], ALU.mult)]
                    if lo + 128 < HALF:
                        m.append(P.dve([], nc.vector.tensor_copy, dst[:, lo + 128:HALF], src[:, lo + 128:HALF]))
                else:
                    m = [P.act([t, free], nc.scalar.copy, dst, src)]
                banks.put(slot, m)
                waiting.append((half, k, slot, m))
                if len(waiting) > 2:
                    last = products(*waiting.pop(0))
            head_in.put(s, [t])
            while waiting:
                last = products(*waiting.pop(0))
            vals.put(s, [last])
            for half in range(2):
                view = P.ps[:, 4 + 2 * s + half, 0:4 * dv].rearrange("p (j d) -> p j d", d=dv)
                accs.put(2 * s + half, finish(s, head, half, view, [last], dens))
        for ring in (banks, slots, accs, head_in, vals, dens):
            ring.close()


def cosformer(P, C, io, X, stack):
    nc = P.nc
    H = 16
    d = io["L1_attn_Wq"].shape[1] // H
    wv = load(P, stack, "wv", io["L1_attn_Wv"])
    bv = load(P, stack, "bv", io["L1_attn_bv_row"])
    wo = load(P, stack, "wo", io["L1_attn_Wo"].rearrange("(k p) n -> p k n", p=128), [128, H * d // 128, D])
    bo = load(P, stack, "bo", io["L1_attn_bo"])
    bqk = tile(P, stack, "bqk", [128, 2, 2])
    cs = load(P, stack, "cs", io["cosformer_table"])
    wts = P.stream("weights").now()
    h, tmp = tile(P, stack, "h", [D, S]), tile(P, stack, "tmp", [D, S])
    V = tile(P, stack, "V", [128, TOK_TILES, H, d + 1])
    O = tile(P, stack, "O", [128, TOK_TILES, H * d])
    den = tile(P, stack, "den", [128, 4, 4])
    n = normalize(P, C, [], X, h, tmp)
    n = values_by_token(P, [n, wts], h, wv, H, d, V, True)
    add_row(P, C, n, V, bv, H, d)
    P.barrier()
    Q, K = (tile(P, stack, n, [128, 2, S]) for n in ("Q", "K"))
    w = tile(P, stack, "w", [128, 2, 2, 2 * d])
    arrive = [P.stream("head0"), P.stream("head1")]

    def make_head(s, head, free, banks):
        for j, name in enumerate(("L1_attn_Wq", "L1_attn_Wk")):
            for c in range(2):
                a = P.sp.dma([free], arrive[s], w[:, s, j, c * d:(c + 1) * d], io[name][:, bass.ds(head * d, d)])
        a = P.sp.dma([], arrive[s], bqk[:, s, :], io["L1_attn_bqk_twice"][bass.ds(head, 1)].rearrange("a p j -> p (a j)"))
        marks = []
        for j, dst in enumerate((Q, K)):
            for sl in halves():
                b = 2 * j + sl.start // HALF
                t = P.pe([a, banks.get(b)], nc.tensor.matmul, P.ps[:, b, :], lhsT=w[:, s, j, :], rhs=h[:, sl], start=True, stop=True)
                r = P.act([t, free], nc.scalar.activation, dst[:, s, sl], P.ps[:, b, :], ACT.Relu, bias=bqk[:, s, j:j + 1])
                banks.put(b, [r])
                marks.append(P.dve([r], nc.vector.tensor_tensor, dst[:, s, sl], dst[:, s, sl], cs[:, sl], ALU.mult))
        return marks

    def finish(s, head, half, view, marks, dens):
        z = 2 * s + half
        r = P.dve([marks, dens.get(z)], nc.vector.tensor_scalar, den[:, z, :], view[:, :, d], 1e-6, None, ALU.max)
        r = P.dve([r], nc.vector.reciprocal, den[:, z, :], den[:, z, :])
        for j in range(4):
            r2 = P.dve([r], nc.vector.tensor_scalar, O[:, half * 4 + j, bass.ds(head * d, d)], view[:, j, 0:d], den[:, z, j:j + 1], None, ALU.mult)
        dens.put(z, [r2])
        return [r2]

    causal_products(P, C, make_head, H, Q, K, V, d + 1, stack, finish)
    P.barrier()
    output_projection(P, C, [], O, lambda k, m: wo[:, k, :], X, stack, bo[:, 0:1])


def add_row(P, C, marks, V, row, H, d):
    nc = P.nc
    out = []
    for c in range(H * d // HALF):
        b = P.bank()
        t = P.pe(marks, nc.tensor.matmul, P.ps[:, b, :], lhsT=C.ones[0:1, :], rhs=row[0:1, c * HALF:(c + 1) * HALF], start=True, stop=True)
        k = HALF // d
        for j in range(V.shape[1]):
            v = V[:, j, c * k:(c + 1) * k, 0:d]
            P.free[b] = P.dve([t], nc.vector.tensor_tensor, v, v, P.ps[:, b, :].rearrange("p (h d) -> p h d", d=d), ALU.add)
        out.append(P.free[b])
    return out


def retention(P, C, io, X, stack):
    nc = P.nc
    H = D // 16
    d = D // H
    names = ("W_Q", "W_Q_turned", "W_K", "W_K_turned", "W_V", "W_G", "W_O")
    w = {n: load(P, stack, n, io["L3_attn_" + n]) for n in names}
    tables = {n: load(P, stack, n, io["retention_" + n]) for n in ("q_cos", "q_sin", "k_cos", "k_sin")}
    gw, gb = (load(P, stack, n, io["L3_attn_" + n]) for n in ("gn_weight", "gn_bias"))
    wts = P.stream("weights").now()
    h, tmp, tmp2 = (tile(P, stack, n, [D, S]) for n in ("h", "tmp", "tmp2"))
    V = tile(P, stack, "V", [128, TOK_TILES, H, d])
    O = tile(P, stack, "O", [128, TOK_TILES, D])
    n = normalize(P, C, [], X, h, tmp)
    v = values_by_token(P, [n, wts], h, w["W_V"], H, d, V, False)
    scratch = nc.dram_tensor("retention_heads", (2, D, S), F32, kind="Internal").ap()
    for j, x in enumerate("QK"):
        write_rotated(P, C, [n, wts], h, w["W_" + x], w["W_" + x + "_turned"], tables["q_cos" if x == "Q" else "k_cos"],
                      tables["q_sin" if x == "Q" else "k_sin"], tmp, tmp2, scratch[j])
    Q, K = (tile(P, stack, n, [128, 2, S]) for n in ("Q", "K"))
    for t in (Q, K):
        P.pool([], nc.gpsimd.memset, t[:], 0.0)
    P.barrier()
    arrive = [P.stream("head0"), P.stream("head1")]

    def make_head(s, head, free, banks):
        P.sp.dma([free], arrive[s], Q[0:d, s, :], scratch[0, bass.ds(head * d, d), :])
        return [P.sp.dma([], arrive[s], K[0:d, s, :], scratch[1, bass.ds(head * d, d), :])]

    def finish(s, head, half, view, marks, dens):
        return [P.dve(marks, nc.vector.tensor_scalar, O[:, half * 4:half * 4 + 4, bass.ds(head * d, d)], view, 1.0, None, ALU.mult)]

    causal_products(P, C, make_head, H, Q, K, V, d, stack, finish)
    P.barrier()
    G = TOK_TILES * H
    sq = tile(P, stack, "sq", [128, G, d])
    st = tile(P, stack, "st", [128, 2, G])
    Og = O[:].rearrange("p j (h d) -> p (j h) d", d=d)
    spread = lambda t: t.unsqueeze(2).to_broadcast([128, G, d])
    r = P.dve([], nc.vector.tensor_reduce, st[:, 0, :], Og, AX, ALU.add)
    r = P.dve([r], nc.vector.tensor_scalar, st[:, 0, :], st[:, 0, :], 1.0 / d, None, ALU.mult)
    r = P.dve([r], nc.vector.tensor_tensor, Og, Og, spread(st[:, 0, :]), ALU.subtract)
    q = P.dve([r], nc.vector.tensor_tensor, sq[:], Og, Og, ALU.mult)
    q = P.dve([q], nc.vector.tensor_reduce, st[:, 1, :], sq[:], AX, ALU.add)
    q = P.act([q], nc.scalar.activation, st[:, 1, :], st[:, 1, :], ACT.Sqrt, bias=C.eps[:, 0:1], scale=1.0 / d)
    q = P.dve([q], nc.vector.reciprocal, st[:, 1, :], st[:, 1, :])
    q = P.dve([q], nc.vector.tensor_tensor, Og, Og, spread(st[:, 1, :]), ALU.mult)
    y = transpose_back(P, C, [q], O[:], tmp, 128)
    y = P.dve([y], nc.vector.tensor_scalar, tmp[:], tmp[:], gw[:, 0:1], gb[:, 0:1], ALU.mult, ALU.add)
    g = linear(P, [], lambda k, m: w["W_G"][:], [h], 1, lambda m, sl, ps, t: P.act([t], nc.scalar.activation, tmp2[:, sl], ps, ACT.Silu))
    y = P.dve([y, g], nc.vector.tensor_tensor, tmp[:], tmp[:], tmp2[:], ALU.mult)
    linear(P, [y], lambda k, m: w["W_O"][:], [tmp], 1, add_to_x(P, X))


def write_rotated(P, C, marks, h, w, w_turned, cos, sin, a, b, dst):
    nc = P.nc
    stored = P.stream("stored")
    old = [stored.now()]
    done = []
    linear(P, [marks], lambda k, m: w[:], [h], 1, lambda m, sl, ps, t: P.dve([t, old], nc.vector.tensor_tensor, a[:, sl], ps, cos[:, sl], ALU.mult))

    def turned(m, sl, ps, t):
        r = P.dve([t], nc.vector.tensor_tensor, b[:, sl], ps, sin[:, sl], ALU.mult)
        done.append(P.dve([r], nc.vector.tensor_tensor, a[:, sl], a[:, sl], b[:, sl], ALU.add))
        return r
    linear(P, [marks], lambda k, m: w_turned[:], [h], 1, turned)
    return P.sp.dma(done, stored, dst, a[:])


def softmax_heads(P, C, head_in, Q, K, V, dv, O, causal, stack, heads):
    nc = P.nc
    PROBS = 4
    Pq, PT = tile(P, stack, "Pq", [128, PROBS, S]), tile(P, stack, "PT", [128, 2, S])
    st = tile(P, stack, "st", [128, PROBS, 4])
    tiles_of = lambda q: q + 1 if causal else TOK_TILES

    def front(n, s, q, ready, R):
        p, slot = n % 2, n % PROBS
        width = tiles_of(q) * 128
        for c in range(0, width, HALF):
            w = min(HALF, width - c)
            t = P.pe([ready[s], R["scores"].get(p)], nc.tensor.matmul, P.ps[:, 2 * p + c // HALF, 0:w], lhsT=Q[:, s, q * 128:(q + 1) * 128],
                     rhs=K[:, s, c:c + w], start=True, stop=True)
        R["queries"].put(s, [t])
        ps = P.ps[:, 2 * p:2 * p + 2, :].rearrange("p a b -> p (a b)")[:, 0:width]
        if causal:
            t = P.dve([t], nc.vector.tensor_tensor, ps[:, width - 128:width], ps[:, width - 128:width], C.below[:], ALU.add)
        m = P.dve([t, R["stats"].get(slot)], nc.vector.tensor_reduce, st[:, slot, 0:1], ps, AX, ALU.max, negate=True)
        e = P.act([m, t, R["probs"].get(slot)], nc.scalar.activation, Pq[:, slot, 0:width], ps, ACT.Exp, bias=st[:, slot, 0:1], accum_out=st[:, slot, 1:2])
        R["scores"].put(p, [e])
        return e

    def turn(n, q, ready, R):
        p, slot = n % 2, n % PROBS
        copies = [P.dve([ready], nc.vector.reciprocal, st[:, slot, 2:3], st[:, slot, 1:2])]
        for c in range(0, tiles_of(q), 4):
            k = min(4, tiles_of(q) - c)
            for j in range(c, c + k):
                t = P.pe([ready, R["turns"].get(c // 4)], nc.tensor.transpose, P.ps[:, 4 + c // 4, (j - c) * 128:(j - c + 1) * 128],
                         Pq[:, slot, j * 128:(j + 1) * 128], C.ident[:])
            eng, op = ((P.act, nc.scalar.copy), (P.dve, nc.vector.tensor_copy))[(c // 4 + q) % 2]
            m = eng([t, R["turned"].get(p)], op, PT[:, p, c * 128:(c + k) * 128], P.ps[:, 4 + c // 4, 0:k * 128])
            copies.append(m)
            R["turns"].put(c // 4, [m])
        R["probs"].put(slot, [t])
        return copies

    def multiply(n, s, q, head, ready, ins, R):
        p, slot = n % 2, n % PROBS
        for j in range(tiles_of(q)):
            t = P.pe([ready, ins[s], R["outs"].get(p)], nc.tensor.matmul, P.ps[:, 6 + p, 0:dv], lhsT=PT[:, p, j * 128:(j + 1) * 128],
                     rhs=V[:, s, j, :], start=j == 0, stop=j == tiles_of(q) - 1)
        R["turned"].put(p, [t])
        dst = O[:, q, 0:dv] if heads == 1 else O[:, q, bass.ds(head * dv, dv)]
        m = P.dve([t], nc.vector.tensor_scalar, dst, P.ps[:, 6 + p, 0:dv], st[:, slot, 2:3], None, ALU.mult)
        R["outs"].put(p, [m])
        R["stats"].put(slot, [m])
        R["values"].put(s, [t])

    def several(first, count):
        R = {n: Ring(P, n, k) for n, k in (("scores", 2), ("probs", PROBS), ("stats", PROBS), ("turns", 2), ("turned", 2), ("outs", 2),
                                            ("queries", count), ("values", count))}
        ins = [head_in(s, first + s, [R["queries"].get(s), R["values"].get(s)]) for s in range(count)]
        work = [(s, q) for s in range(count) for q in range(TOK_TILES)]
        exps, turned = {}, {}
        for n in range(len(work) + 3):
            if n < len(work):
                exps[n] = front(n, *work[n], ins, R)
            if 0 <= n - 2 < len(work):
                turned[n - 2] = turn(n - 2, work[n - 2][1], exps[n - 2], R)
            if 0 <= n - 3:
                s, q = work[n - 3]
                multiply(n - 3, s, q, first + s, turned[n - 3], ins, R)
        return R

    if heads == 1:
        several(0, 1)
    else:
        room = Q.shape[1]
        with P.loop(heads // room) as group:
            for ring in several(group * room, room).values():
                ring.close()


def causal_attention(P, C, io, X, stack):
    nc = P.nc
    H = 16
    d = D // H
    w = {n: load(P, stack, n, io["L0_attn_" + n]) for n in ("W_Q", "W_Q_turned", "W_K", "W_K_turned", "W_V", "W_O")}
    tables = {n: load(P, stack, n, io["rope_" + n]) for n in ("q_cos", "q_sin", "k_cos", "k_sin")}
    wts = P.stream("weights").now()
    h, tmp, tmp2 = (tile(P, stack, n, [D, S]) for n in ("h", "tmp", "tmp2"))
    V = tile(P, stack, "V", [128, TOK_TILES, H, d])
    O = tile(P, stack, "O", [128, TOK_TILES, D])
    n = normalize(P, C, [], X, h, tmp)
    values_by_token(P, [n, wts], h, w["W_V"], H, d, V, False)
    scratch = nc.dram_tensor("rope_heads", (2, D, S), F32, kind="Internal").ap()
    for j, x in enumerate("QK"):
        write_rotated(P, C, [n, wts], h, w["W_" + x], w["W_" + x + "_turned"], tables["q_cos" if x == "Q" else "k_cos"],
                      tables["q_sin" if x == "Q" else "k_sin"], tmp, tmp2, scratch[j])
    room = 4
    Q, K = (tile(P, stack, n, [128, room, S]) for n in ("Q", "K"))
    for t in (Q, K):
        P.pool([], nc.gpsimd.memset, t[:], 0.0)
    P.barrier()
    Vh = tile(P, stack, "Vh", [128, room, TOK_TILES, d])
    arrive = [P.stream(f"head{n}") for n in range(room)]

    def head_in(s, head, free):
        P.sp.dma([free], arrive[s], Q[0:d, s, :], scratch[0, bass.ds(head * d, d), :])
        a = P.sp.dma([], arrive[s], K[0:d, s, :], scratch[1, bass.ds(head * d, d), :])
        return [a, P.dve(free, nc.vector.tensor_scalar, Vh[:, s], head_of(V, head), 1.0, None, ALU.mult)]

    softmax_heads(P, C, head_in, Q, K, Vh, d, O, True, stack, H)
    P.barrier()
    output_projection(P, C, [], O, lambda k, m: w["W_O"][:], X, stack)


def attention_of_experts(P, C, io, X, stack):
    nc = P.nc
    E = io["L2_ffn_sim_matrix"].shape[1]
    sim = load(P, stack, "sim", io["L2_ffn_sim_matrix"])
    gates = load(P, stack, "gates", io["L2_ffn_gates_row"])
    wts = P.stream("weights").now()
    w = tile(P, stack, "w", [128, 2, 4, D])
    h, tmp = tile(P, stack, "h", [D, S]), tile(P, stack, "tmp", [D, S])
    wB = tile(P, stack, "wB", [128, E, S])
    xe = tile(P, stack, "xe", [128, 2, S])
    Q, K, Vt = (tile(P, stack, n, [128, 1, S]) for n in ("Q", "K", "Vt"))
    V = tile(P, stack, "V", [128, 1, TOK_TILES, D])
    O = tile(P, stack, "O", [128, TOK_TILES, D])
    sel, wT = tile(P, stack, "sel", [E, E, 128]), tile(P, stack, "wT", [E, S])
    loads = [P.stream("expert0"), P.stream("expert1")]
    sels = one_hot_rows(P, C, [], None, E, sel)
    names = ("q_proj", "k_proj", "v_proj", "o_proj")

    def fetch(e, marks, which):
        for n in which:
            a = P.sp.dma(marks, loads[e % 2], w[:, e % 2, n, :], io["L2_ffn_" + names[n]][e])
        return a
    here = [fetch(0, [], range(3)), fetch(1, [], range(3))]
    n = normalize(P, C, [], X, h, tmp)
    g = tile(P, stack, "g", [128, 4, E])
    r = P.act([wts], nc.scalar.activation, g[:, 0, :], sim[:], ACT.Square)
    b = P.bank()
    t = P.pe([r], nc.tensor.matmul, P.ps[:, b, 0:E], lhsT=C.mean[:], rhs=g[:, 0, :], start=True, stop=True)
    r = P.act([t], nc.scalar.activation, g[:, 1, :], P.ps[:, b, 0:E], ACT.Sqrt, scale=float(D))
    P.free[b] = r
    r = P.dve([r], nc.vector.tensor_scalar, g[:, 1, :], g[:, 1, :], 1e-12, None, ALU.max)
    r = P.dve([r], nc.vector.reciprocal, g[:, 1, :], g[:, 1, :])
    r = P.dve([r], nc.vector.tensor_tensor, g[:, 0, :], sim[:], g[:, 1, :], ALU.mult)
    b = P.bank()
    t = P.pe([], nc.tensor.matmul, P.ps[:, b, 0:E], lhsT=C.ones[0:1, :], rhs=gates[0:1, :], start=True, stop=True)
    s = P.act([t], nc.scalar.activation, g[:, 2, :], P.ps[:, b, 0:E], ACT.Sigmoid)
    P.free[b] = s
    q = P.act([n], nc.scalar.activation, tmp[:], h[:], ACT.Square)
    L = tile(P, stack, "L", [128, TOK_TILES, E])
    M, F = tile(P, stack, "M", [128, TOK_TILES, E]), tile(P, stack, "F", [128, TOK_TILES, E])
    top, which = tile(P, stack, "top", [128, TOK_TILES, 8]), tile(P, stack, "which", [128, TOK_TILES, 8], U32)
    whichf, norm = tile(P, stack, "whichf", [128, TOK_TILES, 8]), tile(P, stack, "norm", [128, TOK_TILES, 4])
    number = tile(P, stack, "number", [128, E])
    iot = P.pool([], nc.gpsimd.iota, number[:], [[1, E]], 0, 0, allow_small_or_imprecise_dtypes=True)
    b = P.bank()
    b2 = P.bank()
    for j in range(TOK_TILES):
        P.pe([q], nc.tensor.matmul, P.ps[:, b, j:j + 1], lhsT=tmp[:, j * 128:(j + 1) * 128], rhs=C.ones_col[:], start=True, stop=True)
        t = P.pe([r], nc.tensor.matmul, P.ps[:, b2, j * E:(j + 1) * E], lhsT=h[:, j * 128:(j + 1) * 128], rhs=g[:, 0, :], start=True, stop=True)
    r = P.act([t], nc.scalar.activation, norm[:, :, 0:1], P.ps[:, b, 0:TOK_TILES].unsqueeze(2), ACT.Sqrt)
    P.free[b] = r
    r = P.dve([r], nc.vector.tensor_scalar, norm[:, :, 0:1], norm[:, :, 0:1], 1e-12, None, ALU.max)
    r = P.dve([r], nc.vector.reciprocal, norm[:, :, 0:1], norm[:, :, 0:1])
    wide = lambda a: a.to_broadcast([128, TOK_TILES, E])
    each = lambda a: a.unsqueeze(1).to_broadcast([128, TOK_TILES, E])
    r = P.dve([r], nc.vector.tensor_tensor, L[:], P.ps[:, b2, 0:TOK_TILES * E].rearrange("p (j e) -> p j e", e=E), wide(norm[:, :, 0:1]), ALU.mult)
    P.free[b2] = r
    logits = P.dve([r, s], nc.vector.tensor_tensor, L[:], L[:], each(g[:, 2, :]), ALU.subtract)
    for j in range(TOK_TILES):
        m = P.dve([logits], nc.vector.max, top[:, j, :], L[:, j, :])
        m = P.dve([m], nc.vector.max_index, which[:, j, :], top[:, j, :], L[:, j, :])
    m = P.dve([m], nc.vector.tensor_copy, whichf[:], which[:])
    k = P.dve([logits], nc.vector.tensor_scalar, M[:], L[:], 0.0, None, ALU.is_gt)
    f = P.dve([m, iot], nc.vector.tensor_tensor, F[:], each(number[:]), wide(whichf[:, :, 0:1]), ALU.is_equal)
    f2 = P.dve([m, iot], nc.vector.tensor_tensor, wB[:, 0, 0:TOK_TILES * E].rearrange("p (j e) -> p j e", e=E), each(number[:]), wide(whichf[:, :, 1:2]), ALU.is_equal)
    f = P.dve([f, f2], nc.vector.tensor_tensor, F[:], F[:], wB[:, 0, 0:TOK_TILES * E].rearrange("p (j e) -> p j e", e=E), ALU.add)
    i = P.dve([m], nc.vector.tensor_scalar, norm[:, :, 1:2], top[:, :, 0:1], 0.0, None, ALU.is_le)
    f = P.dve([f, i], nc.vector.tensor_tensor, F[:], F[:], wide(norm[:, :, 1:2]), ALU.mult)
    k = P.dve([f, k], nc.vector.tensor_tensor, M[:], M[:], F[:], ALU.add)
    r = P.dve([m], nc.vector.tensor_scalar, norm[:, :, 2:3], top[:, :, 0:1], 0.0, None, ALU.max)
    r = P.dve([r, k, f], nc.vector.tensor_scalar, L[:], L[:], 0.0, None, ALU.max)
    r = P.dve([r], nc.vector.tensor_tensor, L[:], L[:], wide(norm[:, :, 2:3]), ALU.subtract)
    r = P.act([r], nc.scalar.activation, L[:], L[:], ACT.Exp)
    r = P.dve([r], nc.vector.tensor_tensor, L[:], L[:], M[:], ALU.mult)
    r2 = P.dve([r], nc.vector.tensor_reduce, norm[:, :, 3:4], L[:], AX, ALU.add)
    r2 = P.dve([r2], nc.vector.reciprocal, norm[:, :, 3:4], norm[:, :, 3:4])
    r2 = P.dve([r2], nc.vector.tensor_tensor, L[:], L[:], wide(norm[:, :, 3:4]), ALU.mult)
    t = transpose_back(P, C, [r2], L, wT, E)
    spread = linear(P, [t, sels, f], lambda k, m: sel[:, m, :], [wT], E, lambda m, sl, ps, t: P.act([t, f], nc.scalar.copy, wB[:, m, sl], ps))
    P.barrier()
    used = [[], []]
    for e in range(E):
        z = e % 2
        m = P.dve([used[z]], nc.vector.tensor_tensor, xe[:, z, :], h[:], wB[:, e, :], ALU.mult)
        for n in range(3):
            for i, sl in enumerate(halves()):
                t = P.pe([m, here[z]], nc.tensor.matmul, P.ps[:, 2 * n + i, :], lhsT=w[:, z, n, :], rhs=xe[:, z, sl], start=e == 0, stop=e == E - 1)
        used[z] = [t]
        if e + 2 < E:
            here[z] = fetch(e + 2, [t], range(3))
    out = []
    for n, dst in enumerate((Q, K, Vt)):
        for i, sl in enumerate(halves()):
            out.append(P.act([t], nc.scalar.activation, dst[:, 0, sl], P.ps[:, 2 * n + i, :], ACT.Copy, scale=1.0 / math.sqrt(D) if n == 0 else 1.0))
    here = [fetch(0, [t], [3]), fetch(1, [t], [3])]
    P.barrier()
    for i in range(2):
        b = P.bank()
        for j in range(4):
            t = P.pe([], nc.tensor.transpose, P.ps[:, b, j * 128:(j + 1) * 128], Vt[:, 0, (4 * i + j) * 128:(4 * i + j + 1) * 128], C.ident[:])
        P.free[b] = P.act([t], nc.scalar.copy, V[:, 0, 4 * i:4 * i + 4, :], P.ps[:, b, :].rearrange("p (j d) -> p j d", d=D))
    P.barrier()
    softmax_heads(P, C, lambda s, head, free: [], Q, K, V, D, O, False, stack, 1)
    P.barrier()
    t = transpose_back(P, C, [], O[:], Q[:, 0, :], 128)
    P.barrier()
    used = [[], []]
    for e in range(E):
        z = e % 2
        m = P.dve([used[z]], nc.vector.tensor_tensor, xe[:, z, :], Q[:, 0, :], wB[:, e, :], ALU.mult)
        for i, sl in enumerate(halves()):
            t = P.pe([m, here[z]], nc.tensor.matmul, P.ps[:, i, :], lhsT=w[:, z, 3, :], rhs=xe[:, z, sl], start=e == 0, stop=e == E - 1)
        used[z] = [t]
        if e + 2 < E:
            here[z] = fetch(e + 2, [t], [3])
    for i, sl in enumerate(halves()):
        add_to_x(P, X)(0, sl, P.ps[:, i, :], t)



class Cross:

    def __init__(self, P, name, heads, d, split, softmax, masked):
        nc = P.nc
        self.name, self.H, self.d, self.split, self.softmax, self.masked = name, heads, d, split, softmax, masked
        self.dt = BF16 if split else F32
        self.rows = len(TERMS) * d if split else d
        self.dv = d + 1 if softmax else d
        self.groups = {8: 4, 64: 2, 128: 1}[d]
        more = self.more = 2 if heads > 1 else 0
        dram = lambda n, shape, dt: nc.dram_tensor(f"{name}_dram_{n}", shape, dt, kind="Internal").ap()
        self.blocks = len(TERMS) if split else 1
        self.K = dram("K", (CHUNKS, self.blocks, heads + more, d, CHUNK), self.dt)
        self.Q = dram("Q", (heads + more, self.rows, S), self.dt)
        self.V = dram("V", (CHUNKS, heads + more, 128, TPC * self.dv), F32)
        self.O = dram("O", (heads, 128, S), F32)
        if softmax and not split:
            self.Kb, self.Qb = dram("Kb", (CHUNKS, heads + more, d, CHUNK), BF16), dram("Qb", (heads + more, d, S), BF16)
        if softmax:
            self.den = dram("den", (heads, S), F32)
            self.mask = dram("mask", (CHUNKS, CHUNK), F32)
            self.mask_parts = dram("mask_parts", (CHUNKS, 2, CHUNK), BF16)


TERMS = [(0, 0), (1, 0), (2, 0), (0, 1), (1, 1), (0, 2)]
CHUNKS = 0


def split_parts(P, marks, src, parts, rest):
    nc = P.nc
    a = P.dve([marks], nc.vector.tensor_copy, parts[:, 0], src)
    b = P.dve([a], nc.vector.tensor_tensor, rest, src, parts[:, 0], ALU.subtract)
    a = P.dve([b], nc.vector.tensor_copy, parts[:, 1], rest)
    b = P.dve([a], nc.vector.tensor_tensor, src, rest, parts[:, 1], ALU.subtract)
    return P.dve([b], nc.vector.tensor_copy, parts[:, 2], src)


def mask_rows(P, X, mask_src, fill, stack):
    nc = P.nc
    n = N_KEYS
    full, rest = n // CHUNK, n % CHUNK
    m = tile(P, stack, X.name + "_mask", [CHUNKS, CHUNK], F32)
    parts, t = tile(P, stack, X.name + "_mask_parts", [CHUNKS, 2, CHUNK], BF16), tile(P, stack, X.name + "_mask_rest", [CHUNKS, CHUNK])
    raw = tile(P, stack, X.name + "_mask_raw", [CHUNKS, CHUNK], I32 if mask_src is None else mask_src.dtype)
    z = P.dve([], nc.vector.memset, raw[:], 0)
    sig = P.stream("mask")
    src = P.io_ones if mask_src is None else mask_src
    if full:
        P.sp.dma([z], sig, raw[0:full, :], src[0:full * CHUNK].rearrange("(c n) -> c n", n=CHUNK))
    if rest:
        P.sp.dma([z], sig, raw[full:full + 1, 0:rest], src[full * CHUNK:n].unsqueeze(0))
    r = P.dve([sig.now()], nc.vector.tensor_copy, m[:], raw[:])
    r = P.dve([r], nc.vector.tensor_scalar, m[:], m[:], 0.0, fill, ALU.is_equal, ALU.mult)
    P.sp.dma([r], sig, X.mask, m[:])
    a = P.dve([r], nc.vector.tensor_copy, parts[:, 0, :], m[:])
    b = P.dve([a], nc.vector.tensor_tensor, t[:], m[:], parts[:, 0, :], ALU.subtract)
    a = P.dve([b], nc.vector.tensor_copy, parts[:, 1, :], t[:])
    P.sp.dma([a], sig, X.mask_parts, parts[:])


def keys_and_values(P, C, io, X, wk, bk, wv):
    nc = P.nc
    H, d, dv = X.H, X.d, X.dv
    F = H * d
    with ExitStack() as stack:
        if X.softmax:
            mask_rows(P, X, X.masked[0], X.masked[1], stack)
        wk_t, wv_t = (load(P, stack, n, w) for n, w in (("wk", wk), ("wv", wv)))
        bk_t = load(P, stack, "bk", bk) if bk is not None else None
        P.barrier()
        ctxt = tile(P, stack, "ctxt", [128, 2, CHUNK])
        valid = load(P, stack, "valid", io["valid_keys"])
        keep = tile(P, stack, "keep", [128, 2, CHUNK]) if X.split and X.softmax else None
        T = F // 128
        Kf = tile(P, stack, "Kf", [128, 2, T, CHUNK])
        Kb = tile(P, stack, "Kb", [128, 2, T, CHUNK], BF16) if not X.split and X.softmax else None
        parts, rest = (tile(P, stack, "parts", [128, 2, 3, CHUNK], BF16), tile(P, stack, "rest", [128, CHUNK])) if X.split else (None, None)
        Vt = tile(P, stack, "Vt", [128, 2, H, TPC, dv])
        width = min(HALF, F)
        arrive, stored = [P.stream("chunk0"), P.stream("chunk1")], [P.stream("stored0"), P.stream("stored1")]
        P.barrier()

        def fetch(c, z, free):
            a = P.sp.dma([free], arrive[z], ctxt[:, z, :], io["ctx_1024"][:, bass.ds(c * CHUNK, CHUNK)])
            if keep is not None:
                a = P.sp.dma([], arrive[z], keep[:, z, :], X.mask[bass.ds(c, 1), :].to_broadcast([128, CHUNK]))
            P.name_if(f"context{z}", a)
            return a

        def one(c, z, rings, a):
            banks, ins, outs, work = rings
            free = ins.get(z)
            stores = []
            old = outs.get(z)
            n = 0
            for f in range(T):
                b = n % 8
                n += 1
                t = P.pe([a, banks.get(b)], nc.tensor.matmul, P.ps[:, b, :], lhsT=wk_t[:, f * 128:(f + 1) * 128], rhs=ctxt[:, z, :], start=True, stop=True)
                if bk_t is None:
                    r = P.act([t, old, work.get(z)], nc.scalar.copy, Kf[:, z, f, :], P.ps[:, b, :])
                else:
                    r = P.act([t, old, work.get(z)], nc.scalar.activation, Kf[:, z, f, :], P.ps[:, b, :], ACT.Identity, bias=bk_t[:, f:f + 1])
                banks.put(b, [r])
                if Kb is not None:
                    q = P.dve([r, old], nc.vector.tensor_copy, Kb[:, z, f, :], Kf[:, z, f, :])
                    stores.append((q, X.Kb[bass.ds(c, 1), f * 128 // d:(f + 1) * 128 // d].rearrange("a h r n -> (a h r) n"), Kb[:, z, f, :]))
                    if f == 0 and X.more:
                        stores.append((q, X.Kb[bass.ds(c, 1), H:H + 2].rearrange("a h r n -> (a h r) n"), Kb[0:2 * d, z, 0, :]))
                if not X.split:
                    stores.append((r, X.K[bass.ds(c, 1), 0, f * 128 // d:(f + 1) * 128 // d].rearrange("a h r n -> (a h r) n"), Kf[:, z, f, :]))
                    if f == 0 and X.more:
                        stores.append((r, X.K[bass.ds(c, 1), 0, H:H + 2].rearrange("a h r n -> (a h r) n"), Kf[0:2 * d, z, 0, :]))
            if X.split:
                if keep is not None:
                    k = P.dve([a, free], nc.vector.tensor_scalar, keep[:, z, :], keep[:, z, :], 0.0, None, ALU.is_equal)
                    r = P.dve([r, k], nc.vector.tensor_tensor, Kf[:, z, 0, :], Kf[:, z, 0, :], keep[:, z, :], ALU.mult)
                q = split_parts(P, [r, old], Kf[:, z, 0, :], parts[:, z], rest[:])
                work.put(z, [q])
                for p in range(3):
                    g = [n for n, (_, part) in enumerate(TERMS) if part == p]
                    g = slice(g[0], g[-1] + 1)
                    for heads, lines in ((slice(0, H), 128), (slice(H, H + 2), 2 * d)):
                        stores.append((q, X.K[bass.ds(c, 1), g, heads].rearrange("a g h r n -> (a h r) g n"),
                                       parts[0:lines, z, p, :].unsqueeze(1).to_broadcast([lines, g.stop - g.start, CHUNK])))
            for j in range(TPC):
                for w in range(F // width):
                    b = n % 8
                    n += 1
                    t = P.pe([a, banks.get(b)], nc.tensor.matmul, P.ps[:, b, 0:width], lhsT=ctxt[:, z, j * 128:(j + 1) * 128],
                             rhs=wv_t[:, w * width:(w + 1) * width], start=True, stop=True)
                    k = width // d
                    r = P.dve([t, old], nc.vector.tensor_copy, Vt[:, z, w * k:(w + 1) * k, j, 0:d], P.ps[:, b, 0:width].rearrange("p (h d) -> p h d", d=d))
                    banks.put(b, [r])
                if X.softmax:
                    one_col = Vt[:, z, :, j, d:dv].rearrange("p h a -> p (h a)")
                    r = P.dve([old], nc.vector.tensor_scalar, one_col, C.ones16[:, 0:H], valid_chunk[:, z, j:j + 1], None, ALU.mult)
            ins.put(z, [t, r])
            stores.append((r, X.V[bass.ds(c, 1), 0:H].rearrange("a h p x -> p (a h) x"), Vt[:, z].rearrange("p h j x -> p h (j x)")))
            if X.more:
                stores.append((r, X.V[bass.ds(c, 1), H:H + 2].rearrange("a h p x -> p (a h) x"), Vt[:, z, 0:2].rearrange("p h j x -> p h (j x)")))
            for m, dst, src in stores:
                s = P.sp.dma([m], stored[z], dst, src)
            outs.put(z, [s])

        valid_chunk = tile(P, stack, "valid_chunk", [128, 2, TPC])

        def chunk(c, z, rings, a, more):
            if X.softmax:
                P.dve([rings[1].get(z)], nc.vector.tensor_scalar, valid_chunk[:, z, :], valid[:, bass.ds(c * TPC, TPC)], 1.0, None, ALU.mult)
                P.dve.wait(P.dve.sig.now())
            coming = fetch(c + 1, 1 - z, rings[1].get(1 - z)) if more else None
            one(c, z, rings, a)
            return coming

        make = lambda: [Ring(P, n, k) for n, k in (("kv_bank", 8), ("ctx", 2), ("out", 2), ("work", 2))]
        fetch(0, 0, [])
        with P.loop(CHUNKS // 2) as pair:
            rings = make()
            a = P.lags_of("context0")
            for z in range(2):
                a = chunk(pair * 2 + z, z, rings, a, True)
            for r in rings:
                r.close()
        P.barrier()
        chunk(CHUNKS - 1, 0, make(), [], False)
        P.barrier()


def queries(P, C, io, X, h, wq, bq):
    nc = P.nc
    scale = 1.0 / math.sqrt(X.d)
    with ExitStack() as stack:
        wq_t = load(P, stack, "wq", wq)
        bq_t = load(P, stack, "bq", bq) if bq is not None else None
        T = X.H * X.d // 128
        Qf = tile(P, stack, "Qf", [128, T, S])
        Qb = tile(P, stack, "Qb16", [128, T, S], BF16) if not X.split and X.softmax else None
        wts = P.stream("weights").now()
        sig = P.stream("stored0")
        r = linear(P, [wts, C.normed], lambda k, m: wq_t[:, m * 128:(m + 1) * 128], [h], T, lambda m, sl, ps, t: P.dve(
            [t], nc.vector.tensor_scalar, Qf[:, m, sl], ps, bq_t[:, m:m + 1] if bq_t is not None else 0.0, scale, ALU.add, ALU.mult))
        if X.split:
            parts, rest = tile(P, stack, "qparts", [128, 3, S], BF16), tile(P, stack, "qrest", [128, S])
            q = split_parts(P, [r], Qf[:, 0, :], parts, rest[:])
            for g, (p, _) in enumerate(TERMS):
                P.sp.dma([q], sig, X.Q[0:X.H, g * X.d:(g + 1) * X.d, :], parts[:, p, :])
                P.sp.dma([q], sig, X.Q[X.H:X.H + 2, g * X.d:(g + 1) * X.d, :], parts[0:2 * X.d, p, :])
        else:
            for f in range(T):
                k = slice(f * 128 // X.d, (f + 1) * 128 // X.d)
                P.sp.dma([r], sig, X.Q[k].rearrange("h r n -> (h r) n"), Qf[:, f, :])
                if f == 0 and X.more:
                    P.sp.dma([r], sig, X.Q[X.H:].rearrange("h r n -> (h r) n"), Qf[0:2 * X.d, 0, :])
                if Qb is not None:
                    q = P.act([r], nc.scalar.copy, Qb[:, f, :], Qf[:, f, :])
                    P.sp.dma([q], sig, X.Qb[k].rearrange("h r n -> (h r) n"), Qb[:, f, :])
                    if f == 0 and X.more:
                        P.sp.dma([q], sig, X.Qb[X.H:].rearrange("h r n -> (h r) n"), Qb[0:2 * X.d, 0, :])
        P.barrier()


def cross_heads(P, C, X, stack):
    nc = P.nc
    H, d, dv, rows, dt, G = X.H, X.d, X.dv, X.rows, X.dt, X.groups
    wide = d == 128
    aux = 64
    n_m = 1 if (dt == F32 and not wide) else 2
    end = aux + 2 * n_m
    width = 128 // G
    own_sum = X.softmax and d > 32
    v_cols = dv if not own_sum else d

    Kc = tile(P, stack, "Kc", [128, 3, CHUNK], dt)
    Vc = tile(P, stack, "Vc", [128, 2, TPC, dv])
    Qc = tile(P, stack, "Qc", [128, S], dt)
    Pr = tile(P, stack, "Pr", [128, 2 * TPC, S])
    Oc = tile(P, stack, "Oc", [128, S])
    kd = [P.stream(f"key_chunk{n}") for n in range(3)]
    vd = [P.stream(f"value_chunk{n}") for n in range(2)]
    kn = [P.stream(f"next_chunk{n}") for n in range(3)]
    q_in, q_next, stored = P.stream("query"), P.stream("next_query"), P.stream("head_stored")
    if own_sum:
        Ps, Dc = tile(P, stack, "Ps", [128, S]), tile(P, stack, "Dc", [1, S])
        sum_stored = P.stream("sum_stored")
    if not wide:
        for t in (Kc, Qc):
            if aux > rows:
                P.dve([], nc.vector.memset, t[32:aux], 0.0)
            P.dve([], nc.vector.memset, t[aux:128], 0.0)
        P.barrier()
    if X.softmax:
        Kn = tile(P, stack, "Kn", [128, 3, CHUNK], BF16)
        Qn = tile(P, stack, "Qn", [128, S], BF16)
        mx, red = tile(P, stack, "mx", [128, TOK_TILES]), tile(P, stack, "red", [128, 2, TOK_TILES])
        mparts = tile(P, stack, "mparts", [128, 2, TOK_TILES], BF16)
        mneg, mrest = tile(P, stack, "mneg", [128, TOK_TILES]), tile(P, stack, "mrest", [128, TOK_TILES])
        if wide:
            Ka, Qa, Qa0 = tile(P, stack, "Ka", [128, 3, CHUNK], BF16), tile(P, stack, "Qa", [128, S], BF16), tile(P, stack, "Qa0", [128, S], BF16)
            for t in (Ka, Qa, Qa0):
                P.dve([], nc.vector.memset, t[:], 0.0)
            P.barrier()
            P.dve([], nc.vector.memset, Ka[0:2], 1.0)
            P.dve([], nc.vector.memset, Qa[0:4], 1.0)
            P.dve([], nc.vector.memset, Qa0[0:4], 1.0)
            P.barrier()
            P.dve([], nc.vector.memset, Qa0[0:2], 0.0)
        else:
            for t in (Kn, Qn):
                if aux > rows:
                    P.dve([], nc.vector.memset, t[32:aux], 0.0)
                P.dve([], nc.vector.memset, t[aux:128], 0.0)
            P.barrier()
            for t in (Kc, Kn):
                P.dve([], nc.vector.memset, t[aux:aux + n_m], 1.0)
            for t in (Qc, Qn):
                P.dve([], nc.vector.memset, t[aux:end], 1.0)
            P.barrier()
            P.dve([], nc.vector.memset, Qn[aux:aux + n_m], 0.0)
    P.barrier()

    def mask_into(marks, sig, dst, c):
        if dst.dtype == F32:
            return P.sp.dma(marks, sig, dst, X.mask[bass.ds(c, 1), :])
        return P.sp.dma(marks, sig, dst, X.mask_parts[bass.ds(c, 1), 0:n_m].rearrange("a m n -> (a m) n"))

    def fetch_keys(c, z, now, nxt, free):
        if now is not None:
            P.sp.dma(free, kd[z], Kc[0:rows, z, :], X.K[bass.ds(c, 1), :, bass.ds(now, 1)].rearrange("a g h r n -> (a g) (h r) n"))
            if X.softmax and not wide:
                mask_into([], kd[z], Kc[aux + n_m:end, z, :], c)
        if nxt is not None:
            src = (X.K[bass.ds(c, 1), :, bass.ds(nxt, 1)].rearrange("a g h r n -> (a g) (h r) n") if X.split
                   else X.Kb[bass.ds(c, 1), bass.ds(nxt, 1)].rearrange("a h r n -> (a h r) n"))
            P.sp.dma(free, kn[z], Kn[0:rows, z, :], src)
            if not wide:
                mask_into([], kn[z], Kn[aux + n_m:end, z, :], c)
        if wide:
            mask_into(free, kn[z], Ka[2:4, z, :], c)
        P.name_if(f"keys{z}", kd[z].now())
        P.name_if(f"next{z}", kn[z].now())

    def fetch_values(c, z, now, R):
        free = [R["value_readers"].get(z), R["sum_readers"].get(z)]
        a = P.sp.dma(free, vd[z], Vc[:, z].rearrange("p j x -> p (j x)"), X.V[bass.ds(c, 1), bass.ds(now, 1)].rearrange("a h p x -> (a h p) x"))
        P.name_if(f"vals{z}", a)

    def arrived(z, label, sig):
        frame = P.frames[-1] if P.frames else None
        if frame is not None and sig.n == frame.base.get(sig, 0):
            return P.lags_of(f"{label}{z}")
        return [sig.now()]

    piece = HALF // 2 if G == 4 else HALF
    units = [(g, start) for g in range(TPC // G) for start in range(0, S, piece)]

    def step(z, kz, now, nxt, R, first):
        keys = arrived(kz, "keys", kd[kz]) if now is not None else []
        nexts = arrived(kz, "next", kn[kz]) if nxt is not None or wide else []

        def scores(t):
            b, slot = t % 2, z * TPC + t
            for half, sl in enumerate(halves()):
                m = P.pe([keys, nexts if wide else None, R["banks"].get(b), R["rows"].get(0)], nc.tensor.matmul, P.ps[:, 2 * b + half, :],
                         lhsT=Kc[:, kz, t * 128:(t + 1) * 128], rhs=Qc[:, sl], start=True, stop=not wide)
                if wide:
                    m = P.pe([], nc.tensor.matmul, P.ps[:, 2 * b + half, :], lhsT=Ka[:, kz, t * 128:(t + 1) * 128], rhs=Qa[:, sl], start=False, stop=True)
            e = P.act([m, R["probs"].get(slot), R["sums"].get(slot)], nc.scalar.activation, Pr[:, slot, :], P.ps[:, 2 * b:2 * b + 2, :].rearrange("p a n -> p (a n)"),
                      ACT.Exp if X.softmax else ACT.Sigmoid)
            R["banks"].put(b, [e])
            R["exps"].put(slot, [e])
            if own_sum:
                vals = arrived(z, "vals", vd[z])
                valid = Vc[:, z, t, d:dv]
                if first and t == 0:
                    s = P.dve([e, vals, R["sum_read"].get(0)], nc.vector.tensor_scalar, Ps[:], Pr[:, slot, :], valid, None, ALU.mult)
                else:
                    s = P.dve([e, vals, R["sum"].get(0)], nc.vector.scalar_tensor_tensor, Ps[:], Pr[:, slot, :], valid, Ps[:], ALU.mult, ALU.add)
                R["sums"].put(slot, [s])
                R["sum"].put(0, [s])
                R["sum_readers"].put(z, [s])

        def maxima(q):
            b = q % 2
            m = P.pe([nexts, R["nbanks"].get(b), R["next_query"].get(0)], nc.tensor.matmul, P.ps[:, 4 + b, :], lhsT=Qn[:, q * 128:(q + 1) * 128], rhs=Kn[:, kz, :], start=True, stop=not wide)
            if wide:
                m = P.pe([], nc.tensor.matmul, P.ps[:, 4 + b, :], lhsT=Qa0[:, q * 128:(q + 1) * 128], rhs=Ka[:, kz, :], start=False, stop=True)
            r = P.dve([m, R["reds"].get(z)], nc.vector.tensor_reduce, red[:, z, q:q + 1], P.ps[:, 4 + b, :], AX, ALU.max)
            R["nbanks"].put(b, [r])
            return r

        for t in range(TPC):
            if nxt is not None:
                maxima(2 * t)
            if now is not None:
                scores(t)
            if nxt is not None and G == 4:
                r = maxima(2 * t + 1)
            if now is not None and not first:
                for unit in units[t * len(units) // TPC:(t + 1) * len(units) // TPC]:
                    weigh(1 - z, unit, R)
            if nxt is not None and G < 4:
                r = maxima(2 * t + 1)
        if nxt is not None:
            r = P.dve([r, R["mx"].get(0)], nc.vector.tensor_tensor, mx[:], mx[:], red[:, z, :], ALU.max)
            R["reds"].put(z, [r])
            R["mx"].put(0, [r])
        R["key_readers"].put(kz, [P.pe.sig.now()])
        R["query_readers"].put(0, [P.pe.sig.now()])

    def weigh(z, unit, R):
        g, start = unit
        half, at = start // HALF, start % HALF
        slots = [z * TPC + g * G + n for n in range(G)]
        ready = [R["exps"].get(slot) for slot in slots]
        for n, slot in enumerate(slots):
            m = P.pe([ready, arrived(z, "vals", vd[z]), R["accs"].get(half)], nc.tensor.matmul, P.ps[n * width:n * width + v_cols, 6 + half, at:at + piece],
                     lhsT=Vc[:, z, g * G + n, 0:v_cols], rhs=Pr[:, slot, start:start + piece], start=False, stop=True, skip_group_check=True)
            R["probs"].put(slot, [m])
        R["value_readers"].put(z, [m])

    RINGS = {
        "banks": 2, "nbanks": 2,
        "exps": 2 * TPC,
        "probs": 2 * TPC, "sums": 2 * TPC,
        "key_readers": 3, "value_readers": 2, "sum_readers": 2,
        "reds": 2, "mx": 1, "mx_read": 1,
        "sum": 1, "sum_read": 1, "sum_stored": 1,
        "accs": 2, "stored": 1,
        "rows": 1, "rows_read": 1,
        "next_query": 1, "query_readers": 1,
    }

    def rings():
        return {n: Ring(P, n, k) for n, k in RINGS.items()}

    assert CHUNKS % 2 == 1
    unroll = UNROLL if (CHUNKS - 1) % UNROLL == 0 else 2
    groups = (CHUNKS - 1) // unroll

    def run(now, nxt, R, following=None):
        if nxt is not None:
            R["mx"].put(0, [P.dve([R["mx"].get(0), R["mx_read"].get(0)], nc.vector.memset, mx[:], -3.0e38)])

        def one(c, z, first, more):
            if more:
                fetch_keys(c + 1, 1 - z, now, nxt, R["key_readers"].get(1 - z))
            step(z, 2 if first else z, now, nxt, R, first)
            if more and now is not None:
                fetch_values(c + 1, 1 - z, now, R)
        one(0, 1, True, True)
        if now is not None:
            for half in range(2):
                R["accs"].put(half, [P.pe([R["accs"].get(half)], nc.tensor.matmul, P.ps[:, 6 + half, :], lhsT=C.zero[0:1, 0:128],
                                          rhs=C.zero[0:1, :], start=True, stop=True, skip_group_check=True)])
        if groups > 1:
            P.meet_engines()
            for r in R.values():
                r.enter()
            with P.loop(groups - 1) as i:
                for k in range(unroll):
                    one(i * unroll + (1 + k), k % 2, False, True)
                for r in R.values():
                    r.close()
            for r in R.values():
                r.leave()
        for k in range(unroll):
            one(CHUNKS - unroll + k, k % 2, False, k < unroll - 1)
            if following is not None and k == unroll - 2:
                fetch_keys(0, 2, following[0], following[1], R["key_readers"].get(2))

    def drain(R, which):
        for unit in which:
            weigh(1, unit, R)

    def take_off(R):
        r = P.dve([R["mx"].get(0), R["rows_read"].get(0)], nc.vector.tensor_scalar, mneg[:], mx[:], -1.0, None, ALU.mult)
        R["mx_read"].put(0, [r])
        free_banks = [R["nbanks"].get(0), R["nbanks"].get(1)]
        if n_m == 1:
            for q in range(TOK_TILES):
                t = P.pe([r, free_banks], nc.tensor.matmul, P.ps[aux:aux + 1, 4 + q // 4, (q % 4) * 128:(q % 4 + 1) * 128], lhsT=mneg[:, q:q + 1], rhs=C.ident[:], start=True, stop=True)
        else:
            a = P.dve([r], nc.vector.tensor_copy, mparts[:, 0, :], mneg[:])
            b = P.dve([a], nc.vector.tensor_tensor, mrest[:], mneg[:], mparts[:, 0, :], ALU.subtract)
            r = P.dve([b], nc.vector.tensor_copy, mparts[:, 1, :], mrest[:])
            base = 0 if wide else aux
            for q in range(TOK_TILES):
                t = P.pe([r, free_banks], nc.tensor.matmul, P.ps[base:base + 2, 4 + q // 4, (q % 4) * 128:(q % 4 + 1) * 128], lhsT=mparts[:, :, q], rhs=C.ident16[:], start=True, stop=True)
        R["rows_read"].put(0, [t])
        if wide:
            r = P.act([t], nc.scalar.copy, Qa[0:2, :], P.ps[0:2, 4:6, :].rearrange("p a n -> p (a n)"))
        else:
            r = P.act([t], nc.scalar.copy, Qc[aux:aux + n_m, :], P.ps[aux:aux + n_m, 4:6, :].rearrange("p a n -> p (a n)"))
        R["rows"].put(0, [r, q_in.now()])
        for b in range(2):
            R["nbanks"].put(b, [r])

    def next_queries(head, R):
        src = X.Q if X.split else X.Qb
        a = P.act.dma([R["query_readers"].get(0)], q_next, Qn[0:rows, :], src[bass.ds(head, 1)].rearrange("a r n -> (a r) n"))
        R["next_query"].put(0, [a])

    def these_queries(head, R):
        a = P.act.dma([R["query_readers"].get(0)], q_in, Qc[0:rows, :], X.Q[bass.ds(head, 1)].rearrange("a r n -> (a r) n"))
        R["rows"].put(0, [a])

    def store(head, R):
        last = [R["probs"].get(n) for n in range(2 * TPC)]
        if own_sum:
            for half, sl in enumerate(halves()):
                t = P.pe([R["sum"].get(0), R["banks"].get(1)], nc.tensor.matmul, P.ps[0:1, 2 + half, :], lhsT=C.ones_col[:], rhs=Ps[:, sl], start=True, stop=True)
            r = P.act([t, R["sum_stored"].get(0)], nc.scalar.copy, Dc[:], P.ps[0:1, 2:4, :].rearrange("p a n -> p (a n)"))
            R["banks"].put(1, [r])
            R["sum_read"].put(0, [t])
            R["sum_stored"].put(0, [P.sp.dma([r], sum_stored, X.den[bass.ds(head, 1), :], Dc[:])])
        r = P.act([last, R["stored"].get(0)], nc.scalar.copy, Oc[:], P.ps[:, 6:8, :].rearrange("p a n -> p (a n)"))
        for half in range(2):
            R["accs"].put(half, [r])
        R["stored"].put(0, [P.sp.dma([r], stored, X.O[bass.ds(head, 1)].rearrange("a p n -> (a p) n"), Oc[:])])

    R = rings()
    follow = lambda n: n if X.softmax and H > 1 else None
    if X.softmax:
        next_queries(0, R)
        fetch_keys(0, 2, None, 0, [])
        run(None, 0, R)
        P.barrier()
        take_off(rings())
    R = rings()
    these_queries(0, R)
    if follow(1):
        next_queries(1, R)
    fetch_keys(0, 2, 0, follow(1), [])
    fetch_values(0, 1, 0, R)
    P.barrier()
    if H == 1:
        R = rings()
        run(0, None, R)
        drain(R, units)
        store(0, R)
        P.barrier()
        return
    with P.loop(H) as head:
        R = rings()
        run(head, follow(head + 1), R, (head + 1, follow(head + 2)))
        these_queries(head + 1, R)
        if X.softmax:
            next_queries(head + 2, R)
        early = len(units) // 2 if X.softmax else 0
        drain(R, units[:early])
        if X.softmax:
            take_off(R)
        drain(R, units[early:])
        fetch_values(0, 1, head + 1, R)
        store(head, R)
        for r in R.values():
            r.close()
    P.barrier()


def cross_layer(P, C, io, X, stack, name, heads, d, split, softmax, masked, w, bias, out):
    nc = P.nc
    A = Cross(P, name, heads, d, split, softmax, masked)
    bk = io[bias[1]] if bias else None
    keys_and_values(P, C, io, A, io[w[1]], bk, io[w[2]])
    with ExitStack() as inner:
        h, tmp = tile(P, inner, "h", [D, S]), tile(P, inner, "tmp", [D, S])
        C.normed = normalize(P, C, [], X, h, tmp)
        queries(P, C, io, A, h, io[w[0]], io[bias[0]] if bias else None)
    with ExitStack() as inner:
        cross_heads(P, C, A, inner)
    bring_together(P, C, io, A, X, stack, bias, out)


def bring_together(P, C, io, A, X, stack, bias, out):
    nc = P.nc
    H, d, G = A.H, A.d, A.groups
    T, per_tile, width = H * d // 128, 128 // d, 128 // G
    U = tile(P, stack, "U", [128, G, T, S])
    bv = load(P, stack, "bv", io[bias[2]]) if bias else None
    wo = load(P, stack, "wo", io[out[0]].rearrange("(k p) n -> p k n", p=128), [128, T, D]) if out else None
    bo = load(P, stack, "bo", io[out[1]]) if out and out[1] else None
    if A.softmax:
        own_sum = d > 32
        n = 1 if own_sum else G
        sums = tile(P, stack, "sums", [H, n, S])
        for g in range(n):
            P.sp.dma(None, P.stream("sums"), sums[:, g, :], A.den if own_sum else A.O[:, g * width + d, :])
    loads = [P.stream(f"heads{t}") for t in range(T)]
    for t in range(T):
        for g in range(G):
            P.sp.dma(None, loads[t], U[:, g, t, :], A.O[t * per_tile:(t + 1) * per_tile, g * width:g * width + d, :])
    r = None
    if A.softmax:
        r = P.stream("sums").now()
        for g in range(1, n):
            r = P.dve([r], nc.vector.tensor_tensor, sums[:, 0, :], sums[:, 0, :], sums[:, g, :], ALU.add)
        r = P.dve([r], nc.vector.reciprocal, sums[:, 0, :], sums[:, 0, :])
        a = P.sp.dma([r], P.stream("sums"), A.den, sums[:, 0, :])
        over = tile(P, stack, "over", [128, T, S])
        for t in range(T):
            r = P.act.dma([a], P.stream("sums_over"), over[:, t, :], A.den[t * per_tile:(t + 1) * per_tile].unsqueeze(1).to_broadcast([per_tile, d, S]))
    wts = P.stream("weights").now()
    done = []
    for t in range(T):
        m = loads[t].now()
        for g in range(1, G):
            m = P.dve([m], nc.vector.tensor_tensor, U[:, 0, t, :], U[:, 0, t, :], U[:, g, t, :], ALU.add)
        if A.softmax:
            m = P.dve([m, r], nc.vector.tensor_tensor, U[:, 0, t, :], U[:, 0, t, :], over[:, t, :], ALU.mult)
        if bv is not None:
            m = P.dve([m, wts], nc.vector.tensor_scalar, U[:, 0, t, :], U[:, 0, t, :], bv[:, t:t + 1], None, ALU.add)
        done.append(m)
    if out:
        for t in range(T):
            for half, sl in enumerate(halves()):
                m = P.pe([done[t], wts], nc.tensor.matmul, P.ps[:, half, :], lhsT=wo[:, t, :], rhs=U[:, 0, t, sl], start=t == 0, stop=t == T - 1)
        for half, sl in enumerate(halves()):
            add_to_x(P, X, bo[:, 0:1] if bo is not None else None)(0, sl, P.ps[:, half, :], m)
    else:
        P.dve([done], nc.vector.tensor_tensor, X[:], X[:], U[:, 0, 0, :], ALU.add)


def cross_0(P, C, io, X, stack):
    cross_layer(P, C, io, X, stack, "L0", 16, 64, False, True, (io["mask_BxS2_bf1"], MASKED), ("L0_xattn_Wq", "L0_xattn_Wk", "L0_xattn_Wv"),
                ("L0_xattn_bq", "L0_xattn_bk", "L0_xattn_bv"), ("L0_xattn_Wo", "L0_xattn_bo"))


def cross_1(P, C, io, X, stack):
    cross_layer(P, C, io, X, stack, "L1", 1, 128, False, True, (None, MASKED), ("L1_xattn_Wq", "L1_xattn_Wk", "L1_xattn_Wv"), None, None)


def cross_2(P, C, io, X, stack):
    cross_layer(P, C, io, X, stack, "L2", 16, 8, True, False, None, ("L2_xattn_Wq", "L2_xattn_Wk", "L2_xattn_Wv"), None, ("L2_xattn_Wo", None))


def cross_3(P, C, io, X, stack):
    cross_layer(P, C, io, X, stack, "L3", 16, 8, True, True, (io["mask_Bx1x1xS2_ik0"], -1e9), ("L3_xattn_Wq", "L3_xattn_Wk", "L3_xattn_Wv"),
                ("L3_xattn_bq", "L3_xattn_bk", "L3_xattn_bv"), ("L3_xattn_Wo", "L3_xattn_bo"))


def build(nc, io, counts, layers):
    global CHUNKS, N_KEYS
    N_KEYS = io["ones_keys"].shape[0]
    CHUNKS = io["ctx_1024"].shape[1] // CHUNK
    with ExitStack() as ctx:
        P = Prog(nc, ctx, counts)

        class C:
            pass
        C.mean = tile(P, ctx, "mean", [128, 128])
        C.eps = tile(P, ctx, "eps", [128, 1])
        C.one_eps = tile(P, ctx, "one_eps", [128, 1])
        C.ident = tile(P, ctx, "ident", [128, 128])
        C.zero = tile(P, ctx, "zero", [128, HALF])
        C.ones, C.ones_col = tile(P, ctx, "ones", [1, 128]), tile(P, ctx, "ones_col", [128, 1])
        C.ones16, C.ident16 = tile(P, ctx, "ones16", [128, 16]), tile(P, ctx, "ident16", [128, 128], BF16)
        P.dve([], nc.vector.memset, C.ones16[:], 1.0)
        P.io_ones = io["ones_keys"]
        C.causal, C.below = tile(P, ctx, "causal", [128, 128]), tile(P, ctx, "below", [128, 128])
        X = tile(P, ctx, "X", [D, S])
        P.sp.dma(None, P.stream("x"), X[:], io["x"])
        P.dve([], nc.vector.memset, C.mean[:], 1.0 / D)
        P.dve([], nc.vector.memset, C.eps[:], LN_EPS)
        P.dve([], nc.vector.memset, C.one_eps[:], 1.0 + 1e-6)
        P.dve([], nc.vector.memset, C.zero[:], 0.0)
        z = P.pool([], nc.gpsimd.memset, C.ident[:], 0.0)
        P.pool([z], nc.gpsimd.affine_select, out=C.ident[:], in_=C.ident[:], compare_op=ALU.not_equal, fill=1.0,
               base=0, pattern=[[-1, 128]], channel_multiplier=1)
        P.dve([], nc.vector.memset, C.ones[:], 1.0)
        P.dve([], nc.vector.memset, C.ones_col[:], 1.0)
        z = P.pool([], nc.gpsimd.memset, C.causal[:], 1.0)
        P.pool([z], nc.gpsimd.affine_select, out=C.causal[:], in_=C.causal[:], compare_op=ALU.is_ge, fill=0.0,
               base=0, pattern=[[1, 128]], channel_multiplier=-1)
        z = P.pool([], nc.gpsimd.memset, C.below[:], 0.0)
        P.pool([z], nc.gpsimd.affine_select, out=C.below[:], in_=C.below[:], compare_op=ALU.is_ge, fill=MASKED,
               base=0, pattern=[[-1, 128]], channel_multiplier=1)
        P.barrier()
        P.dve([], nc.vector.tensor_copy, C.ident16[:], C.ident[:])
        P.barrier()
        for n in layers:
            with ExitStack() as stack:
                PARTS[n](P, C, io, X, stack)
                P.barrier()
        P.sp.dma(None, P.stream("out"), io["out"], X[:])
        P.barrier()


PARTS = {2: ffn_ternary_gated, 5: ffn_ternary_gelu, 6: recurrent_block, 11: ffn_experts,
         0: causal_attention, 1: cross_0, 4: cross_1, 7: cross_2, 10: cross_3, 3: cosformer, 8: attention_of_experts, 9: retention}



TRANSPOSED = {"L0_ffn_w1_w", "L0_ffn_w2_w", "L0_ffn_h1_w", "L0_ffn_h2_w", "L0_ffn_w3_w", "L1_ffn_W1", "L1_ffn_W2",
              "L2_attn_W_in", "L2_attn_W_gate", "L2_attn_W_out", "L2_attn_rg_in_w", "L2_attn_rg_gate_w",
              "L2_attn_mlp_gate_w", "L2_attn_mlp_up_w", "L2_attn_mlp_down_w",
              "L0_attn_W_Q", "L0_attn_W_K", "L0_attn_W_V", "L0_attn_W_O",
              "L2_xattn_Wq", "L2_xattn_Wk", "L2_xattn_Wv", "L2_xattn_Wo",
              "L3_xattn_Wq", "L3_xattn_Wk", "L3_xattn_Wv", "L3_xattn_Wo"}


def kernel(**inputs):
    import concourse.bacc as bacc
    from concourse.bass_utils import run_bass_kernel_spmd

    arrays = {}
    for name, a in inputs.items():
        a = np.asarray(a)
        if name in TRANSPOSED:
            a = a.T
        if name == "x":
            a = a[0].T
        if name == "ctx_1024":
            n_keys = a.shape[1]
            padded = -(-n_keys // CHUNK) * CHUNK
            a = np.pad(a[0], ((0, padded - n_keys), (0, 0))).T
        if name.startswith("mask"):
            a = a.reshape(-1)
        if a.ndim == 1 and not name.startswith("mask"):
            a = a.reshape(-1, 96 if a.size == 192 else min(128, a.size)).T
        if a.dtype == np.bool_:
            a = a.view(np.uint8)
        arrays[name] = np.ascontiguousarray(a)
    arrays.update(layout(inputs))
    arrays["ones_keys"] = np.ones(n_keys, np.int32)
    valid = (np.arange(padded) < n_keys).astype(np.float32)
    arrays["valid_keys"] = np.ascontiguousarray(valid.reshape(-1, 128).T)

    def program(counts):
        nc = bacc.Bacc("TRN2", target_bir_lowering=False, num_devices=1)
        io = {n: nc.dram_tensor(n + "_dram", a.shape, mybir.dt.from_np(a.dtype), kind="ExternalInput").ap()
              for n, a in arrays.items()}
        io["out"] = nc.dram_tensor("out_dram", (D, S), F32, kind="ExternalOutput").ap()
        build(nc, io, counts, LAYERS)
        return nc

    counts = {}
    program(counts)
    nc = program(counts)
    r = run_bass_kernel_spmd(nc, [{n + "_dram": a for n, a in arrays.items()}], core_ids=[0])
    return np.ascontiguousarray(r.results[0]["out_dram"].T)[None]


def exchanged(a):
    return a.reshape(a.shape[0], -1, 2)[:, :, ::-1].reshape(a.shape)


def block_diagonal(w):
    h, d, _ = w.shape
    out = np.zeros((h * d, h * d), w.dtype)
    for n in range(h):
        out[n * d:(n + 1) * d, n * d:(n + 1) * d] = w[n]
    return out


def tables():
    pos = np.arange(S, dtype=np.float64)
    out = {}

    def table(d, cos, sin, factor):
        c = np.repeat(cos, 2, axis=1).T
        s = np.stack([-sin, sin], axis=2).reshape(S, d).T
        n = D // d
        return [np.ascontiguousarray((np.tile(t, (n, 1)) * factor).astype(np.float32)) for t in (c, s)]

    d = D // 16
    inv = 10000.0 ** (-2.0 * np.arange(d // 2) / d)
    ang = (np.float32(1) * pos[:, None].astype(np.float32) * inv.astype(np.float32)).astype(np.float64)
    out["rope_q_cos"], out["rope_q_sin"] = table(d, np.cos(ang), np.sin(ang), 1.0 / math.sqrt(d))
    out["rope_k_cos"], out["rope_k_sin"] = table(d, np.cos(ang), np.sin(ang), 1.0)

    H, d = 8, 16
    gamma = (1.0 - np.exp(np.linspace(math.log(1.0 / 32.0), math.log(1.0 / 512.0), H))).astype(np.float32).astype(np.float64)
    scale = (np.arange(0, d, 2) + 0.4 * d) / (1.4 * d)
    sc = scale[None, :] ** (pos / 512.0)[:, None]
    inv = (1.0 / 10000.0 ** (np.arange(d // 2) / (d // 2))).astype(np.float32)
    ang = (pos[:, None].astype(np.float32) * inv).astype(np.float64)
    decay = np.repeat(gamma[:, None] ** pos[None, :], d, axis=0)
    out["retention_q_cos"], out["retention_q_sin"] = table(d, np.cos(ang) * sc, np.sin(ang) * sc, decay)
    out["retention_k_cos"], out["retention_k_sin"] = table(d, np.cos(ang) / sc, np.sin(ang) / sc, 1.0 / decay)

    ang = (np.float32(math.pi / (2.0 * S)) * pos.astype(np.float32)).astype(np.float64)
    out["cosformer_table"] = np.repeat(np.stack([np.cos(ang), np.sin(ang)]), 64, axis=0).astype(np.float32)
    return out


def layout(inputs):
    out = tables()
    get = lambda n: np.asarray(inputs[n])
    for x in ("Q", "K"):
        out[f"L0_attn_W_{x}_turned"] = exchanged(get(f"L0_attn_W_{x}").T)
        out[f"L3_attn_W_{x}"] = block_diagonal(get(f"L3_attn_W_{x}"))
        out[f"L3_attn_W_{x}_turned"] = exchanged(out[f"L3_attn_W_{x}"])
    out["L3_attn_W_V"] = block_diagonal(get("L3_attn_W_V"))
    heads = lambda n: np.tile(get(n).reshape(16, 64).T, (2, 1))
    out["L1_attn_bqk_twice"] = np.stack([heads("L1_attn_bq"), heads("L1_attn_bk")], axis=2).transpose(1, 0, 2)
    for n in ("L1_attn_bv", "L0_xattn_bv", "L3_xattn_bv", "L2_ffn_gates"):
        out[n + "_row"] = get(n)[None]
    out["L1_xattn_Wk"], out["L1_xattn_Wv"] = np.split(get("L1_xattn_Wkv"), 2, axis=1)
    return {n: np.ascontiguousarray(a) for n, a in out.items()}
```
